# Optimizing a Trainium2 kernel written in Bass

```python
import numpy as np
import jax
import jax.numpy as jnp

def _softmax(x, axis=-1):
    return jax.nn.softmax(x, axis=axis)

def _gelu(x):
    return jax.nn.gelu(x, approximate=True)

def _silu(x):
    return jax.nn.silu(x)

def _sigmoid(x):
    return jax.nn.sigmoid(x)

def _layernorm(x, axis=-1, eps=1e-05):
    m = jnp.mean(x, axis=axis, keepdims=True)
    v = jnp.var(x, axis=axis, keepdims=True)
    return (x - m) / jnp.sqrt(v + eps)

def _scatter_add(tgt, idx, src, axis=0):
    return tgt.at[idx].add(src)

def _segment_sum(src, seg, n):
    return jax.ops.segment_sum(src, seg, n)
kernel_name = 'mk_lm_tower_d1_tok_ids1024_r4_60df3b'

def setup_inputs(seed: int=0):
    np.random.seed(seed)
    _w = jnp.asarray

    def _rec_inputs():
        import jax
        import jax.numpy as jnp
        _rk = jax.random.key(seed)
        x = jax.random.randint(jax.random.fold_in(_rk, 1), (1, 2048), 0, 31993, jnp.int32)
        return x
    x = _rec_inputs()

    def _L0_tok_setup():
        import jax, jax.numpy as jnp
        import numpy as np
        N_BLOCKS = 6
        D_MODEL = 256
        N_HEADS = 8
        D_K = D_MODEL // N_HEADS
        D_FF = 1024
        VSIZE = 8000
        B, LS = (4, 512)
        LN_EPS = 1e-05

        def _layernorm(x, w, b):
            m = jnp.mean(x, axis=-1, keepdims=True)
            v = jnp.mean((x - m) ** 2, axis=-1, keepdims=True)
            return (x - m) * jax.lax.rsqrt(v + LN_EPS) * w + b
        key = jax.random.key(seed)
        ks = jax.random.split(key, 10)
        s = 0.02
        return {'source': jax.random.randint(ks[0], (B, LS), 0, VSIZE), 'emb_table': s * jax.random.normal(ks[1], (VSIZE, D_MODEL), jnp.float32), 'Wq': s * jax.random.normal(ks[2], (N_BLOCKS, N_HEADS, D_K, D_MODEL), jnp.float32), 'Wk': s * jax.random.normal(ks[3], (N_BLOCKS, N_HEADS, D_K, D_MODEL), jnp.float32), 'Wv': s * jax.random.normal(ks[4], (N_BLOCKS, N_HEADS, D_K, D_MODEL), jnp.float32), 'Wo': s * jax.random.normal(ks[5], (N_BLOCKS, D_MODEL, D_MODEL), jnp.float32), 'ff_w1': s * jax.random.normal(ks[6], (N_BLOCKS, D_FF, D_MODEL), jnp.float32), 'ff_b1': jnp.zeros((N_BLOCKS, D_FF), jnp.float32), 'ff_w2': s * jax.random.normal(ks[7], (N_BLOCKS, D_MODEL, D_FF), jnp.float32), 'ff_b2': jnp.zeros((N_BLOCKS, D_MODEL), jnp.float32), 'ln1_w': jnp.ones((N_BLOCKS, D_MODEL), jnp.float32), 'ln1_b': jnp.zeros((N_BLOCKS, D_MODEL), jnp.float32), 'ln2_w': jnp.ones((N_BLOCKS, D_MODEL), jnp.float32), 'ln2_b': jnp.zeros((N_BLOCKS, D_MODEL), jnp.float32)}
    _L0_tok_all = _L0_tok_setup()
    _L0_tok_in = {k: v for k, v in _L0_tok_all.items() if k in ('emb_table', 'Wq', 'Wk', 'Wv', 'Wo', 'ff_w1', 'ff_b1', 'ff_w2', 'ff_b2', 'ln1_w', 'ln1_b', 'ln2_w', 'ln2_b')}
    del _L0_tok_all

    def _L0_attn_setup():
        import jax, jax.numpy as jnp
        import numpy as np
        B, N, D, H, DH, M = (4, 1024, 256, 16, 64, 64)
        EPS = 0.0001

        def softmax_kernel(data, P, is_query):
            dn = data.shape[-1] ** (-0.25)
            ratio = P.shape[0] ** (-0.5)
            dd = jnp.einsum('bhnd,md->bhnm', dn * data, P)
            diag = (jnp.sum(data * data, axis=-1) * 0.5 * dn * dn)[..., None]
            if is_query:
                mx = jnp.max(dd, axis=-1, keepdims=True)
            else:
                mx = jnp.max(dd)
            return ratio * (jnp.exp(dd - diag - mx) + EPS)
        key = jax.random.key(seed)
        ks = jax.random.split(key, 6)
        s = 1.0 / np.sqrt(D).astype(np.float32)
        x = jax.random.normal(ks[0], (B, N, D), jnp.float32)
        Wq = jax.random.normal(ks[1], (D, H * DH), jnp.float32) * s
        Wk = jax.random.normal(ks[2], (D, H * DH), jnp.float32) * s
        Wv = jax.random.normal(ks[3], (D, H * DH), jnp.float32) * s
        Wo = jax.random.normal(ks[4], (H * DH, D), jnp.float32) * s
        bo = jnp.zeros((D,), jnp.float32)
        P = jax.random.normal(ks[5], (M, DH), jnp.float32)
        return {'x': x, 'Wq': Wq, 'Wk': Wk, 'Wv': Wv, 'Wo': Wo, 'bo': bo, 'P': P}
    _L0_attn_all = _L0_attn_setup()
    _L0_attn_in = {k: v for k, v in _L0_attn_all.items() if k in ('Wq', 'Wk', 'Wv', 'Wo', 'bo', 'P')}
    del _L0_attn_all

    def _L0_ffn_setup():
        import jax, jax.numpy as jnp
        import numpy as np
        H, I, E_ROUTED, TOP_K = (256, 704, 7, 2)
        B, S = (4, 512)

        def _expert(h, g, u, d):
            return jnp.einsum('...i,hi->...h', jax.nn.silu(h @ g.T) * (h @ u.T), d)
        key = jax.random.key(seed)
        ks = jax.random.split(key, 10)
        sc = 0.02
        return {'x': jax.random.normal(ks[0], (B, S, H), dtype=jnp.float32), 'sg': jax.random.normal(ks[1], (I, H), dtype=jnp.float32) * sc, 'su': jax.random.normal(ks[2], (I, H), dtype=jnp.float32) * sc, 'sd': jax.random.normal(ks[3], (H, I), dtype=jnp.float32) * sc, 'rg': jax.random.normal(ks[4], (E_ROUTED, I, H), dtype=jnp.float32) * sc, 'ru': jax.random.normal(ks[5], (E_ROUTED, I, H), dtype=jnp.float32) * sc, 'rd': jax.random.normal(ks[6], (E_ROUTED, H, I), dtype=jnp.float32) * sc, 'wr': jax.random.normal(ks[7], (E_ROUTED, H), dtype=jnp.float32) * sc, 'rb': jnp.zeros((E_ROUTED,), dtype=jnp.float32)}
    _L0_ffn_all = _L0_ffn_setup()
    _L0_ffn_in = {k: v for k, v in _L0_ffn_all.items() if k in ('sg', 'su', 'sd', 'rg', 'ru', 'rd', 'wr', 'rb')}
    del _L0_ffn_all
    return {'x': x, 'L0_tok_emb_table': _L0_tok_in['emb_table'], 'L0_tok_Wq': _L0_tok_in['Wq'], 'L0_tok_Wk': _L0_tok_in['Wk'], 'L0_tok_Wv': _L0_tok_in['Wv'], 'L0_tok_Wo': _L0_tok_in['Wo'], 'L0_tok_ff_w1': _L0_tok_in['ff_w1'], 'L0_tok_ff_b1': _L0_tok_in['ff_b1'], 'L0_tok_ff_w2': _L0_tok_in['ff_w2'], 'L0_tok_ff_b2': _L0_tok_in['ff_b2'], 'L0_tok_ln1_w': _L0_tok_in['ln1_w'], 'L0_tok_ln1_b': _L0_tok_in['ln1_b'], 'L0_tok_ln2_w': _L0_tok_in['ln2_w'], 'L0_tok_ln2_b': _L0_tok_in['ln2_b'], 'L0_attn_Wq': _L0_attn_in['Wq'], 'L0_attn_Wk': _L0_attn_in['Wk'], 'L0_attn_Wv': _L0_attn_in['Wv'], 'L0_attn_Wo': _L0_attn_in['Wo'], 'L0_attn_bo': _L0_attn_in['bo'], 'L0_attn_P': _L0_attn_in['P'], 'L0_ffn_sg': _L0_ffn_in['sg'], 'L0_ffn_su': _L0_ffn_in['su'], 'L0_ffn_sd': _L0_ffn_in['sd'], 'L0_ffn_rg': _L0_ffn_in['rg'], 'L0_ffn_ru': _L0_ffn_in['ru'], 'L0_ffn_rd': _L0_ffn_in['rd'], 'L0_ffn_wr': _L0_ffn_in['wr'], 'L0_ffn_rb': _L0_ffn_in['rb']}

def reference(x, L0_tok_emb_table, L0_tok_Wq, L0_tok_Wk, L0_tok_Wv, L0_tok_Wo, L0_tok_ff_w1, L0_tok_ff_b1, L0_tok_ff_w2, L0_tok_ff_b2, L0_tok_ln1_w, L0_tok_ln1_b, L0_tok_ln2_w, L0_tok_ln2_b, L0_attn_Wq, L0_attn_Wk, L0_attn_Wv, L0_attn_Wo, L0_attn_bo, L0_attn_P, L0_ffn_sg, L0_ffn_su, L0_ffn_sd, L0_ffn_rg, L0_ffn_ru, L0_ffn_rd, L0_ffn_wr, L0_ffn_rb):
    import jax
    import jax.numpy as jnp

    def _L0_tok_ref(source, emb_table, Wq, Wk, Wv, Wo, ff_w1, ff_b1, ff_w2, ff_b2, ln1_w, ln1_b, ln2_w, ln2_b):
        import jax, jax.numpy as jnp
        import numpy as np
        N_BLOCKS = 6
        D_MODEL = 256
        N_HEADS = 8
        D_K = D_MODEL // N_HEADS
        D_FF = 1024
        VSIZE = 8000
        B, LS = (4, 512)
        LN_EPS = 1e-05

        def _layernorm(x, w, b):
            m = jnp.mean(x, axis=-1, keepdims=True)
            v = jnp.mean((x - m) ** 2, axis=-1, keepdims=True)
            return (x - m) * jax.lax.rsqrt(v + LN_EPS) * w + b
        x = emb_table[source]
        Bx, L, Dm = x.shape
        n_blocks = Wq.shape[0]
        for i in range(n_blocks):
            heads = jnp.einsum('bld,hkd->blhk', x, Wq[i]).reshape(Bx, L, Dm)
            z1 = heads @ Wo[i].T
            a1 = _layernorm(z1 + x, ln1_w[i], ln1_b[i])
            h = jax.nn.relu(a1 @ ff_w1[i].T + ff_b1[i])
            z2 = h @ ff_w2[i].T + ff_b2[i]
            x = _layernorm(z2 + a1, ln2_w[i], ln2_b[i])
        return x

    def _L0_attn_ref(x, Wq, Wk, Wv, Wo, bo, P):
        import jax, jax.numpy as jnp
        import numpy as np
        B, N, D, H, DH, M = (4, 1024, 256, 16, 64, 64)
        EPS = 0.0001

        def softmax_kernel(data, P, is_query):
            dn = data.shape[-1] ** (-0.25)
            ratio = P.shape[0] ** (-0.5)
            dd = jnp.einsum('bhnd,md->bhnm', dn * data, P)
            diag = (jnp.sum(data * data, axis=-1) * 0.5 * dn * dn)[..., None]
            if is_query:
                mx = jnp.max(dd, axis=-1, keepdims=True)
            else:
                mx = jnp.max(dd)
            return ratio * (jnp.exp(dd - diag - mx) + EPS)
        b, n, _ = x.shape

        def proj(W):
            return (x @ W).reshape(b, n, H, DH).transpose(0, 2, 1, 3)
        q, k, v = (proj(Wq), proj(Wk), proj(Wv))
        qp = softmax_kernel(q, P, is_query=True)
        kp = softmax_kernel(k, P, is_query=False)
        k_cumsum = kp.sum(axis=-2)
        D_inv = 1.0 / jnp.einsum('bhnm,bhm->bhn', qp, k_cumsum)
        ctx = jnp.einsum('bhnm,bhne->bhme', kp, v)
        out = jnp.einsum('bhme,bhnm,bhn->bhne', ctx, qp, D_inv)
        out = out.transpose(0, 2, 1, 3).reshape(b, n, H * DH)
        return out @ Wo + bo

    def _L0_ffn_ref(x, sg, su, sd, rg, ru, rd, wr, rb):
        import jax, jax.numpy as jnp
        import numpy as np
        H, I, E_ROUTED, TOP_K = (256, 704, 7, 2)
        B, S = (4, 512)

        def _expert(h, g, u, d):
            return jnp.einsum('...i,hi->...h', jax.nn.silu(h @ g.T) * (h @ u.T), d)
        shared_out = _expert(x, sg, su, sd)
        logits = x @ wr.T + rb
        probs = jax.nn.softmax(logits, axis=-1)
        scores, idx = jax.lax.top_k(probs, TOP_K)
        scores = scores / scores.sum(axis=-1, keepdims=True)
        w = jnp.sum(scores[..., None] * jax.nn.one_hot(idx, E_ROUTED, dtype=x.dtype), axis=-2)
        out = shared_out
        for e in range(E_ROUTED):
            out = out + w[..., e:e + 1] * _expert(x, rg[e], ru[e], rd[e])
        return out
    h = _L0_tok_ref(x, L0_tok_emb_table, L0_tok_Wq, L0_tok_Wk, L0_tok_Wv, L0_tok_Wo, L0_tok_ff_w1, L0_tok_ff_b1, L0_tok_ff_w2, L0_tok_ff_b2, L0_tok_ln1_w, L0_tok_ln1_b, L0_tok_ln2_w, L0_tok_ln2_b)
    h = h + _L0_attn_ref(_layernorm(h, axis=-1), L0_attn_Wq, L0_attn_Wk, L0_attn_Wv, L0_attn_Wo, L0_attn_bo, L0_attn_P)
    h = h + _L0_ffn_ref(_layernorm(h, axis=-1), L0_ffn_sg, L0_ffn_su, L0_ffn_sd, L0_ffn_rg, L0_ffn_ru, L0_ffn_rd, L0_ffn_wr, L0_ffn_rb)
    return h

_drawn_inputs = setup_inputs


def setup_inputs(seed=0):
    import zlib

    import numpy as np

    out = dict(_drawn_inputs(seed))
    spreads = {'L0_tok_ff_b1': (0.0, 0.1),
     'L0_tok_ff_b2': (0.0, 0.1),
     'L0_tok_ln1_w': (1.0, 0.2),
     'L0_tok_ln1_b': (0.0, 0.1),
     'L0_tok_ln2_w': (1.0, 0.2),
     'L0_tok_ln2_b': (0.0, 0.1),
     'L0_attn_bo': (0.0, 0.1),
     'L0_ffn_rb': (0.0, 0.8)}
    factors = {'L0_attn_Wq': 8.0,
     'L0_attn_Wk': 8.0,
     'L0_attn_P': 8.0,
     'L0_ffn_sg': 4.032,
     'L0_ffn_su': 3.775,
     'L0_ffn_sd': 3.872,
     'L0_ffn_rg': 5.563,
     'L0_ffn_ru': 5.263,
     'L0_ffn_rd': 4.995,
     'L0_ffn_wr': 5.616}
    for name, (base, spread) in spreads.items():
        noise = np.random.default_rng([zlib.crc32(name.encode()), seed]).standard_normal(out[name].shape)
        drawn = base * np.exp(spread * noise) if base else spread * noise
        out[name] = jnp.asarray(drawn.astype(out[name].dtype))
    for name, factor in factors.items():
        out[name] = (out[name] * factor).astype(out[name].dtype)
    return out
```

```python
from contextlib import ExitStack

import numpy as np
import concourse.bass as bass
from concourse import mybir

F32 = mybir.dt.float32
I32 = mybir.dt.int32
U32 = mybir.dt.uint32
ALU = mybir.AluOpType
ACT = mybir.ActivationFunctionType
AX = mybir.AxisListType
RMAX = bass.bass_isa.ReduceOp.max
ds = bass.ds

P = 128
T = 2048
NT = T // P
D = 256
KD = D // P
NL = 6
F = 1024
FC = F // P
GT = 4
NG = NT // GT
GN = GT * P
V = 8000
H = 16
DH = 64
HD = H * DH
NP = H // 2
HALF = HD // 2
HH = H // 2
PW = P + 2
NE = 7
FI = 704
FIC = 6
U = 256
NR = 2 * T // U + NE
NS = T // U
NU = NR + NS
EW = KD * FI * 2 + FIC * D
COLV = FC + 4 * KD
LN_EPS = 1e-5
EPS = 1e-4
DN = DH ** -0.25
NB = 4


def build(nc, d, out):
    ctx = ExitStack()
    with ctx:
        def sem(name):
            return ctx.enter_context(nc.semaphore(name))

        def allocator(stack):
            return lambda name, shape, dt=F32: stack.enter_context(nc.sbuf_tensor(name, shape, dt))

        bank = [ctx.enter_context(nc.psum_tensor(f"bank{i}", [P, 512], F32)) for i in range(8)]
        slots_x = nc.dram_tensor("slots_x", (NU * U, D), F32, kind="Internal").ap()
        slots_y = nc.dram_tensor("slots_y", (NU * U, D), F32, kind="Internal").ap()

        sb = allocator(ctx)
        ident = sb("ident", [P, P])
        eps_t = sb("eps_t", [P, 1])
        hres = sb("hres", [P, NT * D])
        hn = sb("hn", [P, NT * D])
        lnst = sb("lnst", [P, GT, 6])
        lnm4 = sb("lnm4", [P, GT * 2])
        lnmv = sb("lnmv", [P, NT * 2])
        lnsd = sb("lnsd", [P, NT])
        lnrs = sb("lnrs", [P, NT])
        wqkv = sb("wqkv", [P, 3, KD, HD])
        wqkT = sb("wqkT", [P, 2, NP, D])
        wo = sb("wo", [P, NP, D])
        bp = sb("bp", [P, P])
        rowv = sb("rowv", [P, 3, D])

        phase = ExitStack()
        sb = allocator(phase)
        ids = sb("ids", [P, NT], I32)
        idf = sb("idf", [P, NT])
        neg = sb("neg", [P, NT])
        idu = sb("idu", [P, NT], I32)
        eye2 = sb("eye2", [P, KD, D])
        mixw = sb("mixw", [P, 4, D])
        mixT = sb("mixT", [P, KD, D])
        w1T = sb("w1T", [P, KD, F])
        w2T = sb("w2T", [P, FC, D])
        colv = sb("colv", [P, NL * COLV])
        ln1row = sb("ln1row", [P, 3, NL * D])
        xn = [sb(f"xn{g}", [P, GT, D]) for g in range(NG)]
        xT = sb("xT", [P, KD, GN])
        an = [sb(f"an{i}", [P, GT, D]) for i in range(2)]
        ares = [sb(f"ares{i}", [P, GT, D]) for i in range(2)]
        aT = sb("aT", [P, KD, GN])
        hT = sb("hT", [P, FC, GN])
        s2 = sb("s2", [P, GT, D])
        stat = [sb(f"stat{i}", [P, GT, 6]) for i in range(2)]
        mv = [sb(f"mv{i}", [P, GT, 2]) for i in range(2)]
        sd = [sb(f"sd{i}", [P, GT]) for i in range(2)]
        rs = [sb(f"rs{i}", [P, GT]) for i in range(2)]
        phase.close()

        phase = ExitStack()
        sb = allocator(phase)
        wp = sb("wp", [P, 2, KD, HD])
        hnT_all = sb("hnT_all", [P, NT * D])
        hnT = [sb(f"hnT{i}", [P, KD, P]) for i in range(2)]
        zero = sb("zero", [P, 512])
        keys = ExitStack()
        sb = allocator(keys)
        ddk = sb("ddk", [P, NT * HD])
        sq = [sb(f"sq{i}", [P, HALF]) for i in range(2)]
        dg = [sb(f"dg{i}", [P, HH]) for i in range(2)]
        mxk = sb("mxk", [P, 2 * NT])
        mx1 = sb("mx1", [P, 1])
        mxa = sb("mxa", [P, 1])
        nmx = sb("nmx", [P, 1])
        kp = [sb(f"kp{i}", [P, HD]) for i in range(2)]
        vx = [sb(f"vx{i}", [P, NP, PW]) for i in range(2)]
        keys.close()
        sb = allocator(phase)
        ctxs = sb("ctxs", [P, NP, P])
        kcol = sb("kcol", [P, NP])
        kcb = sb("kcb", [P, NP, P])
        ctxT = sb("ctxT", [P, NP, P])
        kcum = sb("kcum", [P, HD])
        cmat = sb("cmat", [P, NP, D])
        qsq = [sb(f"qsq{i}", [P, HALF]) for i in range(2)]
        qd = [sb(f"qd{i}", [P, HALF]) for i in range(2)]
        qe = [sb(f"qe{i}", [P, HALF]) for i in range(2)]
        qt = sb("qt", [P, HALF])
        qp = [sb(f"qp{i}", [P, HALF]) for i in range(2)]
        qT = [sb(f"qT{i}", [P, 4, P]) for i in range(2)]
        qs = sb("qs", [P, 4, HH])
        qr = sb("qr", [P, 2, HH])
        phase.close()

        sb = allocator(ctx)
        wrT = sb("wrT", [P, KD, 8])
        rb = sb("rb", [P, 8])
        rT = [sb(f"rT{i}", [P, KD, P]) for i in range(2)]
        lg = sb("lg", [P, NT, 8])
        pr = sb("pr", [P, NT, 8])
        rsm = sb("rsm", [P, 3, NT])
        top = sb("top", [P, NT, 8])
        idx = sb("idx", [P, NT, 8], U32)
        idxf = sb("idxf", [P, 2, NT])
        io8 = sb("io8", [P, 8])
        io8i = sb("io8i", [P, 8], I32)
        io256 = sb("io256", [P, 8])
        ioui = sb("ioui", [P, NU], I32)
        iou = sb("iou", [P, NU])
        hot = [sb(f"hot{i}", [P, NT, 8]) for i in range(2)]
        hots = sb("hots", [P, NT, 8])
        tri = sb("tri", [P, P])
        ones = sb("ones", [P, P])
        tot = sb("tot", [P, NT + 1, 8])
        pos = sb("pos", [P, NT, 8])
        over = sb("over", [P, 8, 8])
        ended = sb("ended", [P, NU, 8])
        nun = sb("nun", [P, 8])
        off = sb("off", [P, 9])
        offs = sb("offs", [P, 9])
        pick = sb("pick", [P, NT, 8])
        slotf = sb("slotf", [P, 2, NT])
        sloti = sb("sloti", [P, 2 * NT], I32)
        wsc = sb("wsc", [P, 2, NT])
        uef = sb("uef", [P, NU])
        uei = sb("uei", [P, NU], I32)
        we = [sb(f"we{i}", [P, EW]) for i in range(2)]
        xs = [sb(f"xs{i}", [P, 2, D]) for i in range(2)]
        xsT = sb("xsT", [P, KD, U])
        sg = [sb(f"sg{i}", [P, U]) for i in range(2)]
        hx = sb("hx", [P, FIC, U])
        ys = [sb(f"ys{i}", [P, 2, D]) for i in range(2)]
        y1 = [sb(f"y1_{i}", [P, D]) for i in range(NB)]
        y2 = [sb(f"y2_{i}", [P, D]) for i in range(NB)]
        y3 = [sb(f"y3_{i}", [P, D]) for i in range(NB)]
        yo = [sb(f"yo_{i}", [P, D]) for i in range(NB)]

        cst, cst_ok, waited = sem("cst"), sem("cst_ok"), sem("waited")
        ids_in, ids_step, gathered = sem("ids_in"), sem("ids_step"), [sem(f"gathered{g}") for g in range(NG)]
        vec_in, rows_ok, aw_in = sem("vec_in"), sem("rows_ok"), sem("aw_in")
        mix_in, w1_in, w2_in = sem("mix_in"), sem("w1_in"), sem("w2_in")
        mm_done, mix_ok = sem("mm_done"), sem("mix_ok")
        xn_ok, tx_done, xt_ok = sem("xn_ok"), sem("tx_done"), sem("xt_ok")
        s_done, ln1_step, std1, an_ok = sem("s_done"), sem("ln1_step"), sem("std1"), sem("an_ok")
        ares_half, ares_ok = sem("ares_half"), sem("ares_ok")
        ta_done, at_ok, h_done, h_evac = sem("ta_done"), sem("at_ok"), sem("h_done"), sem("h_evac")
        z_done, s2_ok, ln2_step, std2 = sem("z_done"), sem("s2_ok"), sem("ln2_step"), sem("std2")
        hres_half, hres_ok = sem("hres_half"), sem("hres_ok")
        lnb_step = [sem(f"lnb_step{i}") for i in range(2)]
        lnb_std = [sem(f"lnb_std{i}") for i in range(2)]
        lnb_ok = [sem(f"lnb_ok{i}") for i in range(2)]
        wp_done, wp_ok, ta2_done, ta2_ok = sem("wp_done"), sem("wp_ok"), sem("ta2_done"), sem("ta2_ok")
        hnT_in = [sem(f"hnT_in{i}") for i in range(2)]
        k_done, kd_done, sq_ok, dg_ok, ddk_ok = sem("k_done"), sem("kd_done"), sem("sq_ok"), sem("dg_ok"), sem("ddk_ok")
        mx_step, mxa_ok, nmx_ok = sem("mx_step"), sem("mxa_ok"), sem("nmx_ok")
        z0_done, kset = sem("z0_done"), sem("kset")
        v_done, vx_ok, ke_ok, kp_ok, ctx_done = sem("v_done"), sem("vx_ok"), sem("ke_ok"), sem("kp_ok"), sem("ctx_done")
        ctxs_ok, ct_done, ct_ok, kc_done, kc_ok = sem("ctxs_ok"), sem("ct_done"), sem("ct_ok"), sem("kc_done"), sem("kc_ok")
        c_done, c_ok = sem("c_done"), sem("c_ok")
        q_done, qdd_done, qsq_ok, aq_step, qd_ok = sem("q_done"), sem("qdd_done"), sem("qsq_ok"), sem("aq_step"), sem("qd_ok")
        qe_ok, bq_step, qp_ok, tq_done, qT_ok = sem("qe_ok"), sem("bq_step"), sem("qp_ok"), sem("tq_done"), sem("qT_ok")
        o_done, h2_ok, bo_ok = sem("o_done"), sem("h2_ok"), sem("bo_ok")
        rw_in, io_ok, rt_done, rT_ok, l_done = sem("rw_in"), sem("io_ok"), sem("rt_done"), sem("rT_ok"), sem("l_done")
        rt_step, pe_exp, hots_ok, cnt_done, slots_ok = sem("rt_step"), sem("pe_exp"), sem("hots_ok"), sem("cnt_done"), sem("slots_ok")
        zero_in, scattered, shared_in = sem("zero_in"), sem("scattered"), sem("shared_in")
        we_in, xs_in = [sem(f"we_in{i}") for i in range(2)], [sem(f"xs_in{i}") for i in range(2)]
        tu_done, xsT_ok, gu_done, sg_ok = sem("tu_done"), sem("xsT_ok"), sem("gu_done"), sem("sg_ok")
        hx_ok, y_done, ys_ok = sem("hx_ok"), sem("y_done"), sem("ys_ok")
        y_out = [sem(f"y_out{i}") for i in range(2)]
        y1_in, y2_in, y3_in, o_out = ([sem(f"{k}_{i}") for i in range(NB)] for k in ("y1_in", "y2_in", "y3_in", "o_out"))
        y1_in, y2_in, y3_in, o_out = list(y1_in), list(y2_in), list(y3_in), list(o_out)
        f_step, yo_ok = sem("f_step"), sem("yo_ok")

        block = ctx.enter_context(nc.Block())

        def alone(eng):
            eng.sem_inc(waited, 1)

        @block.sync
        def _(sp):
            sp.dma_start(ids[:], d["ids"]).then_inc(ids_in, 16)
            sp.dma_start(mixw[:], d["mixw"][0]).then_inc(mix_in, 16)
            sp.dma_start(colv[:], d["colv"]).then_inc(vec_in, 16)
            sp.dma_start(w1T[:], d["w1T"][0]).then_inc(w1_in, 16)
            sp.dma_start(w2T[:], d["w2T"][0]).then_inc(w2_in, 16)
            sp.dma_start(ln1row[:].rearrange("p a n -> p (a n)"),
                         d["ln1row"].rearrange("a n -> (a n)").partition_broadcast(P)).then_inc(vec_in, 16)
            sp.dma_start(rowv[:].rearrange("p a n -> p (a n)"),
                         d["rowv"].rearrange("a n -> (a n)").partition_broadcast(P)).then_inc(vec_in, 16)
            sp.dma_start(wqkv[:], d["wqkv"]).then_inc(aw_in, 16)
            sp.dma_start(wqkT[:], d["wqkT"]).then_inc(aw_in, 16)
            sp.dma_start(wo[:], d["wo"]).then_inc(aw_in, 16)
            sp.dma_start(bp[:], d["bp"]).then_inc(aw_in, 16)
            with sp.Fori(0, NL - 1) as l:
                sp.wait_ge(mm_done, l + 1)
                sp.dma_start(mixw[:], d["mixw"][ds(l + 1, 1)].rearrange("o p a n -> (o p) a n")).then_inc(mix_in, 16)
                sp.wait_ge(h_done, l * (NG * FC) + NG * FC)
                sp.dma_start(w1T[:], d["w1T"][ds(l + 1, 1)].rearrange("o p a n -> (o p) a n")).then_inc(w1_in, 16)
                sp.wait_ge(z_done, l * (2 * NG) + 2 * NG)
                sp.dma_start(w2T[:], d["w2T"][ds(l + 1, 1)].rearrange("o p a n -> (o p) a n")).then_inc(w2_in, 16)

            def hnT_load(b, t):
                sp.dma_start(hnT[b][:].rearrange("p a n -> p (a n)"), hnT_all[:, ds(t * D, D)]).then_inc(hnT_in[b], 16)

            for step, (used, per) in enumerate([(None, 0), (kd_done, 2), (v_done, 2)]):
                for b in range(2):
                    if step == 0:
                        sp.wait_ge(ta2_ok, 2 * NG)
                    else:
                        sp.wait_ge(used, per * (NT - 1 + b))
                    hnT_load(b, b)
                now = [kd_done, v_done, qdd_done][step]
                with sp.Fori(1, NT // 2) as i:
                    for b in range(2):
                        sp.wait_ge(now, i * 4 + (2 * b - 2))
                        hnT_load(b, i * 2 + b)

            sp.wait_ge(h2_ok, NT + 2)
            sp.dma_start(wrT[:], d["wrT"]).then_inc(rw_in, 16)
            sp.dma_start(rb[:], d["rb"].partition_broadcast(P)).then_inc(rw_in, 16)
            sp.wait_ge(slots_ok, 1)
            sp.wait_ge(zero_in, 16 * NR)

            def we_load(b, e):
                sp.dma_start(we[b][:], d["we"][ds(e, 1)].rearrange("o p n -> (o p) n")).then_inc(we_in[b], 16)

            def xs_load(b, u):
                sp.dma_start(xs[b][:], slots_x[ds(u * U, U), :].rearrange("(s p) n -> p s n", p=P)).then_inc(xs_in[b], 16)

            def expert(u):
                return sp.value_load(uei[0:1, ds(u, 1)], min_val=0, max_val=NE)

            def y_store(b, u):
                sp.wait_ge(ys_ok, u + 1)
                sp.dma_start(slots_y[ds(u * U, U), :].rearrange("(s p) n -> p s n", p=P), ys[b][:]).then_inc(y_out[b], 16)

            for b in range(2):
                we_load(b, expert(b))
            sp.wait_ge(lnb_ok[1], NT)
            sp.dma_start(slots_x[NR * U:NU * U, :].rearrange("(t p) n -> p t n", p=P),
                         hn[:].rearrange("p (t n) -> p t n", t=NT)).then_inc(shared_in, 16)
            sp.wait_ge(shared_in, 16)
            sp.wait_ge(scattered, 16 * 2 * NT)
            for b in range(2):
                xs_load(b, b)
            with sp.Fori(0, NU // 2 - 1) as i:
                for b in range(2):
                    sp.wait_ge(y_done, i * 2 + (b + 1))
                    we_load(b, expert(i * 2 + (b + 2)))
                    xs_load(b, i * 2 + (b + 2))
                    y_store(b, i * 2 + b)
            sp.wait_ge(y_done, NU - 2)
            we_load(0, expert(NU - 1))
            xs_load(0, NU - 1)
            for u in range(NU - 3, NU):
                y_store(u % 2, u)
            sp.wait_ge(y_out[0], 16 * (NU // 2 + 1))
            sp.wait_ge(y_out[1], 16 * (NU // 2))
            def store_out(t):
                sp.wait_ge(yo_ok, t + 1)
                sp.dma_start(out[t * P:(t + 1) * P, :], yo[t % NB][:]).then_inc(o_out[t % NB], 16)

            for t in range(NT):
                b = t % NB
                if t >= NB:
                    sp.wait_ge(yo_ok, t - NB + 1)
                sp.dma_start(y3[b][:], slots_y[NR * U + t * P:NR * U + (t + 1) * P, :]).then_inc(y3_in[b], 16)
                if t >= 2:
                    store_out(t - 2)
            for t in (NT - 2, NT - 1):
                store_out(t)
            for b in range(NB):
                sp.wait_ge(o_out[b], 16 * (NT // NB))

        @block.gpsimd
        def _(pool):
            pool.memset(ident[:], 0.0).then_inc(cst, 1)
            pool.memset(eye2[:], 0.0).then_inc(cst, 1)
            pool.memset(eps_t[:], LN_EPS).then_inc(cst_ok, 1)
            pool.wait_ge(cst, 2)
            pool.affine_select(out=ident[:], in_=ident[:], compare_op=ALU.not_equal, fill=1.0, base=0,
                               pattern=[[-1, P]], channel_multiplier=1).then_inc(cst_ok, 1)
            pool.affine_select(out=eye2[:], in_=eye2[:], compare_op=ALU.not_equal, fill=1.0, base=0,
                               pattern=[[P, KD], [-1, D]], channel_multiplier=1).then_inc(cst_ok, 1)
            pool.wait_ge(ids_step, 4)
            for t in range(NT):
                pool.indirect_dma_start(out=hn[:, t * D:(t + 1) * D], out_offset=None, in_=d["emb"],
                                        in_offset=bass.IndirectOffsetOnAxis(ap=idu[:, t:t + 1], axis=0))\
                    .then_inc(gathered[t // GT], 16)
            pool.wait_ge(vec_in, 48)
            pool.tensor_tensor(ln1row[:, 1, :], ln1row[:, 1, :], ln1row[:, 2, :], ALU.add).then_inc(rows_ok, 1)
            pool.wait_ge(rows_ok, 1)

            def residual(l, n, b):
                pool.wait_ge(an_ok, n + 1)
                alone(pool)
                pool.tensor_tensor(ares[b][:], an[b][:],
                                   ln1row[:, 0, ds(l * D, D)].unsqueeze(1).to_broadcast([P, GT, D]), ALU.mult)\
                    .then_inc(ares_half, 1)
                pool.wait_ge(ares_half, n + 1)
                alone(pool)
                pool.tensor_tensor(ares[b][:], ares[b][:],
                                   ln1row[:, 1, ds(l * D, D)].unsqueeze(1).to_broadcast([P, GT, D]), ALU.add)\
                    .then_inc(ares_ok, 1)

            with pool.Fori(0, NL - 1) as l:
                for u in range(NG):
                    residual(l, l * NG + u, u % 2)
            for u in range(NG):
                residual(NL - 1, (NL - 1) * NG + u, u % 2)
            for g in range(NG):
                hg = hres[:, g * GT * D:(g + 1) * GT * D].rearrange("p (t n) -> p t n", t=GT)
                pool.wait_ge(xn_ok, NL * NG + g + 1)
                pool.tensor_tensor(hg, xn[g][:], rowv[:, 0:1, :].to_broadcast([P, GT, D]), ALU.mult).then_inc(hres_half, 1)
                pool.wait_ge(hres_half, g + 1)
                pool.tensor_tensor(hg, hg, rowv[:, 1:2, :].to_broadcast([P, GT, D]), ALU.add).then_inc(hres_ok, 1)
            pool.memset(zero[:], 0.0).then_inc(kset, 1)
            for b in range(2):
                pool.memset(vx[b][:, :, P:PW], 1.0).then_inc(kset, 1)
            pool.wait_ge(kset, 1)
            for i in range(NR):
                pool.dma_start(slots_x[i * 2 * P:(i + 1) * 2 * P, :].rearrange("(s p) n -> p s n", p=P),
                               zero[:].rearrange("p (s n) -> p s n", s=2)).then_inc(zero_in, 16)
            pool.wait_ge(lnb_ok[0], NT)
            pool.tensor_tensor(hres[:].rearrange("p (t n) -> p t n", t=NT), hres[:].rearrange("p (t n) -> p t n", t=NT),
                               rowv[:, 2:3, :].to_broadcast([P, NT, D]), ALU.add).then_inc(bo_ok, 1)
            pool.wait_ge(mx_step, 1)
            pool.partition_all_reduce(mxa[:], mx1[:], P, RMAX).then_inc(mxa_ok, 1)
            pool.wait_ge(h2_ok, NT + 2)
            pool.memset(ones[:], 1.0).then_inc(io_ok, 1)
            pool.iota(io8i[:], [[1, 8]], base=0, channel_multiplier=0).then_inc(io_ok, 1)
            pool.iota(ioui[:], [[1, NU]], base=0, channel_multiplier=0).then_inc(io_ok, 1)
            pool.wait_ge(io_ok, 1)
            pool.affine_select(out=tri[:], in_=ones[:], compare_op=ALU.is_gt, fill=0.0, base=0,
                               pattern=[[1, P]], channel_multiplier=-1).then_inc(io_ok, 1)
            pool.wait_ge(zero_in, 16 * NR)
            pool.wait_ge(slots_ok, 1)
            pool.wait_ge(lnb_ok[1], NT)
            for k in range(2):
                for t in range(NT):
                    pool.indirect_dma_start(out=slots_x, out_offset=bass.IndirectOffsetOnAxis(
                        ap=sloti[:, k * NT + t:k * NT + t + 1], axis=0),
                        in_=hn[:, t * D:(t + 1) * D], in_offset=None).then_inc(scattered, 16)
            pool.wait_ge(y_out[0], 16 * (NU // 2 + 1))
            pool.wait_ge(y_out[1], 16 * (NU // 2))
            for t in range(NT):
                b = t % NB
                if t >= NB:
                    pool.wait_ge(yo_ok, t - NB + 1)
                for k, (y, y_in) in enumerate([(y1, y1_in), (y2, y2_in)]):
                    pool.indirect_dma_start(out=y[b][:], out_offset=None, in_=slots_y,
                                            in_offset=bass.IndirectOffsetOnAxis(
                                                ap=sloti[:, k * NT + t:k * NT + t + 1], axis=0)).then_inc(y_in[b], 16)

        @block.tensor
        def _(pe):
            def mm_mix(l):
                pe.wait_ge(mix_in, l * 16 + 16)
                for ic in range(KD):
                    for jc in range(KD):
                        mm = pe.matmul(bank[0][:, ic * D:(ic + 1) * D], mixw[:, jc, ic * P:(ic + 1) * P],
                                       mixw[:, KD + jc, :], start=(jc == 0), stop=(jc == KD - 1))
                mm.then_inc(mm_done, 1)

            def turn_x(n, g):
                pe.wait_ge(xn_ok, n + 1)
                for c in range(KD):
                    for t in range(GT):
                        mm = pe.transpose(bank[c][:, t * P:(t + 1) * P], xn[g][:, t, c * P:(c + 1) * P], ident[:])
                mm.then_inc(tx_done, 1)

            def turn_a(n, b):
                pe.wait_ge(an_ok, n + 1)
                for c in range(KD):
                    for t in range(GT):
                        mm = pe.transpose(bank[c][:, t * P:(t + 1) * P], an[b][:, t, c * P:(c + 1) * P], ident[:])
                mm.then_inc(ta_done, 1)

            def mix(n):
                pe.wait_ge(xt_ok, n + 1)
                for t in range(GT):
                    for kc in range(KD):
                        mm = pe.matmul(bank[2 + t // 2][:, (t % 2) * D:(t % 2 + 1) * D], xT[:, kc, t * P:(t + 1) * P],
                                       mixT[:, kc, :], start=(kc == 0), stop=(kc == KD - 1))
                    if t % 2:
                        mm.then_inc(s_done, 1)

            def widen(l, n, first_waits=True):
                pe.wait_ge(w1_in, l * 16 + 16)
                pe.wait_ge(at_ok, n + 1)
                for c in range(FC):
                    if c >= 2:
                        pe.wait_ge(h_evac, n * FC + (c - 1))
                    for kc in range(KD):
                        mm = pe.matmul(bank[4 + c % 2][:], w1T[:, kc, c * P:(c + 1) * P], aT[:, kc, :],
                                       start=(kc == 0), stop=(kc == KD - 1))
                    mm.then_inc(h_done, 1)

            def narrow(l, n, half):
                if half == 0:
                    pe.wait_ge(w2_in, l * 16 + 16)
                    pe.wait_ge(h_evac, n * FC + FC)
                    pe.wait_ge(s2_ok, n * 2)
                for t in (2 * half, 2 * half + 1):
                    for c in range(FC):
                        mm = pe.matmul(bank[6 + half][:, (t % 2) * D:(t % 2 + 1) * D], hT[:, c, t * P:(t + 1) * P],
                                       w2T[:, c, :], start=(c == 0), stop=(c == FC - 1))
                mm.then_inc(z_done, 1)

            def group(l, u, last):
                n = l * NG + u
                ahead2 = not last or u + 2 < NG
                ahead1 = not last or u + 1 < NG
                if u == 2 and not last:
                    pe.wait_ge(at_ok, n + 1)
                    mm_mix(l + 1)
                widen(l, n)
                if ahead2:
                    if u == 2:
                        pe.wait_ge(mix_ok, l + 2)
                    turn_x(n + 2, (u + 2) % NG)
                narrow(l, n, 0)
                if ahead1:
                    if ahead2:
                        pe.wait_ge(xt_ok, n + 3)
                    turn_a(n + 1, (u + 1) % 2)
                narrow(l, n, 1)
                if ahead2:
                    pe.wait_ge(an_ok, n + 2)
                    mix(n + 2)

            pe.wait_ge(cst_ok, 3)
            mm_mix(0)
            pe.wait_ge(mix_ok, 1)
            turn_x(0, 0)
            mix(0)
            turn_x(1, 1)
            pe.wait_ge(an_ok, 1)
            mix(1)
            turn_a(0, 0)
            with pe.Fori(0, NL - 1) as l:
                for u in range(NG):
                    group(l, u, False)
            for u in range(NG):
                group(NL - 1, u, True)

            pe.wait_ge(aw_in, 64)
            pe.wait_ge(at_ok, NL * NG)
            pe.wait_ge(an_ok, NL * NG)
            i = 0
            for w in range(2):
                for ic in range(KD):
                    for hf in range(2):
                        if i >= 4:
                            pe.wait_ge(wp_ok, i - 3)
                        for q in range(4):
                            mm = pe.matmul(bank[i % 4][:, q * P:(q + 1) * P], wqkT[:, w, hf * 4 + q, ic * P:(ic + 1) * P],
                                           bp[:], start=True, stop=True)
                        mm.then_inc(wp_done, 1)
                        i += 1
            pe.wait_ge(h_evac, NL * NG * FC)
            pe.wait_ge(s2_ok, NL * NG * 2)
            for i in range(2 * NG):
                pe.wait_ge(lnb_ok[0], 2 * i + 2)
                if i >= 4:
                    pe.wait_ge(ta2_ok, i - 3)
                for j in range(4):
                    t, c = 2 * i + j // 2, j % 2
                    mm = pe.transpose(bank[4 + i % 4][:, j * P:(j + 1) * P], hn[:, t * D + c * P:t * D + (c + 1) * P], ident[:])
                mm.then_inc(ta2_done, 1)

            def project(b, dst, w, hf, done):
                for kc in range(KD):
                    mm = pe.matmul(bank[dst][:], hnT[b][:, kc, :], w[:, kc, hf * HALF:(hf + 1) * HALF],
                                   start=(kc == 0), stop=(kc == KD - 1))
                mm.then_inc(done, 1)

            pe.wait_ge(wp_ok, 8)
            with pe.Fori(0, NT // 2) as i:
                for b in range(2):
                    pe.wait_ge(hnT_in[b], i * 16 + 16)
                    for hf in range(2):
                        w = i * 4 + (2 * b + hf)
                        pe.wait_ge(sq_ok, w + 1)
                        project(b, 2 * hf, wqkv[:, 1], hf, k_done)
                        pe.wait_ge(ddk_ok, w + 1)
                        project(b, 2 * hf + 1, wp[:, 1], hf, kd_done)

            pe.sem_inc(ctx_done, 2)
            pe.sem_inc(tq_done, 2)
            cbank = [6, 7, 0]
            pe.wait_ge(ta2_ok, 2 * NG)
            pe.wait_ge(kset, 3)
            pe.wait_ge(sq_ok, 2 * NT + 2)
            for c in range(3):
                mm = pe.matmul(bank[cbank[c]][:, 0:3 * PW], zero[:, 0:P], zero[:, 0:3 * PW], start=True, stop=False,
                               skip_group_check=True)
            mm.then_inc(z0_done, 1)
            with pe.Fori(0, NT // 2) as i:
                for b in range(2):
                    pe.wait_ge(hnT_in[b], i * 16 + 16 * (NT // 2 + 1))
                    for hf in range(2):
                        pe.wait_ge(vx_ok, i * 4 + (2 * b + hf + 1))
                        project(b, 4 + hf, wqkv[:, 2], hf, v_done)
                for b in range(2):
                    pe.wait_ge(kp_ok, i * 2 + (b + 1))
                    pe.wait_ge(vx_ok, i * 4 + (2 * b + 4))
                    for p in range(NP):
                        mm = pe.matmul(bank[cbank[p // 3]][:, (p % 3) * PW:(p % 3 + 1) * PW], kp[b][:, p * P:(p + 1) * P],
                                       vx[b][:, p, :], start=False, stop=False, skip_group_check=True)
                    mm.then_inc(ctx_done, 1)
            pe.wait_ge(ctxs_ok, 12)
            for p in range(NP):
                mm = pe.transpose(bank[1 + p // 4][:, (p % 4) * P:(p % 4 + 1) * P], ctxs[:, p, :], ident[:])
            mm.then_inc(ct_done, 1)
            for p in range(NP):
                mm = pe.matmul(bank[3 + p // 4][:, (p % 4) * P:(p % 4 + 1) * P], kcb[:, p, :], ident[:], start=True, stop=True)
            mm.then_inc(kc_done, 1)
            pe.wait_ge(ct_ok, 2)
            for p in range(NP):
                mm = pe.matmul(bank[(5 + p // 2) % 8][:, (p % 2) * D:(p % 2 + 1) * D], ctxT[:, p, :], wo[:, p, :],
                               start=True, stop=True)
            mm.then_inc(c_done, 1)

            pe.wait_ge(c_ok, 4)
            pe.wait_ge(kc_ok, 2)

            def query(i, j):
                b, hf, w = j // 2 % 2, j % 2, i * 4 + j
                if hf == 0:
                    pe.wait_ge(hnT_in[b], i * 16 + 16 * (NT + 1 + j // 4))
                pe.wait_ge(qsq_ok, w + 1)
                project(b, 2 * hf, wqkv[:, 0], hf, q_done)
                pe.wait_ge(qd_ok, w + 1)
                project(b, 2 * hf + 1, wp[:, 0], hf, qdd_done)

            def turn_features(i, j):
                hf = j % 2
                pe.wait_ge(qp_ok, i * 4 + (j + 3))
                for p in range(4):
                    mm = pe.transpose(bank[4 + hf][:, p * P:(p + 1) * P], qp[hf][:, p * P:(p + 1) * P], ident[:])
                mm.then_inc(tq_done, 1)

            def attended(i, j):
                b, hf = j // 2 % 2, j % 2
                pe.wait_ge(qT_ok, i * 4 + (j + 1))
                if hf == 0:
                    pe.wait_ge(h2_ok, i * 2 + (j // 2 + 1))
                for p in range(4):
                    mm = pe.matmul(bank[6 + b][:, 0:D], qT[hf][:, p, :], cmat[:, hf * 4 + p, :],
                                   start=(hf == 0 and p == 0), stop=(hf == 1 and p == 3))
                if hf == 1:
                    mm.then_inc(o_done, 1)

            for j in range(4):
                query(0, j)
                if j == 3:
                    attended(0, 0)
                if j >= 2:
                    turn_features(0, j - 2)
            with pe.Fori(1, NT // 2) as i:
                for j in range(4):
                    query(i, j)
                    attended(i, j - 3)
                    turn_features(i, j - 2)
            last = NT // 2 - 1
            for j in (4, 5, 6):
                attended(last, j - 3)
                if j < 6:
                    turn_features(last, j - 2)

            pe.wait_ge(qsq_ok, 2 * NT + 2)
            pe.wait_ge(qd_ok, 2 * NT + 2)
            pe.wait_ge(rw_in, 32)

            def turn_r(t):
                pe.wait_ge(lnb_ok[1], t + 1)
                for c in range(KD):
                    mm = pe.transpose(bank[t % 2][:, c * P:(c + 1) * P], hn[:, t * D + c * P:t * D + (c + 1) * P], ident[:])
                mm.then_inc(rt_done, 1)

            turn_r(0)
            for t in range(NT):
                if t + 1 < NT:
                    turn_r(t + 1)
                pe.wait_ge(rT_ok, t + 1)
                for kc in range(KD):
                    mm = pe.matmul(bank[2][:, t * 8:(t + 1) * 8], rT[t % 2][:, kc, :], wrT[:, kc, :],
                                   start=(kc == 0), stop=(kc == KD - 1))
            mm.then_inc(l_done, 1)
            pe.wait_ge(io_ok, 4)
            pe.wait_ge(hots_ok, 1)
            hv = hots[:].rearrange("p t e -> p (t e)")
            pe.matmul(bank[3][:, 0:P], tri[:], hv, start=True, stop=True)
            pe.matmul(bank[3][:, P:2 * P], ones[:], hv, start=True, stop=True).then_inc(cnt_done, 1)

            wg = [w[:, 0:KD * FI].rearrange("p (k n) -> p k n", k=KD) for w in we]
            wu = [w[:, KD * FI:2 * KD * FI].rearrange("p (k n) -> p k n", k=KD) for w in we]
            wd = [w[:, 2 * KD * FI:EW].rearrange("p (c n) -> p c n", c=FIC) for w in we]

            def turn_slots(b, loads):
                pe.wait_ge(xs_in[b], loads)
                for kc in range(KD):
                    for s in range(2):
                        mm = pe.transpose(bank[b][:, kc * U + s * P:kc * U + (s + 1) * P], xs[b][:, s, kc * P:(kc + 1) * P],
                                          ident[:])
                mm.then_inc(tu_done, 1)

            def gate_up(i, b):
                u = i * 2 + b
                pe.wait_ge(we_in[b], i * 16 + 16)
                pe.wait_ge(xsT_ok, u + 1)
                for c in range(FIC):
                    m = min(P, FI - c * P)
                    bk = bank[2 + (FIC * b + c) % 4]
                    pe.wait_ge(hx_ok, i * (2 * FIC) + (b * FIC + c + 1))
                    for k, w in enumerate((wg, wu)):
                        for kc in range(KD):
                            mm = pe.matmul(bk[0:m, k * U:(k + 1) * U], w[b][:, kc, c * P:c * P + m], xsT[:, kc, :],
                                           start=(kc == 0), stop=(kc == KD - 1))
                    mm.then_inc(gu_done, 1)

            def down(i, b):
                u = i * 2 + b
                pe.wait_ge(hx_ok, i * (2 * FIC) + (b * FIC + FIC + 4))
                pe.wait_ge(ys_ok, u)
                for s in range(2):
                    for c in range(FIC):
                        m = min(P, FI - c * P)
                        mm = pe.matmul(bank[6 + b][:, s * D:(s + 1) * D], hx[0:m, c, s * P:(s + 1) * P], wd[b][0:m, c, :],
                                       start=(c == 0), stop=(c == FIC - 1))
                mm.then_inc(y_done, 1)

            turn_slots(0, 16)
            with pe.Fori(0, NU // 2) as i:
                for b in range(2):
                    gate_up(i, b)
                    turn_slots(1 - b, i * 16 + 16 * (b + 1))
                    down(i, b)
            gate_up(NU // 2, 0)
            down(NU // 2, 0)

        @block.scalar
        def _(act):
            def widened(l, n):
                for c in range(FC):
                    act.wait_ge(h_done, n * FC + (c + 1))
                    alone(act)
                    act.activation(hT[:, c, :], bank[4 + c % 2][:], ACT.Relu, bias=colv[:, ds(l * COLV + c, 1)])\
                        .then_inc(h_evac, 1)

            def turned(done, n, dst, l, at, ok):
                act.wait_ge(done, n + 1)
                alone(act)
                for c in range(KD):
                    ins = act.activation(dst[:, c, :], bank[c][:], ACT.Identity,
                                         scale=colv[:, ds(l * COLV + (at + c), 1)],
                                         bias=colv[:, ds(l * COLV + (at + KD + c), 1)])
                ins.then_inc(ok, 1)

            def root(step, n, i, std):
                act.wait_ge(step, n * 3 + 2)
                act.activation(sd[i][:], mv[i][:, :, 1], ACT.Sqrt, bias=eps_t[:, 0:1]).then_inc(std, 1)

            def group(l, u, last):
                n = l * NG + u
                ahead2 = not last or u + 2 < NG
                ahead1 = not last or u + 1 < NG
                widened(l, n)
                if ahead2:
                    turned(tx_done, n + 2, xT, l if u < 2 else l + 1, FC + 2 * KD, xt_ok)
                if ahead1:
                    turned(ta_done, n + 1, aT, l if u < 3 else l + 1, FC, at_ok)
                root(ln2_step, n, 1, std2)
                if ahead2:
                    root(ln1_step, n + 2, 0, std1)

            act.wait_ge(vec_in, 48)
            act.wait_ge(cst_ok, 3)
            turned(tx_done, 0, xT, 0, FC + 2 * KD, xt_ok)
            root(ln1_step, 0, 0, std1)
            turned(tx_done, 1, xT, 0, FC + 2 * KD, xt_ok)
            root(ln1_step, 1, 0, std1)
            turned(ta_done, 0, aT, 0, FC, at_ok)
            with act.Fori(0, NL - 1) as l:
                for u in range(NG):
                    group(l, u, False)
            for u in range(NG):
                group(NL - 1, u, True)

            def root_all(i):
                act.wait_ge(lnb_step[i], 3 * NG)
                act.activation(lnsd[:], lnmv[:].rearrange("p (t k) -> p t k", k=2)[:, :, 1], ACT.Sqrt,
                               bias=eps_t[:, 0:1]).then_inc(lnb_std[i], 1)

            root_all(0)
            act.wait_ge(hres_ok, NG)
            i = 0
            for w in range(2):
                for ic in range(KD):
                    for hf in range(2):
                        act.wait_ge(wp_done, i + 1)
                        act.activation(wp[:, w, ic, hf * HALF:(hf + 1) * HALF], bank[i % 4][:], ACT.Copy, scale=DN)\
                            .then_inc(wp_ok, 1)
                        i += 1
            for i in range(2 * NG):
                act.wait_ge(ta2_done, i + 1)
                act.activation(hnT_all[:, i * 512:(i + 1) * 512], bank[4 + i % 4][:], ACT.Copy).then_inc(ta2_ok, 1)

            act.sem_inc(sq_ok, 2)
            with act.Fori(0, NT // 2) as i:
                for j in range(4):
                    act.wait_ge(k_done, i * 4 + (j + 1))
                    act.wait_ge(dg_ok, i * 4 + (j + 1))
                    act.activation(sq[j % 2][:], bank[2 * (j % 2)][:], ACT.Square, scale=0.25).then_inc(sq_ok, 1)
            act.sem_inc(vx_ok, 2)
            act.wait_ge(nmx_ok, 1)
            act.wait_ge(kset, 3)
            with act.Fori(0, NT // 2) as i:
                for b in range(2):
                    act.wait_ge(ctx_done, i * 2 + (b + 1))
                    alone(act)
                    act.activation(kp[b][:], ddk[:, ds(i * (2 * HD) + b * HD, HD)], ACT.Exp, bias=nmx[:, 0:1])\
                        .then_inc(ke_ok, 1)
                    for hf in range(2):
                        act.wait_ge(v_done, i * 4 + (2 * b + hf + 1))
                        act.activation(vx[b][:, 4 * hf:4 * hf + 4, 0:P], bank[4 + hf][:].rearrange("p (a n) -> p a n", a=4),
                                       ACT.Copy).then_inc(vx_ok, 1)
            act.wait_ge(ct_done, 1)
            for k in range(2):
                act.activation(ctxT[:, 4 * k:4 * k + 4, :].rearrange("p a n -> p (a n)"), bank[1 + k][:], ACT.Copy)\
                    .then_inc(ct_ok, 1)
            act.wait_ge(c_done, 1)
            for k in range(4):
                act.activation(cmat[:, 2 * k:2 * k + 2, :].rearrange("p a n -> p (a n)"), bank[(5 + k) % 8][:], ACT.Copy)\
                    .then_inc(c_ok, 1)

            def q_turned(i, j):
                act.wait_ge(tq_done, i * 4 + (j + 3))
                act.activation(qT[j % 2][:].rearrange("p a n -> p (a n)"), bank[4 + j % 2][:], ACT.Copy).then_inc(qT_ok, 1)

            def q_square(i, j):
                act.wait_ge(q_done, i * 4 + (j + 1))
                act.activation(qsq[j % 2][:], bank[2 * (j % 2)][:], ACT.Square, scale=0.25).then_inc(qsq_ok, 1)

            def q_exp(i, j):
                act.wait_ge(qd_ok, i * 4 + (j + 3))
                act.wait_ge(qp_ok, i * 4 + (j + 1))
                act.activation(qe[j % 2][:], qd[j % 2][:], ACT.Exp).then_inc(qe_ok, 1)

            act.sem_inc(qsq_ok, 2)
            for j in range(4):
                if j == 3:
                    q_turned(0, 0)
                q_square(0, j)
                if j >= 1:
                    q_exp(0, j - 1)
            with act.Fori(1, NT // 2) as i:
                for j in range(4):
                    q_turned(i, j - 3)
                    q_square(i, j)
                    q_exp(i, j - 1)
            last = NT // 2 - 1
            q_turned(last, 1)
            q_exp(last, 3)
            q_turned(last, 2)
            q_turned(last, 3)

            root_all(1)
            for t in range(NT):
                act.wait_ge(rt_done, t + 1)
                act.activation(rT[t % 2][:].rearrange("p a n -> p (a n)"), bank[t % 2][:, 0:D], ACT.Copy).then_inc(rT_ok, 1)
            act.wait_ge(rt_step, 3)
            act.activation(pr[:], pr[:], ACT.Exp).then_inc(pe_exp, 1)

            def turned_slots(i, b):
                act.wait_ge(tu_done, i * 2 + (b + 1))
                act.activation(xsT[:].rearrange("p a n -> p (a n)"), bank[b % 2][:], ACT.Copy).then_inc(xsT_ok, 1)

            def gates(i, b):
                for c in range(FIC):
                    m = min(P, FI - c * P)
                    act.wait_ge(gu_done, i * (2 * FIC) + (b * FIC + c + 1))
                    act.wait_ge(hx_ok, i * (2 * FIC) + (b * FIC + c + 3))
                    act.activation(sg[c % 2][0:m, :], bank[2 + (FIC * b + c) % 4][0:m, 0:U], ACT.Silu).then_inc(sg_ok, 1)

            def outputs(i, b):
                u = i * 2 + b
                act.wait_ge(y_done, u + 1)
                if isinstance(i, int):
                    act.wait_ge(y_out[b], 16 * i)
                else:
                    act.wait_ge(y_out[b], i * 16)
                act.activation(ys[b][:].rearrange("p a n -> p (a n)"), bank[6 + b][:], ACT.Copy).then_inc(ys_ok, 1)

            turned_slots(0, 0)
            with act.Fori(0, NU // 2) as i:
                for b in range(2):
                    gates(i, b)
                    turned_slots(i, b + 1)
                    outputs(i, b)
            gates(NU // 2, 0)
            outputs(NU // 2, 0)

        @block.vector
        def _(dve):
            dve.wait_ge(ids_in, 16)
            dve.tensor_copy(idf[:], ids[:]).then_inc(ids_step, 1)
            dve.wait_ge(ids_step, 1)
            dve.tensor_scalar(neg[:], idf[:], 0.0, float(V), ALU.is_lt, ALU.mult).then_inc(ids_step, 1)
            dve.wait_ge(ids_step, 2)
            dve.tensor_tensor(idf[:], idf[:], neg[:], ALU.add).then_inc(ids_step, 1)
            dve.wait_ge(ids_step, 3)
            dve.tensor_scalar(idu[:], idf[:], 0.0, float(V - 1), ALU.max, ALU.min).then_inc(ids_step, 1)

            def embed(g):
                dve.wait_ge(gathered[g], 16 * GT)
                dve.tensor_copy(xn[g][:].rearrange("p a n -> p (a n)"), hn[:, g * GT * D:(g + 1) * GT * D]).then_inc(xn_ok, 1)

            def mixed(l):
                dve.wait_ge(mm_done, l + 1)
                dve.tensor_tensor(mixT[:].rearrange("p a n -> p (a n)"), bank[0][:], eye2[:].rearrange("p a n -> p (a n)"),
                                  ALU.add).then_inc(mix_ok, 1)

            def norm(n, i, src, step, std, dst, ok):
                for t in range(GT):
                    ins = dve.bn_stats(stat[i][:, t, :], src(t))
                ins.then_inc(step, 1)
                dve.wait_ge(step, n * 3 + 1)
                alone(dve)
                for t in range(GT):
                    ins = dve.bn_aggr(mv[i][:, t, :], stat[i][:, t, :])
                ins.then_inc(step, 1)
                dve.wait_ge(std, n + 1)
                dve.reciprocal(rs[i][:], sd[i][:]).then_inc(step, 1)
                dve.wait_ge(step, n * 3 + 3)
                for t in range(GT):
                    ins = dve.tensor_scalar(dst[:, t, :], src(t), mv[i][:, t, 0:1], rs[i][:, t:t + 1], ALU.subtract, ALU.mult)
                ins.then_inc(ok, 1)

            def norm1(n, b):
                dve.wait_ge(s_done, n * 2 + 2)
                norm(n, 0, lambda t: bank[2 + t // 2][:, (t % 2) * D:(t % 2 + 1) * D], ln1_step, std1, an[b], an_ok)

            def norm2(n, u):
                dve.wait_ge(xn_ok, n + NG)
                dve.wait_ge(ares_ok, n + 1)
                for half in range(2):
                    dve.wait_ge(z_done, n * 2 + (half + 1))
                    dve.tensor_tensor(s2[:, 2 * half:2 * half + 2, :].rearrange("p a n -> p (a n)"), bank[6 + half][:],
                                      ares[u % 2][:, 2 * half:2 * half + 2, :].rearrange("p a n -> p (a n)"), ALU.add)\
                        .then_inc(s2_ok, 1)
                dve.wait_ge(s2_ok, n * 2 + 2)
                norm(n, 1, lambda t: s2[:, t, :], ln2_step, std2, xn[u], xn_ok)

            def group(l, u, last):
                n = l * NG + u
                if u == 2 and not last:
                    mixed(l + 1)
                norm2(n, u)
                if not last or u + 2 < NG:
                    norm1(n + 2, u % 2)

            dve.wait_ge(cst_ok, 3)
            mixed(0)
            for g in range(NG):
                embed(g)
            norm1(0, 0)
            norm1(1, 1)
            with dve.Fori(0, NL - 1) as l:
                for u in range(NG):
                    group(l, u, False)
            for u in range(NG):
                group(NL - 1, u, True)

            def norm_all(k):
                with dve.Fori(0, NG) as g:
                    if k == 0:
                        dve.wait_ge(hres_ok, g + 1)
                    else:
                        dve.wait_ge(h2_ok, g * GT + (GT + 2))
                    for t in range(GT):
                        ins = dve.bn_stats(lnst[:, t, :], hres[:, ds(g * (GT * D) + t * D, D)])
                    ins.then_inc(lnb_step[k], 1)
                    dve.wait_ge(lnb_step[k], g * 3 + 1)
                    alone(dve)
                    for t in range(GT):
                        ins = dve.bn_aggr(lnm4[:, 2 * t:2 * t + 2], lnst[:, t, :])
                    ins.then_inc(lnb_step[k], 1)
                    dve.wait_ge(lnb_step[k], g * 3 + 2)
                    dve.tensor_copy(lnmv[:, ds(g * (2 * GT), 2 * GT)], lnm4[:]).then_inc(lnb_step[k], 1)
                dve.wait_ge(lnb_std[k], 1)
                dve.reciprocal(lnrs[:], lnsd[:]).then_inc(lnb_step[k], 1)
                dve.wait_ge(lnb_step[k], 3 * NG + 1)
                with dve.Fori(0, NT) as t:
                    dve.tensor_scalar(hn[:, ds(t * D, D)], hres[:, ds(t * D, D)], lnmv[:, ds(t * 2, 1)], lnrs[:, ds(t, 1)],
                                      ALU.subtract, ALU.mult).then_inc(lnb_ok[k], 1)

            norm_all(0)

            def heads(ap):
                return ap.rearrange("p (h n) -> p h n", n=DH)

            def spread(ap):
                return ap.unsqueeze(2).to_broadcast([P, HH, DH])

            dve.sem_inc(dg_ok, 2)
            dve.sem_inc(ddk_ok, 2)
            with dve.Fori(0, NT // 2) as i:
                for j in range(4):
                    hf = j % 2
                    dve.wait_ge(kd_done, i * 4 + (j + 1))
                    dve.tensor_reduce(mxk[:, ds(i * 4 + j, 1)], bank[2 * hf + 1][:], AX.X, ALU.max)
                    dve.wait_ge(sq_ok, i * 4 + (j + 3))
                    dve.tensor_reduce(dg[hf][:], heads(sq[hf][:]), AX.X, ALU.add).then_inc(dg_ok, 1)
                    dve.wait_ge(dg_ok, i * 4 + (j + 3))
                    dve.tensor_tensor(heads(ddk[:, ds(i * (4 * HALF) + j * HALF, HALF)]), heads(bank[2 * hf + 1][:]),
                                      spread(dg[hf][:]), ALU.subtract).then_inc(ddk_ok, 1)
            dve.wait_ge(ddk_ok, 2 * NT + 2)
            dve.tensor_reduce(mx1[:], mxk[:], AX.X, ALU.max).then_inc(mx_step, 1)
            dve.wait_ge(mxa_ok, 1)
            dve.tensor_scalar(nmx[:], mxa[:], -1.0, None, ALU.mult).then_inc(nmx_ok, 1)
            with dve.Fori(0, NT // 2) as i:
                for b in range(2):
                    dve.wait_ge(ke_ok, i * 2 + (b + 1))
                    dve.tensor_scalar(kp[b][:], kp[b][:], EPS, None, ALU.add).then_inc(kp_ok, 1)

            dve.wait_ge(ctx_done, NT + 2)
            dve.memset(ctxs[:], 0.0).then_inc(ctxs_ok, 1)
            dve.wait_ge(ctxs_ok, 1)
            for c, (bk, np_) in enumerate([(6, 3), (7, 3), (0, 2)]):
                src = bank[bk][:, 0:np_ * PW].rearrange("p (a n) -> p a n", n=PW)
                for k in range(2):
                    r = slice(k * DH, (k + 1) * DH)
                    dve.tensor_copy(ctxs[r, 3 * c:3 * c + np_, r], src[r, :, r]).then_inc(ctxs_ok, 1)
                dve.tensor_copy(kcol[:, 3 * c:3 * c + np_], src[:, :, P]).then_inc(ctxs_ok, 1)
            dve.wait_ge(ctxs_ok, 10)
            for k in range(2):
                dve.tensor_copy(kcb[:, 4 * k:4 * k + 4, :], kcol[:, 4 * k:4 * k + 4].unsqueeze(2).to_broadcast([P, 4, P]))\
                    .then_inc(ctxs_ok, 1)
            dve.wait_ge(kc_done, 1)
            for k in range(2):
                dve.tensor_copy(kcum[:, k * HALF:(k + 1) * HALF], bank[3 + k][:]).then_inc(kc_ok, 1)

            def exponents(i, j):
                hf = j % 2
                src = bank[2 * hf + 1]
                dve.wait_ge(qdd_done, i * 4 + (j + 1))
                dve.tensor_reduce(qs[:, 0, :], heads(src[:]), AX.X, ALU.max)
                dve.wait_ge(qsq_ok, i * 4 + (j + 3))
                dve.tensor_reduce(qs[:, 1, :], heads(qsq[hf][:]), AX.X, ALU.add).then_inc(aq_step, 1)
                dve.wait_ge(aq_step, i * 8 + (2 * j + 1))
                dve.tensor_tensor(qs[:, 2, :], qs[:, 0, :], qs[:, 1, :], ALU.add).then_inc(aq_step, 1)
                dve.wait_ge(aq_step, i * 8 + (2 * j + 2))
                dve.tensor_tensor(heads(qd[hf][:]), heads(src[:]), spread(qs[:, 2, :]), ALU.subtract).then_inc(qd_ok, 1)

            def features(i, j):
                hf = j % 2
                dve.wait_ge(qe_ok, i * 4 + (j + 1))
                dve.scalar_tensor_tensor(out=qt[:], in0=qe[hf][:], scalar=EPS, in1=kcum[:, hf * HALF:(hf + 1) * HALF],
                                         op0=ALU.add, op1=ALU.mult).then_inc(bq_step, 1)
                dve.wait_ge(bq_step, i * 12 + (3 * j + 1))
                dve.tensor_reduce(qr[:, 0, :], heads(qt[:]), AX.X, ALU.add).then_inc(bq_step, 1)
                dve.wait_ge(bq_step, i * 12 + (3 * j + 2))
                dve.reciprocal(qr[:, 1, :], qr[:, 0, :]).then_inc(bq_step, 1)
                dve.wait_ge(bq_step, i * 12 + (3 * j + 3))
                dve.wait_ge(tq_done, i * 4 + (j + 1))
                dve.scalar_tensor_tensor(out=heads(qp[hf][:]), in0=heads(qe[hf][:]), scalar=EPS, in1=spread(qr[:, 1, :]),
                                         op0=ALU.add, op1=ALU.mult).then_inc(qp_ok, 1)

            def residual(i, b):
                dve.wait_ge(o_done, i * 2 + (b + 1))
                dve.tensor_tensor(hres[:, ds(i * (2 * D) + b * D, D)], bank[6 + b % 2][:, 0:D],
                                  hres[:, ds(i * (2 * D) + b * D, D)], ALU.add).then_inc(h2_ok, 1)

            dve.sem_inc(qd_ok, 2)
            dve.sem_inc(qp_ok, 2)
            dve.sem_inc(h2_ok, 2)
            dve.wait_ge(bo_ok, 1)
            for j in range(1, 4):
                exponents(0, j - 1)
                if j >= 2:
                    features(0, j - 2)
            with dve.Fori(1, NT // 2) as i:
                for j in range(4):
                    exponents(i, j - 1)
                    features(i, j - 2)
                    if j % 2 == 1:
                        residual(i, j // 2 - 2)
            last = NT // 2 - 1
            exponents(last, 3)
            features(last, 2)
            residual(last, 0)
            features(last, 3)
            residual(last, 1)
            norm_all(1)

            count = [0]

            def step(ins):
                count[0] += 1
                ins.then_inc(rt_step, 1)
                dve.wait_ge(rt_step, count[0])

            def over_experts(ap):
                return ap.unsqueeze(2).to_broadcast([P, NT, 8])

            dve.wait_ge(rw_in, 32)
            dve.wait_ge(l_done, 1)
            step(dve.tensor_tensor(lg[:], bank[2][:, 0:NT * 8].rearrange("p (t e) -> p t e", e=8),
                                   rb[:].unsqueeze(1).to_broadcast([P, NT, 8]), ALU.add))
            step(dve.tensor_reduce(rsm[:, 0, :], lg[:], AX.X, ALU.max))
            step(dve.tensor_tensor(pr[:], lg[:], over_experts(rsm[:, 0, :]), ALU.subtract))
            dve.wait_ge(pe_exp, 1)
            step(dve.tensor_reduce(rsm[:, 1, :], pr[:], AX.X, ALU.add))
            step(dve.reciprocal(rsm[:, 2, :], rsm[:, 1, :]))
            step(dve.tensor_tensor(pr[:], pr[:], over_experts(rsm[:, 2, :]), ALU.mult))
            for t in range(NT):
                ins = dve.max(top[:, t, :], pr[:, t, :])
            step(ins)
            for t in range(NT):
                ins = dve.max_index(idx[:, t, :], top[:, t, :], pr[:, t, :])
            step(ins)
            step(dve.tensor_tensor(rsm[:, 0, :], top[:, :, 0], top[:, :, 1], ALU.add))
            step(dve.reciprocal(rsm[:, 1, :], rsm[:, 0, :]))
            for k in range(2):
                step(dve.tensor_tensor(wsc[:, k, :], top[:, :, k], rsm[:, 1, :], ALU.mult))
                step(dve.tensor_copy(idxf[:, k, :], idx[:, :, k]))
            dve.wait_ge(io_ok, 4)
            step(dve.tensor_copy(io8[:], io8i[:]))
            step(dve.tensor_copy(iou[:], ioui[:]))
            step(dve.tensor_scalar(io256[:], io8[:], float(U), None, ALU.mult))
            for k in range(2):
                step(dve.tensor_tensor(hot[k][:], io8[:].unsqueeze(1).to_broadcast([P, NT, 8]), over_experts(idxf[:, k, :]),
                                       ALU.is_equal))
            dve.tensor_tensor(hots[:], hot[0][:], hot[1][:], ALU.add).then_inc(hots_ok, 1)
            step(dve.memset(tot[:, 0, :], 0.0))
            step(dve.memset(off[:], 0.0))
            dve.wait_ge(cnt_done, 1)
            counts = bank[3][:, P:2 * P].rearrange("p (t e) -> p t e", e=8)
            for t in range(NT):
                step(dve.tensor_tensor(tot[:, t + 1, :], counts[:, t, :], tot[:, t, :], ALU.add))
            step(dve.tensor_tensor(over[:], tot[:, NT, :].unsqueeze(2).to_broadcast([P, 8, 8]),
                                   io256[:].unsqueeze(1).to_broadcast([P, 8, 8]), ALU.is_gt))
            step(dve.tensor_reduce(nun[:], over[:], AX.X, ALU.add))
            for e in range(8):
                step(dve.tensor_tensor(off[:, e + 1:e + 2], off[:, e:e + 1], nun[:, e:e + 1], ALU.add))
            step(dve.tensor_scalar(offs[:], off[:], float(U), None, ALU.mult))
            step(dve.tensor_tensor(pos[:], bank[3][:, 0:P].rearrange("p (t e) -> p t e", e=8), tot[:, 0:NT, :], ALU.add))
            step(dve.tensor_tensor(pos[:], pos[:], offs[:, 0:8].unsqueeze(1).to_broadcast([P, NT, 8]), ALU.add))
            for k in range(2):
                step(dve.tensor_tensor(pick[:], hot[k][:], pos[:], ALU.mult))
                step(dve.tensor_reduce(slotf[:, k, :], pick[:], AX.X, ALU.add))
            step(dve.tensor_copy(sloti[:], slotf[:].rearrange("p k t -> p (k t)")))
            ne1 = NE - 1
            step(dve.tensor_tensor(ended[:, :, 0:ne1], iou[:].unsqueeze(2).to_broadcast([P, NU, ne1]),
                                   off[:, 1:NE].unsqueeze(1).to_broadcast([P, NU, ne1]), ALU.is_ge))
            step(dve.tensor_reduce(uef[:], ended[:, :, 0:ne1], AX.X, ALU.add))
            step(dve.memset(uef[:, NR:NU], float(NE)))
            dve.tensor_copy(uei[:], uef[:]).then_inc(slots_ok, 1)

            def unit(i, b):
                for c in range(FIC):
                    m = min(P, FI - c * P)
                    dve.wait_ge(sg_ok, i * (2 * FIC) + (b * FIC + c + 1))
                    dve.tensor_tensor(hx[0:m, c, :], bank[2 + (FIC * b + c) % 4][0:m, U:2 * U], sg[c % 2][0:m, :], ALU.mult)\
                        .then_inc(hx_ok, 1)

            dve.sem_inc(hx_ok, 4)
            with dve.Fori(0, NU // 2) as i:
                for b in range(2):
                    unit(i, b)
            unit(NU // 2, 0)

            for t in range(NT):
                b = t % NB
                n = 16 * (t // NB + 1)
                dve.wait_ge(y1_in[b], n)
                if t >= NB:
                    dve.wait_ge(o_out[b], n - 16)
                dve.scalar_tensor_tensor(out=yo[b][:], in0=y1[b][:], scalar=wsc[:, 0, t:t + 1],
                                         in1=hres[:, t * D:(t + 1) * D], op0=ALU.mult, op1=ALU.add).then_inc(f_step, 1)
                dve.wait_ge(f_step, 2 * t + 1)
                dve.wait_ge(y2_in[b], n)
                dve.scalar_tensor_tensor(out=yo[b][:], in0=y2[b][:], scalar=wsc[:, 1, t:t + 1], in1=yo[b][:],
                                         op0=ALU.mult, op1=ALU.add).then_inc(f_step, 1)
                dve.wait_ge(f_step, 2 * t + 2)
                dve.wait_ge(y3_in[b], n)
                dve.tensor_tensor(yo[b][:], yo[b][:], y3[b][:], ALU.add).then_inc(yo_ok, 1)


def kernel(**inputs):
    import concourse.bacc as bacc
    from concourse.bass_utils import run_bass_kernel_spmd

    a = {k: np.asarray(v) for k, v in inputs.items()}

    def chunks(w, n):
        lead = w.shape[:-2]
        return np.moveaxis(w.reshape(*lead, n, P, w.shape[-1]), -3, -2)

    wq = a["L0_tok_Wq"].reshape(NL, D, D)
    woT = a["L0_tok_Wo"].transpose(0, 2, 1)
    one, nil = np.ones((1, D), np.float32), np.zeros((1, D), np.float32)
    cols = [a["L0_tok_ff_b1"], a["L0_tok_ln1_w"], a["L0_tok_ln1_b"],
            np.concatenate([one, a["L0_tok_ln2_w"][:-1]]), np.concatenate([nil, a["L0_tok_ln2_b"][:-1]])]
    colv = np.concatenate([c.reshape(NL, -1, P) for c in cols], 1)
    pt = a["L0_attn_P"].T
    bp = np.zeros((P, P), np.float32)
    bp[:DH, :DH] = pt
    bp[DH:, DH:] = pt
    gate = np.concatenate([a["L0_ffn_rg"], a["L0_ffn_sg"][None]]).transpose(0, 2, 1)
    up = np.concatenate([a["L0_ffn_ru"], a["L0_ffn_su"][None]]).transpose(0, 2, 1)
    dn = np.concatenate([a["L0_ffn_rd"], a["L0_ffn_sd"][None]]).transpose(0, 2, 1)
    dn = np.concatenate([dn, np.zeros((NE + 1, FIC * P - FI, D), np.float32)], 1)
    flat = [w.reshape(NE + 1, P, -1) for w in (chunks(gate, KD), chunks(up, KD), chunks(dn, FIC))]
    arrays = {
        "ids": a["x"].reshape(NT, P).T,
        "emb": a["L0_tok_emb_table"],
        "mixw": np.concatenate([chunks(wq, KD), chunks(woT, KD)], 2),
        "w1T": chunks(a["L0_tok_ff_w1"].transpose(0, 2, 1), KD),
        "w2T": chunks(a["L0_tok_ff_w2"].transpose(0, 2, 1), FC),
        "colv": colv.transpose(2, 0, 1).reshape(P, -1),
        "ln1row": np.stack([a["L0_tok_ln1_w"].ravel(), a["L0_tok_ln1_b"].ravel(), a["L0_tok_ff_b2"].ravel()]),
        "rowv": np.stack([a["L0_tok_ln2_w"][-1], a["L0_tok_ln2_b"][-1], a["L0_attn_bo"]]),
        "wqkv": np.stack([chunks(a[f"L0_attn_W{k}"], KD) for k in "qkv"], 1),
        "wqkT": np.stack([chunks(a[f"L0_attn_W{k}"].T, NP) for k in "qk"], 1),
        "wo": chunks(a["L0_attn_Wo"], NP),
        "bp": bp,
        "wrT": chunks(np.concatenate([a["L0_ffn_wr"].T, np.zeros((D, 1), np.float32)], 1), KD),
        "rb": np.concatenate([a["L0_ffn_rb"], np.full((1,), -1e30, np.float32)]),
        "we": np.concatenate(flat, 2),
    }
    arrays = {k: np.ascontiguousarray(v) for k, v in arrays.items()}
    nc = bacc.Bacc("TRN2", target_bir_lowering=False, num_devices=1)
    d = {k: nc.dram_tensor(f"in_{k}", v.shape, mybir.dt.from_np(v.dtype), kind="ExternalInput").ap()
         for k, v in arrays.items()}
    out = nc.dram_tensor("out", (T, D), F32, kind="ExternalOutput").ap()
    build(nc, d, out)
    r = run_bass_kernel_spmd(nc, [{f"in_{k}": v for k, v in arrays.items()}], core_ids=[0])
    return r.results[0]["out"].reshape(1, T, D)
```

```python
from contextlib import ExitStack

import numpy as np
import concourse.bass as bass
from concourse import mybir

F32 = mybir.dt.float32
I32 = mybir.dt.int32
U32 = mybir.dt.uint32
ALU = mybir.AluOpType
ACT = mybir.ActivationFunctionType
AX = mybir.AxisListType
RMAX = bass.bass_isa.ReduceOp.max
ds = bass.ds

P = 128
T = 2048
NT = T // P
D = 256
KD = D // P
NL = 6
F = 1024
FC = F // P
GT = 4
NG = NT // GT
GN = GT * P
V = 8000
H = 16
DH = 64
HD = H * DH
NP = H // 2
HALF = HD // 2
HH = H // 2
PW = P + 2
NE = 7
FI = 704
FIC = 6
FH = FI // 2
NR = 2 * T // P + NE
NU = NT + NR
ND = P
MU = T // P
EW = KD * FI * 2 + FIC * D
COLV = FC + 4 * KD
LN_EPS = 1e-5
EPS = 1e-4
DN = DH ** -0.25
LG = 4


def build(nc, d, out):
    ctx = ExitStack()
    with ctx:
        def sem(name):
            return ctx.enter_context(nc.semaphore(name))

        def allocator(stack):
            return lambda name, shape, dt=F32: stack.enter_context(nc.sbuf_tensor(name, shape, dt))

        bank = [ctx.enter_context(nc.psum_tensor(f"bank{i}", [P, 512], F32)) for i in range(8)]
        slots_x = nc.dram_tensor("slots_x", (NR * P, D), F32, kind="Internal").ap()
        slots_a = nc.dram_tensor("slots_a", (NR * P, 1), I32, kind="Internal").ap()
        y_tok = nc.dram_tensor("y_tok", (2 * T + ND, D), F32, kind="Internal").ap()

        sb = allocator(ctx)
        ident = sb("ident", [P, P])
        eps_t = sb("eps_t", [P, 1])
        hres = sb("hres", [P, NT * D])
        hn = sb("hn", [P, NT * D])
        lnst = sb("lnst", [P, GT, 6])
        lnm4 = sb("lnm4", [P, GT * 2])
        lnmv = sb("lnmv", [P, NT * 2])
        lnsd = sb("lnsd", [P, NT])
        lnrs = sb("lnrs", [P, NT])
        wrT = sb("wrT", [P, KD, 8])
        rb = sb("rb", [P, 8])

        both = ExitStack()
        sb = allocator(both)
        wqkv = sb("wqkv", [P, 3, KD, HD])
        wqkT = sb("wqkT", [P, 2, NP, D])
        wo = sb("wo", [P, NP, D])
        bp = sb("bp", [P, P])
        rowv = sb("rowv", [P, 3, D])

        phase = ExitStack()
        sb = allocator(phase)
        ids = sb("ids", [P, NT], I32)
        idf = sb("idf", [P, NT])
        neg = sb("neg", [P, NT])
        idu = sb("idu", [P, NT], I32)
        eye2 = sb("eye2", [P, KD, D])
        mixw = sb("mixw", [P, 4, D])
        mixT = sb("mixT", [P, KD, D])
        w1T = sb("w1T", [P, KD, F])
        w2T = sb("w2T", [P, FC, D])
        colv = sb("colv", [P, NL * COLV])
        ln1row = sb("ln1row", [P, 3, NL * D])
        xn = [sb(f"xn{g}", [P, GT, D]) for g in range(NG)]
        xT = sb("xT", [P, KD, GN])
        an = [sb(f"an{i}", [P, GT, D]) for i in range(2)]
        ares = [sb(f"ares{i}", [P, GT, D]) for i in range(2)]
        aT = sb("aT", [P, KD, GN])
        hT = sb("hT", [P, FC, GN])
        s2 = sb("s2", [P, GT, D])
        stat = [sb(f"stat{i}", [P, GT, 6]) for i in range(2)]
        mv = [sb(f"mv{i}", [P, GT, 2]) for i in range(2)]
        sd = [sb(f"sd{i}", [P, GT]) for i in range(2)]
        rs = [sb(f"rs{i}", [P, GT]) for i in range(2)]
        phase.close()

        phase = ExitStack()
        sb = allocator(phase)
        wp = sb("wp", [P, 2, KD, HD])
        hnT_all = sb("hnT_all", [P, NT * D])
        hnT = [sb(f"hnT{i}", [P, KD, P]) for i in range(2)]
        zero = sb("zero", [P, 512])
        keys = ExitStack()
        sb = allocator(keys)
        ddk = sb("ddk", [P, NT * HD])
        sq = [sb(f"sq{i}", [P, HALF]) for i in range(2)]
        dg = [sb(f"dg{i}", [P, HH]) for i in range(2)]
        mxk = sb("mxk", [P, 2 * NT])
        mx1 = sb("mx1", [P, 1])
        mxa = sb("mxa", [P, 1])
        nmx = sb("nmx", [P, 1])
        kp = [sb(f"kp{i}", [P, HD]) for i in range(2)]
        vx = [sb(f"vx{i}", [P, NP, PW]) for i in range(2)]
        keys.close()
        sb = allocator(phase)
        ctxs = sb("ctxs", [P, NP, P])
        kcol = sb("kcol", [P, NP])
        kcb = sb("kcb", [P, NP, P])
        ctxT = sb("ctxT", [P, NP, P])
        kcum = sb("kcum", [P, HD])
        cmat = sb("cmat", [P, NP, D])
        qsq = [sb(f"qsq{i}", [P, HALF]) for i in range(2)]
        qd = [sb(f"qd{i}", [P, HALF]) for i in range(2)]
        qe = [sb(f"qe{i}", [P, HALF]) for i in range(2)]
        qt = sb("qt", [P, HALF])
        qp = [sb(f"qp{i}", [P, HALF]) for i in range(2)]
        qT = [sb(f"qT{i}", [P, 4, P]) for i in range(2)]
        qs = sb("qs", [P, 4, HH])
        qr = sb("qr", [P, 2, HH])
        phase.close()
        both.close()

        sb = allocator(ctx)
        wall = sb("wall", [P, NE * EW])
        lg = sb("lg", [P, NT, 8])
        pr = sb("pr", [P, NT, 8])
        rsm = sb("rsm", [P, 3, NT])
        top = sb("top", [P, NT, 8])
        idx = sb("idx", [P, NT, 8], U32)
        idxf = sb("idxf", [P, 2, NT])
        io8 = sb("io8", [P, MU])
        io8i = sb("io8i", [P, MU], I32)
        iou8 = sb("iou8", [P, MU])
        ioui = sb("ioui", [P, NR], I32)
        iou = sb("iou", [P, NR])
        hot = [sb(f"hot{i}", [P, NT, 8]) for i in range(2)]
        hots = sb("hots", [P, NT, 8])
        tri = sb("tri", [P, P])
        ones = sb("ones", [P, P])
        tot = sb("tot", [P, NT + 1, 8])
        pos = sb("pos", [P, NT, 8])
        over = sb("over", [P, 8, MU])
        ended = sb("ended", [P, NR, NE - 1])
        nun = sb("nun", [P, 8])
        off = sb("off", [P, 9])
        offs = sb("offs", [P, 9])
        pick = sb("pick", [P, NT, 8])
        slotf = sb("slotf", [P, 2, NT])
        sloti = sb("sloti", [P, 2 * NT], I32)
        wsc = sb("wsc", [P, 2, NT])
        uef = sb("uef", [P, NR])
        uei = sb("uei", [P, NR], I32)
        asg = sb("asg", [P, 2 * NT], I32)
        dump = sb("dump", [P, P], I32)
        sa = sb("sa", [P, NR], I32)
        xT1 = [sb(f"xT1_{i}", [P, KD, P]) for i in range(2)]
        sg = [sb(f"sg{i}", [P, FH]) for i in range(2)]
        h = sb("h", [P, FIC * P])
        hhT = sb("hhT", [P, FIC, P])
        ys = [sb(f"ys{i}", [P, D]) for i in range(2)]
        rT = sb("rT", [P, NT * D])
        wsh = sb("wsh", [P, EW])
        xs = [rT[:, i * D:(i + 1) * D] for i in range(2)]
        yl = [hn, rT]

        cst, cst_ok, waited = sem("cst"), sem("cst_ok"), sem("waited")
        ids_in, ids_step, gathered = sem("ids_in"), sem("ids_step"), [sem(f"gathered{g}") for g in range(NG)]
        vec_in, rows_ok, aw_in = sem("vec_in"), sem("rows_ok"), sem("aw_in")
        mix_in, w1_in, w2_in = sem("mix_in"), sem("w1_in"), sem("w2_in")
        mm_done, mix_ok = sem("mm_done"), sem("mix_ok")
        xn_ok, tx_done, xt_ok = sem("xn_ok"), sem("tx_done"), sem("xt_ok")
        s_done, ln1_step, std1, an_ok = sem("s_done"), sem("ln1_step"), sem("std1"), sem("an_ok")
        ares_half, ares_ok = sem("ares_half"), sem("ares_ok")
        ta_done, at_ok, h_done, h_evac = sem("ta_done"), sem("at_ok"), sem("h_done"), sem("h_evac")
        z_done, s2_ok, ln2_step, std2 = sem("z_done"), sem("s2_ok"), sem("ln2_step"), sem("std2")
        hres_half, hres_ok = sem("hres_half"), sem("hres_ok")
        lnb_step = [sem(f"lnb_step{i}") for i in range(2)]
        lnb_std = [sem(f"lnb_std{i}") for i in range(2)]
        lnb_ok = [sem(f"lnb_ok{i}") for i in range(2)]
        wp_done, wp_ok, ta2_done, ta2_ok = sem("wp_done"), sem("wp_ok"), sem("ta2_done"), sem("ta2_ok")
        hnT_in = [sem(f"hnT_in{i}") for i in range(2)]
        k_done, kd_done, sq_ok, dg_ok, ddk_ok = sem("k_done"), sem("kd_done"), sem("sq_ok"), sem("dg_ok"), sem("ddk_ok")
        mx_step, mxa_ok, nmx_ok = sem("mx_step"), sem("mxa_ok"), sem("nmx_ok")
        z0_done, kset = sem("z0_done"), sem("kset")
        v_done, vx_ok, ke_ok, kp_ok, ctx_done = sem("v_done"), sem("vx_ok"), sem("ke_ok"), sem("kp_ok"), sem("ctx_done")
        ctxs_ok, ct_done, ct_ok, kc_done, kc_ok = sem("ctxs_ok"), sem("ct_done"), sem("ct_ok"), sem("kc_done"), sem("kc_ok")
        c_done, c_ok = sem("c_done"), sem("c_ok")
        q_done, qdd_done, qsq_ok, aq_step, qd_ok = sem("q_done"), sem("qdd_done"), sem("qsq_ok"), sem("aq_step"), sem("qd_ok")
        qe_ok, bq_step, qp_ok, tq_done, qT_ok = sem("qe_ok"), sem("bq_step"), sem("qp_ok"), sem("tq_done"), sem("qT_ok")
        o_done, h2_ok, bo_ok = sem("o_done"), sem("h2_ok"), sem("bo_ok")
        ln2p, ln2p_std, ln2p_ok = sem("ln2p"), sem("ln2p_std"), sem("ln2p_ok")
        rw_in, io_ok, rt_done, rT_ok, l_done = sem("rw_in"), sem("io_ok"), sem("rt_done"), sem("rT_ok"), sem("l_done")
        rt_step, pe_exp, hots_ok, cnt_done, slots_ok = sem("rt_step"), sem("pe_exp"), sem("hots_ok"), sem("cnt_done"), sem("slots_ok")
        zero_in, dump_in, scattered, ids_scattered = sem("zero_in"), sem("dump_in"), sem("scattered"), sem("ids_scattered")
        sa_in, sh_in, wall_in, pad_ok = sem("sa_in"), sem("sh_in"), sem("wall_in"), sem("pad_ok")
        xs_in = [sem(f"xs_in{i}") for i in range(2)]
        tu_done, xT1_ok, gu_done, sg_ok = sem("tu_done"), sem("xT1_ok"), sem("gu_done"), sem("sg_ok")
        h_ok, th_done, hhT_ok = sem("h_ok"), sem("th_done"), sem("hhT_ok")
        y_done, y_used = sem("y_done"), sem("y_used")
        y_out = [sem(f"y_out{i}") for i in range(2)]
        y_in = [sem(f"y_in{g}") for g in range(NT // LG)]
        f_step, yo_ok, o_out = sem("f_step"), sem("yo_ok"), sem("o_out")

        gub, thb, yb, xb, cb = [bank[0], bank[1], bank[4], bank[5]], [bank[2], bank[3]], bank[6], bank[7], bank[7]

        block = ctx.enter_context(nc.Block())

        def alone(eng):
            eng.sem_inc(waited, 1)

        @block.sync
        def _(sp):
            sp.dma_start(ids[:], d["ids"]).then_inc(ids_in, 16)
            sp.dma_start(mixw[:], d["mixw"][0]).then_inc(mix_in, 16)
            sp.dma_start(colv[:], d["colv"]).then_inc(vec_in, 16)
            sp.dma_start(w1T[:], d["w1T"][0]).then_inc(w1_in, 16)
            sp.dma_start(w2T[:], d["w2T"][0]).then_inc(w2_in, 16)
            sp.dma_start(ln1row[:].rearrange("p a n -> p (a n)"),
                         d["ln1row"].rearrange("a n -> (a n)").partition_broadcast(P)).then_inc(vec_in, 16)
            sp.dma_start(rowv[:].rearrange("p a n -> p (a n)"),
                         d["rowv"].rearrange("a n -> (a n)").partition_broadcast(P)).then_inc(vec_in, 16)
            sp.dma_start(wqkv[:], d["wqkv"]).then_inc(aw_in, 16)
            sp.dma_start(wqkT[:], d["wqkT"]).then_inc(aw_in, 16)
            sp.dma_start(wo[:], d["wo"]).then_inc(aw_in, 16)
            sp.dma_start(bp[:], d["bp"]).then_inc(aw_in, 16)
            sp.dma_start(wrT[:], d["wrT"]).then_inc(rw_in, 16)
            sp.dma_start(rb[:], d["rb"].partition_broadcast(P)).then_inc(rw_in, 16)
            with sp.Fori(0, NL - 1) as l:
                sp.wait_ge(mm_done, l + 1)
                sp.dma_start(mixw[:], d["mixw"][ds(l + 1, 1)].rearrange("o p a n -> (o p) a n")).then_inc(mix_in, 16)
                sp.wait_ge(h_done, l * (NG * FC) + NG * FC)
                sp.dma_start(w1T[:], d["w1T"][ds(l + 1, 1)].rearrange("o p a n -> (o p) a n")).then_inc(w1_in, 16)
                sp.wait_ge(z_done, l * (2 * NG) + 2 * NG)
                sp.dma_start(w2T[:], d["w2T"][ds(l + 1, 1)].rearrange("o p a n -> (o p) a n")).then_inc(w2_in, 16)

            def hnT_load(b, t):
                sp.dma_start(hnT[b][:].rearrange("p a n -> p (a n)"), hnT_all[:, ds(t * D, D)]).then_inc(hnT_in[b], 16)

            for step, (used, per) in enumerate([(None, 0), (kd_done, 2), (v_done, 2)]):
                for b in range(2):
                    if step == 0:
                        sp.wait_ge(ta2_ok, 2 * NG)
                    else:
                        sp.wait_ge(used, per * (NT - 1 + b))
                    hnT_load(b, b)
                if step == 2:
                    sp.wait_ge(ctx_done, NT + 2)
                    sp.dma_start(wsh[:], d["we"][NE]).then_inc(sh_in, 16)
                now = [kd_done, v_done, qdd_done][step]
                with sp.Fori(1, NT // 2) as i:
                    for b in range(2):
                        sp.wait_ge(now, i * 4 + (2 * b - 2))
                        hnT_load(b, i * 2 + b)

            sp.wait_ge(h2_ok, NT + 2)
            sp.wait_ge(zero_in, 16 * NR)
            for e in range(NE):
                sp.dma_start(wall[:, e * EW:(e + 1) * EW], d["we"][e]).then_inc(wall_in, 16)
            sp.wait_ge(ids_scattered, 16 * 2 * NT)
            sp.dma_start(sa[:], slots_a.rearrange("(u p) o -> p (u o)", p=P), allow_slow_non_contiguous=True).then_inc(sa_in, 16)

            def xs_load(b, r):
                sp.dma_start(xs[b], slots_x[ds(r * P, P), :]).then_inc(xs_in[b], 16)

            sp.wait_ge(scattered, 16 * 2 * NT)
            sp.wait_ge(xT1_ok, NT)
            for b in range(2):
                xs_load(b, b)
            with sp.Fori(0, NR // 2 - 1) as i:
                for b in range(2):
                    sp.wait_ge(tu_done, i * 2 + (b + 1))
                    xs_load(b, i * 2 + (b + 2))
            sp.wait_ge(tu_done, NR - 2)
            xs_load(0, NR - 1)
            sp.wait_ge(y_out[0], 16 * ((NR + 1) // 2))
            sp.wait_ge(y_out[1], 16 * (NR // 2))
            for g in range(NT // LG):
                for k in range(2):
                    r = k * T + g * LG * P
                    sp.dma_start(yl[k][:, g * LG * D:(g + 1) * LG * D].rearrange("p (t n) -> p t n", t=LG),
                                 y_tok[r:r + LG * P, :].rearrange("(t p) n -> p t n", p=P)).then_inc(y_in[g], 16)
            for g in range(NT // 2):
                sp.wait_ge(yo_ok, 2 * g + 2)
                sp.dma_start(out[g * 2 * P:(g + 1) * 2 * P, :].rearrange("(t p) n -> p t n", p=P),
                             hres[:, g * 2 * D:(g + 1) * 2 * D].rearrange("p (t n) -> p t n", t=2)).then_inc(o_out, 16)
            sp.wait_ge(o_out, 16 * (NT // 2))

        @block.gpsimd
        def _(pool):
            pool.memset(ident[:], 0.0).then_inc(cst, 1)
            pool.memset(eye2[:], 0.0).then_inc(cst, 1)
            pool.memset(eps_t[:], LN_EPS).then_inc(cst_ok, 1)
            pool.wait_ge(cst, 2)
            pool.affine_select(out=ident[:], in_=ident[:], compare_op=ALU.not_equal, fill=1.0, base=0,
                               pattern=[[-1, P]], channel_multiplier=1).then_inc(cst_ok, 1)
            pool.affine_select(out=eye2[:], in_=eye2[:], compare_op=ALU.not_equal, fill=1.0, base=0,
                               pattern=[[P, KD], [-1, D]], channel_multiplier=1).then_inc(cst_ok, 1)
            pool.wait_ge(ids_step, 4)
            for t in range(NT):
                pool.indirect_dma_start(out=hn[:, t * D:(t + 1) * D], out_offset=None, in_=d["emb"],
                                        in_offset=bass.IndirectOffsetOnAxis(ap=idu[:, t:t + 1], axis=0))\
                    .then_inc(gathered[t // GT], 16)
            pool.wait_ge(vec_in, 48)
            pool.tensor_tensor(ln1row[:, 1, :], ln1row[:, 1, :], ln1row[:, 2, :], ALU.add).then_inc(rows_ok, 1)
            pool.wait_ge(rows_ok, 1)

            def residual(l, n, b):
                pool.wait_ge(an_ok, n + 1)
                alone(pool)
                pool.tensor_tensor(ares[b][:], an[b][:],
                                   ln1row[:, 0, ds(l * D, D)].unsqueeze(1).to_broadcast([P, GT, D]), ALU.mult)\
                    .then_inc(ares_half, 1)
                pool.wait_ge(ares_half, n + 1)
                alone(pool)
                pool.tensor_tensor(ares[b][:], ares[b][:],
                                   ln1row[:, 1, ds(l * D, D)].unsqueeze(1).to_broadcast([P, GT, D]), ALU.add)\
                    .then_inc(ares_ok, 1)

            with pool.Fori(0, NL - 1) as l:
                for u in range(NG):
                    residual(l, l * NG + u, u % 2)
            for u in range(NG):
                residual(NL - 1, (NL - 1) * NG + u, u % 2)
            for g in range(NG):
                hg = hres[:, g * GT * D:(g + 1) * GT * D].rearrange("p (t n) -> p t n", t=GT)
                pool.wait_ge(xn_ok, NL * NG + g + 1)
                pool.tensor_tensor(hg, xn[g][:], rowv[:, 0:1, :].to_broadcast([P, GT, D]), ALU.mult).then_inc(hres_half, 1)
                pool.wait_ge(hres_half, g + 1)
                pool.tensor_tensor(hg, hg, rowv[:, 1:2, :].to_broadcast([P, GT, D]), ALU.add).then_inc(hres_ok, 1)
            pool.memset(zero[:], 0.0).then_inc(kset, 1)
            for b in range(2):
                pool.memset(vx[b][:, :, P:PW], 1.0).then_inc(kset, 1)
            pool.wait_ge(kset, 1)
            for i in range(NR):
                pool.dma_start(slots_x[i * P:(i + 1) * P, :], zero[:, 0:D]).then_inc(zero_in, 16)
            pool.wait_ge(lnb_ok[0], NT)
            pool.tensor_tensor(hres[:].rearrange("p (t n) -> p t n", t=NT), hres[:].rearrange("p (t n) -> p t n", t=NT),
                               rowv[:, 2:3, :].to_broadcast([P, NT, D]), ALU.add).then_inc(bo_ok, 1)
            pool.wait_ge(mx_step, 1)
            pool.partition_all_reduce(mxa[:], mx1[:], P, RMAX).then_inc(mxa_ok, 1)
            pool.wait_ge(h2_ok, NT + 2)
            pool.memset(ones[:], 1.0).then_inc(io_ok, 1)
            pool.iota(io8i[:], [[1, MU]], base=0, channel_multiplier=0).then_inc(io_ok, 1)
            pool.iota(ioui[:], [[1, NR]], base=0, channel_multiplier=0).then_inc(io_ok, 1)
            pool.wait_ge(io_ok, 1)
            pool.affine_select(out=tri[:], in_=ones[:], compare_op=ALU.is_gt, fill=0.0, base=0,
                               pattern=[[1, P]], channel_multiplier=-1).then_inc(io_ok, 1)
            pool.memset(h[:, FI:FIC * P], 0.0).then_inc(pad_ok, 1)
            pool.iota(asg[:], [[P, 2 * NT]], base=0, channel_multiplier=1).then_inc(io_ok, 1)
            pool.iota(dump[:], [[1, P]], base=2 * T, channel_multiplier=0).then_inc(io_ok, 1)
            pool.wait_ge(io_ok, 6)
            pool.dma_start(slots_a.rearrange("(u p) o -> u (p o)", p=P), dump[0:NR, :]).then_inc(dump_in, 16)
            pool.wait_ge(dump_in, 16)
            pool.wait_ge(zero_in, 16 * NR)
            pool.wait_ge(slots_ok, 1)
            for k in range(2):
                for t in range(NT):
                    at = bass.IndirectOffsetOnAxis(ap=sloti[:, k * NT + t:k * NT + t + 1], axis=0)
                    pool.indirect_dma_start(out=slots_x, out_offset=at, in_=hn[:, t * D:(t + 1) * D], in_offset=None)\
                        .then_inc(scattered, 16)
            for j in range(2 * NT):
                at = bass.IndirectOffsetOnAxis(ap=sloti[:, j:j + 1], axis=0)
                pool.indirect_dma_start(out=slots_a, out_offset=at, in_=asg[:, j:j + 1], in_offset=None)\
                    .then_inc(ids_scattered, 16)
            pool.wait_ge(sa_in, 16)
            for r in range(NR):
                pool.wait_ge(y_used, NT + r + 2)
                if r > 0:
                    pool.wait_ge(y_out[(r - 1) % 2], 16 * ((r - 1) // 2 + 1))
                pool.indirect_dma_start(out=y_tok, out_offset=bass.IndirectOffsetOnAxis(ap=sa[:, r:r + 1], axis=0),
                                        in_=ys[r % 2][:], in_offset=None).then_inc(y_out[r % 2], 16)

        @block.tensor
        def _(pe):
            def mm_mix(l):
                pe.wait_ge(mix_in, l * 16 + 16)
                for ic in range(KD):
                    for jc in range(KD):
                        mm = pe.matmul(bank[0][:, ic * D:(ic + 1) * D], mixw[:, jc, ic * P:(ic + 1) * P],
                                       mixw[:, KD + jc, :], start=(jc == 0), stop=(jc == KD - 1))
                mm.then_inc(mm_done, 1)

            def turn_x(n, g):
                pe.wait_ge(xn_ok, n + 1)
                for c in range(KD):
                    for t in range(GT):
                        mm = pe.transpose(bank[c][:, t * P:(t + 1) * P], xn[g][:, t, c * P:(c + 1) * P], ident[:])
                mm.then_inc(tx_done, 1)

            def turn_a(n, b):
                pe.wait_ge(an_ok, n + 1)
                for c in range(KD):
                    for t in range(GT):
                        mm = pe.transpose(bank[c][:, t * P:(t + 1) * P], an[b][:, t, c * P:(c + 1) * P], ident[:])
                mm.then_inc(ta_done, 1)

            def mix(n):
                pe.wait_ge(xt_ok, n + 1)
                for t in range(GT):
                    for kc in range(KD):
                        mm = pe.matmul(bank[2 + t // 2][:, (t % 2) * D:(t % 2 + 1) * D], xT[:, kc, t * P:(t + 1) * P],
                                       mixT[:, kc, :], start=(kc == 0), stop=(kc == KD - 1))
                    if t % 2:
                        mm.then_inc(s_done, 1)

            def widen(l, n, first_waits=True):
                pe.wait_ge(w1_in, l * 16 + 16)
                pe.wait_ge(at_ok, n + 1)
                for c in range(FC):
                    if c >= 2:
                        pe.wait_ge(h_evac, n * FC + (c - 1))
                    for kc in range(KD):
                        mm = pe.matmul(bank[4 + c % 2][:], w1T[:, kc, c * P:(c + 1) * P], aT[:, kc, :],
                                       start=(kc == 0), stop=(kc == KD - 1))
                    mm.then_inc(h_done, 1)

            def narrow(l, n, half):
                if half == 0:
                    pe.wait_ge(w2_in, l * 16 + 16)
                    pe.wait_ge(h_evac, n * FC + FC)
                    pe.wait_ge(s2_ok, n * 2 + 2)
                for t in (2 * half, 2 * half + 1):
                    for c in range(FC):
                        mm = pe.matmul(bank[6 + half][:, (t % 2) * D:(t % 2 + 1) * D], hT[:, c, t * P:(t + 1) * P],
                                       w2T[:, c, :], start=(c == 0), stop=(c == FC - 1))
                mm.then_inc(z_done, 1)

            def group(l, u, last):
                n = l * NG + u
                ahead2 = not last or u + 2 < NG
                ahead1 = not last or u + 1 < NG
                if u == 2 and not last:
                    pe.wait_ge(at_ok, n + 1)
                    mm_mix(l + 1)
                widen(l, n)
                if ahead2:
                    if u == 2:
                        pe.wait_ge(mix_ok, l + 2)
                    turn_x(n + 2, (u + 2) % NG)
                narrow(l, n, 0)
                if ahead1:
                    if ahead2:
                        pe.wait_ge(xt_ok, n + 3)
                    turn_a(n + 1, (u + 1) % 2)
                narrow(l, n, 1)
                if ahead2:
                    pe.wait_ge(an_ok, n + 2)
                    mix(n + 2)

            pe.wait_ge(cst_ok, 3)
            mm_mix(0)
            pe.wait_ge(mix_ok, 1)
            turn_x(0, 0)
            mix(0)
            turn_x(1, 1)
            pe.wait_ge(an_ok, 1)
            mix(1)
            turn_a(0, 0)
            with pe.Fori(0, NL - 1) as l:
                for u in range(NG):
                    group(l, u, False)
            for u in range(NG):
                group(NL - 1, u, True)

            pe.wait_ge(aw_in, 64)
            pe.wait_ge(at_ok, NL * NG)
            pe.wait_ge(an_ok, NL * NG)
            i = 0
            for w in range(2):
                for ic in range(KD):
                    for hf in range(2):
                        if i >= 4:
                            pe.wait_ge(wp_ok, i - 3)
                        for q in range(4):
                            mm = pe.matmul(bank[i % 4][:, q * P:(q + 1) * P], wqkT[:, w, hf * 4 + q, ic * P:(ic + 1) * P],
                                           bp[:], start=True, stop=True)
                        mm.then_inc(wp_done, 1)
                        i += 1
            pe.wait_ge(h_evac, NL * NG * FC)
            pe.wait_ge(s2_ok, NL * NG * 2 + 2)
            for i in range(2 * NG):
                pe.wait_ge(lnb_ok[0], 2 * i + 2)
                if i >= 4:
                    pe.wait_ge(ta2_ok, i - 3)
                for j in range(4):
                    t, c = 2 * i + j // 2, j % 2
                    mm = pe.transpose(bank[4 + i % 4][:, j * P:(j + 1) * P], hn[:, t * D + c * P:t * D + (c + 1) * P], ident[:])
                mm.then_inc(ta2_done, 1)

            def project(b, dst, w, hf, done):
                for kc in range(KD):
                    mm = pe.matmul(bank[dst][:], hnT[b][:, kc, :], w[:, kc, hf * HALF:(hf + 1) * HALF],
                                   start=(kc == 0), stop=(kc == KD - 1))
                mm.then_inc(done, 1)

            pe.wait_ge(wp_ok, 8)
            with pe.Fori(0, NT // 2) as i:
                for b in range(2):
                    pe.wait_ge(hnT_in[b], i * 16 + 16)
                    for hf in range(2):
                        w = i * 4 + (2 * b + hf)
                        pe.wait_ge(sq_ok, w + 1)
                        project(b, 2 * hf, wqkv[:, 1], hf, k_done)
                        pe.wait_ge(ddk_ok, w + 1)
                        project(b, 2 * hf + 1, wp[:, 1], hf, kd_done)

            pe.sem_inc(ctx_done, 2)
            pe.sem_inc(tq_done, 2)
            cbank = [6, 7, 0]
            pe.wait_ge(ta2_ok, 2 * NG)
            pe.wait_ge(kset, 3)
            pe.wait_ge(sq_ok, 2 * NT + 2)
            for c in range(3):
                mm = pe.matmul(bank[cbank[c]][:, 0:3 * PW], zero[:, 0:P], zero[:, 0:3 * PW], start=True, stop=False,
                               skip_group_check=True)
            mm.then_inc(z0_done, 1)
            with pe.Fori(0, NT // 2) as i:
                for b in range(2):
                    pe.wait_ge(hnT_in[b], i * 16 + 16 * (NT // 2 + 1))
                    for hf in range(2):
                        pe.wait_ge(vx_ok, i * 4 + (2 * b + hf + 1))
                        project(b, 4 + hf, wqkv[:, 2], hf, v_done)
                for b in range(2):
                    pe.wait_ge(kp_ok, i * 2 + (b + 1))
                    pe.wait_ge(vx_ok, i * 4 + (2 * b + 4))
                    for p in range(NP):
                        mm = pe.matmul(bank[cbank[p // 3]][:, (p % 3) * PW:(p % 3 + 1) * PW], kp[b][:, p * P:(p + 1) * P],
                                       vx[b][:, p, :], start=False, stop=False, skip_group_check=True)
                    mm.then_inc(ctx_done, 1)
            pe.wait_ge(ctxs_ok, 12)
            for p in range(NP):
                mm = pe.transpose(bank[1 + p // 4][:, (p % 4) * P:(p % 4 + 1) * P], ctxs[:, p, :], ident[:])
            mm.then_inc(ct_done, 1)
            for p in range(NP):
                mm = pe.matmul(bank[3 + p // 4][:, (p % 4) * P:(p % 4 + 1) * P], kcb[:, p, :], ident[:], start=True, stop=True)
            mm.then_inc(kc_done, 1)
            pe.wait_ge(ct_ok, 2)
            for p in range(NP):
                mm = pe.matmul(bank[(5 + p // 2) % 8][:, (p % 2) * D:(p % 2 + 1) * D], ctxT[:, p, :], wo[:, p, :],
                               start=True, stop=True)
            mm.then_inc(c_done, 1)

            pe.wait_ge(c_ok, 4)
            pe.wait_ge(kc_ok, 2)

            def query(i, j):
                b, hf, w = j // 2 % 2, j % 2, i * 4 + j
                if hf == 0:
                    pe.wait_ge(hnT_in[b], i * 16 + 16 * (NT + 1 + j // 4))
                pe.wait_ge(qsq_ok, w + 1)
                project(b, 2 * hf, wqkv[:, 0], hf, q_done)
                pe.wait_ge(qd_ok, w + 1)
                project(b, 2 * hf + 1, wp[:, 0], hf, qdd_done)

            def turn_features(i, j):
                hf = j % 2
                pe.wait_ge(qp_ok, i * 4 + (j + 3))
                for p in range(4):
                    mm = pe.transpose(bank[4 + hf][:, p * P:(p + 1) * P], qp[hf][:, p * P:(p + 1) * P], ident[:])
                mm.then_inc(tq_done, 1)

            def attended(i, j):
                b, hf = j // 2 % 2, j % 2
                pe.wait_ge(qT_ok, i * 4 + (j + 1))
                if hf == 0:
                    pe.wait_ge(h2_ok, i * 2 + (j // 2 + 1))
                for p in range(4):
                    mm = pe.matmul(bank[6 + b][:, 0:D], qT[hf][:, p, :], cmat[:, hf * 4 + p, :],
                                   start=(hf == 0 and p == 0), stop=(hf == 1 and p == 3))
                if hf == 1:
                    mm.then_inc(o_done, 1)

            for j in range(4):
                query(0, j)
                if j == 3:
                    attended(0, 0)
                if j >= 2:
                    turn_features(0, j - 2)
            with pe.Fori(1, NT // 2) as i:
                for j in range(4):
                    query(i, j)
                    attended(i, j - 3)
                    turn_features(i, j - 2)
            def turn_r(p):
                pe.wait_ge(ln2p_ok, p + 2)
                if p >= 2:
                    pe.wait_ge(rT_ok, p - 1)
                for j in range(4):
                    at = (2 * p + j // 2) * D + j % 2 * P
                    mm = pe.transpose(bank[p % 2][:, j * P:(j + 1) * P], hn[:, at:at + P], ident[:])
                mm.then_inc(rt_done, 1)

            last = NT // 2 - 1
            attended(last, 1)
            pe.wait_ge(qd_ok, 2 * NT - 1 + 2)
            for p in (0, 1):
                turn_r(p)
            turn_features(last, 2)
            for p in (2, 3):
                turn_r(p)
            attended(last, 2)
            turn_features(last, 3)
            for p in (4, 5, 6):
                turn_r(p)
            attended(last, 3)
            turn_r(7)

            pe.wait_ge(qsq_ok, 2 * NT + 2)
            pe.wait_ge(qd_ok, 2 * NT + 2)
            pe.wait_ge(rw_in, 32)
            for t in range(NT):
                if t % 2 == 0:
                    pe.wait_ge(rT_ok, t // 2 + 1)
                for kc in range(KD):
                    mm = pe.matmul(bank[2][:, t * 8:(t + 1) * 8], rT[:, t * D + kc * P:t * D + (kc + 1) * P], wrT[:, kc, :],
                                   start=(kc == 0), stop=(kc == KD - 1))
            mm.then_inc(l_done, 1)

            def columns(w, base, at, n):
                return w[:, ds(base + at, n)] if base is not None else w[:, at:at + n]

            def gate_up(i, j, half, w, base):
                if half == 0:
                    pe.wait_ge(xT1_ok, i * 2 + (j + 1))
                pe.wait_ge(h_ok, i * 4 + (2 * j + half + 1))
                for k in range(2):
                    for kc in range(KD):
                        mm = pe.matmul(gub[2 * half + k][:, 0:FH], xT1[j % 2][:, kc, :],
                                       columns(w, base, (k * KD + kc) * FI + half * FH, FH),
                                       start=(kc == 0), stop=(kc == KD - 1))
                mm.then_inc(gu_done, 1)

            def turn_h(i, j):
                pe.wait_ge(h_ok, i * 4 + (2 * j + 4))
                for c in range(FIC):
                    mm = pe.transpose(thb[c // 4][:, (c % 4) * P:(c % 4 + 1) * P], h[:, c * P:(c + 1) * P], ident[:])
                    if c in (3, FIC - 1):
                        mm.then_inc(th_done, 1)

            def down(i, j, w, base):
                pe.wait_ge(hhT_ok, i * 4 + (2 * j + 2))
                pe.wait_ge(y_used, i * 2 + (j + 1))
                for c in range(FIC):
                    mm = pe.matmul(yb[:, 0:D], hhT[:, c, :], columns(w, base, 2 * KD * FI + c * D, D),
                                   start=(c == 0), stop=(c == FIC - 1))
                mm.then_inc(y_done, 1)

            def turn_slots(i, j):
                pe.wait_ge(xs_in[j % 2], i * 16 + 16 * (j // 2 + 1))
                for kc in range(KD):
                    mm = pe.transpose(xb[:, kc * P:(kc + 1) * P], xs[j % 2][:, kc * P:(kc + 1) * P], ident[:])
                mm.then_inc(tu_done, 1)

            def expert(i, j):
                return pe.value_load(uei[0:1, ds(i * 2 + j, 1)], min_val=0, max_val=NE - 1) * EW

            pe.wait_ge(sh_in, 16)
            pe.wait_ge(io_ok, 4)
            pe.wait_ge(pad_ok, 1)

            def shared(i, j, first=False):
                gate_up(i, j, 0, wsh, None)
                gate_up(i, j, 1, wsh, None)
                if not first:
                    down(i, j - 1, wsh, None)
                turn_h(i, j)

            for v in range(3):
                shared(v // 2, v % 2, v == 0)
            pe.wait_ge(hots_ok, 1)
            hv = hots[:].rearrange("p t e -> p (t e)")
            pe.matmul(cb[:, 0:P], tri[:], hv, start=True, stop=True)
            pe.matmul(cb[:, P:2 * P], ones[:], hv, start=True, stop=True).then_inc(cnt_done, 1)
            shared(1, 1)
            with pe.Fori(2, NT // 2 - 1) as i:
                for j in range(2):
                    shared(i, j)
            i = NT // 2 - 1
            shared(i, 0)
            gate_up(i, 1, 0, wsh, None)
            turn_slots(0, 0)
            gate_up(i, 1, 1, wsh, None)
            down(i, 0, wsh, None)
            turn_h(i, 1)

            HT = NT // 2
            pe.wait_ge(wall_in, 16 * NE)
            pe.wait_ge(slots_ok, 1)

            def routed(i, j, more=True):
                e = expert(i, j)
                gate_up(i + HT, j, 0, wall, e)
                if more:
                    turn_slots(i, j + 1)
                gate_up(i + HT, j, 1, wall, e)
                if isinstance(i, int) and 2 * i + j == 0:
                    down(HT, -1, wsh, None)
                else:
                    down(i + HT, j - 1, wall, expert(i, j - 1))
                turn_h(i + HT, j)

            routed(0, 0)
            with pe.Fori(0, NR // 2 - 1) as i:
                for j in (1, 2):
                    routed(i, j)
            i = NR // 2 - 1
            routed(i, 1)
            routed(i, 2, False)
            down(i + HT, 2, wall, expert(i, 2))

        @block.scalar
        def _(act):
            def widened(l, n):
                for c in range(FC):
                    act.wait_ge(h_done, n * FC + (c + 1))
                    alone(act)
                    act.activation(hT[:, c, :], bank[4 + c % 2][:], ACT.Relu, bias=colv[:, ds(l * COLV + c, 1)])\
                        .then_inc(h_evac, 1)

            def turned(done, n, dst, l, at, ok):
                act.wait_ge(done, n + 1)
                alone(act)
                for c in range(KD):
                    ins = act.activation(dst[:, c, :], bank[c][:], ACT.Identity,
                                         scale=colv[:, ds(l * COLV + (at + c), 1)],
                                         bias=colv[:, ds(l * COLV + (at + KD + c), 1)])
                ins.then_inc(ok, 1)

            def root(step, n, i, std):
                act.wait_ge(step, n * 3 + 2)
                act.activation(sd[i][:], mv[i][:, :, 1], ACT.Sqrt, bias=eps_t[:, 0:1]).then_inc(std, 1)

            def group(l, u, last):
                n = l * NG + u
                ahead2 = not last or u + 2 < NG
                ahead1 = not last or u + 1 < NG
                widened(l, n)
                if ahead2:
                    turned(tx_done, n + 2, xT, l if u < 2 else l + 1, FC + 2 * KD, xt_ok)
                if ahead1:
                    turned(ta_done, n + 1, aT, l if u < 3 else l + 1, FC, at_ok)
                root(ln2_step, n, 1, std2)
                if ahead2:
                    root(ln1_step, n + 2, 0, std1)

            act.wait_ge(vec_in, 48)
            act.wait_ge(cst_ok, 3)
            turned(tx_done, 0, xT, 0, FC + 2 * KD, xt_ok)
            root(ln1_step, 0, 0, std1)
            turned(tx_done, 1, xT, 0, FC + 2 * KD, xt_ok)
            root(ln1_step, 1, 0, std1)
            turned(ta_done, 0, aT, 0, FC, at_ok)
            with act.Fori(0, NL - 1) as l:
                for u in range(NG):
                    group(l, u, False)
            for u in range(NG):
                group(NL - 1, u, True)

            def root_all(i):
                act.wait_ge(lnb_step[i], 3 * NG)
                act.activation(lnsd[:], lnmv[:].rearrange("p (t k) -> p t k", k=2)[:, :, 1], ACT.Sqrt,
                               bias=eps_t[:, 0:1]).then_inc(lnb_std[i], 1)

            root_all(0)
            act.wait_ge(hres_ok, NG)
            i = 0
            for w in range(2):
                for ic in range(KD):
                    for hf in range(2):
                        act.wait_ge(wp_done, i + 1)
                        act.activation(wp[:, w, ic, hf * HALF:(hf + 1) * HALF], bank[i % 4][:], ACT.Copy, scale=DN)\
                            .then_inc(wp_ok, 1)
                        i += 1
            for i in range(2 * NG):
                act.wait_ge(ta2_done, i + 1)
                act.activation(hnT_all[:, i * 512:(i + 1) * 512], bank[4 + i % 4][:], ACT.Copy).then_inc(ta2_ok, 1)

            act.sem_inc(sq_ok, 2)
            with act.Fori(0, NT // 2) as i:
                for j in range(4):
                    act.wait_ge(k_done, i * 4 + (j + 1))
                    act.wait_ge(dg_ok, i * 4 + (j + 1))
                    act.activation(sq[j % 2][:], bank[2 * (j % 2)][:], ACT.Square, scale=0.25).then_inc(sq_ok, 1)
            act.sem_inc(vx_ok, 2)
            act.wait_ge(nmx_ok, 1)
            act.wait_ge(kset, 3)
            with act.Fori(0, NT // 2) as i:
                for b in range(2):
                    act.wait_ge(ctx_done, i * 2 + (b + 1))
                    alone(act)
                    act.activation(kp[b][:], ddk[:, ds(i * (2 * HD) + b * HD, HD)], ACT.Exp, bias=nmx[:, 0:1])\
                        .then_inc(ke_ok, 1)
                    for hf in range(2):
                        act.wait_ge(v_done, i * 4 + (2 * b + hf + 1))
                        act.activation(vx[b][:, 4 * hf:4 * hf + 4, 0:P], bank[4 + hf][:].rearrange("p (a n) -> p a n", a=4),
                                       ACT.Copy).then_inc(vx_ok, 1)
            act.wait_ge(ct_done, 1)
            for k in range(2):
                act.activation(ctxT[:, 4 * k:4 * k + 4, :].rearrange("p a n -> p (a n)"), bank[1 + k][:], ACT.Copy)\
                    .then_inc(ct_ok, 1)
            act.wait_ge(c_done, 1)
            for k in range(4):
                act.activation(cmat[:, 2 * k:2 * k + 2, :].rearrange("p a n -> p (a n)"), bank[(5 + k) % 8][:], ACT.Copy)\
                    .then_inc(c_ok, 1)

            def q_turned(i, j):
                act.wait_ge(tq_done, i * 4 + (j + 3))
                act.activation(qT[j % 2][:].rearrange("p a n -> p (a n)"), bank[4 + j % 2][:], ACT.Copy).then_inc(qT_ok, 1)

            def q_square(i, j):
                act.wait_ge(q_done, i * 4 + (j + 1))
                act.activation(qsq[j % 2][:], bank[2 * (j % 2)][:], ACT.Square, scale=0.25).then_inc(qsq_ok, 1)

            def q_exp(i, j):
                act.wait_ge(qd_ok, i * 4 + (j + 3))
                act.wait_ge(qp_ok, i * 4 + (j + 1))
                act.activation(qe[j % 2][:], qd[j % 2][:], ACT.Exp).then_inc(qe_ok, 1)

            def pair_root(i):
                act.wait_ge(ln2p, i * 4 - 1)
                act.activation(lnsd[:, 0:2], lnm4[:, 0:4].rearrange("p (t k) -> p t k", k=2)[:, :, 1], ACT.Sqrt,
                               bias=eps_t[:, 0:1]).then_inc(ln2p_std, 1)

            act.sem_inc(qsq_ok, 2)
            for j in range(4):
                if j == 3:
                    q_turned(0, 0)
                q_square(0, j)
                if j >= 1:
                    q_exp(0, j - 1)
            with act.Fori(1, NT // 2) as i:
                for j in range(4):
                    q_turned(i, j - 3)
                    if j == 3:
                        pair_root(i)
                    q_square(i, j)
                    q_exp(i, j - 1)

            def tokens_turned(p):
                act.wait_ge(rt_done, p + 1)
                act.activation(rT[:, p * 2 * D:(p + 1) * 2 * D], bank[p % 2][:], ACT.Copy).then_inc(rT_ok, 1)

            last = NT // 2 - 1
            q_turned(last, 1)
            q_exp(last, 3)
            tokens_turned(0)
            tokens_turned(1)
            q_turned(last, 2)
            tokens_turned(2)
            tokens_turned(3)
            q_turned(last, 3)
            for p in (4, 5, 6):
                tokens_turned(p)
            pair_root(last + 1)
            tokens_turned(7)

            act.wait_ge(rt_step, 3)
            act.activation(pr[:], pr[:], ACT.Exp).then_inc(pe_exp, 1)

            def gates(i, j, half):
                act.wait_ge(gu_done, i * 4 + (2 * j + half + 1))
                act.activation(sg[half][:], gub[2 * half][:, 0:FH], ACT.Silu).then_inc(sg_ok, 1)

            def h_turned(i, j):
                for k, n in enumerate((4, 2)):
                    act.wait_ge(th_done, i * 4 + (2 * j + k + 1))
                    act.activation(hhT[:, 4 * k:4 * k + n, :].rearrange("p c n -> p (c n)"), thb[k][:, 0:n * P], ACT.Copy)\
                        .then_inc(hhT_ok, 1)

            def tokens(i, j):
                act.wait_ge(gu_done, i * 4 + (2 * j - 2))
                alone(act)
                act.activation(xT1[j % 2][:].rearrange("p a n -> p (a n)"), rT[:, ds(i * (2 * D) + j * D, D)], ACT.Copy)\
                    .then_inc(xT1_ok, 1)

            def slots_turned(i, j):
                act.wait_ge(tu_done, i * 2 + (j + 1))
                act.activation(xT1[j % 2][:].rearrange("p a n -> p (a n)"), xb[:, 0:D], ACT.Copy).then_inc(xT1_ok, 1)

            def outputs(i, j, waits=True):
                act.wait_ge(y_done, i * 2 + (j + 1 + NT))
                if waits:
                    act.wait_ge(y_out[j % 2], i * 16 + 16 * (j // 2))
                act.activation(ys[j % 2][:], yb[:, 0:D], ACT.Copy).then_inc(y_used, 1)

            HT = NT // 2
            for v in range(2):
                act.activation(xT1[v][:].rearrange("p a n -> p (a n)"), rT[:, v * D:(v + 1) * D], ACT.Copy).then_inc(xT1_ok, 1)
            gates(0, 0, 0)
            gates(0, 0, 1)
            h_turned(0, 0)

            def shared(i, j):
                gates(i, j, 0)
                tokens(i, j + 1)
                gates(i, j, 1)
                h_turned(i, j)

            with act.Fori(0, HT - 1) as i:
                for j in (1, 2):
                    shared(i, j)
            gates(HT - 1, 1, 0)
            slots_turned(0, 0)
            gates(HT - 1, 1, 1)
            h_turned(HT - 1, 1)

            def routed(i, j, more=True, y_too=True, y_waits=True):
                gates(i + HT, j, 0)
                if more:
                    slots_turned(i, j + 1)
                gates(i + HT, j, 1)
                if y_too:
                    outputs(i, j - 1, y_waits)
                h_turned(i + HT, j)

            routed(0, 0, y_too=False)
            routed(0, 1, y_waits=False)
            routed(0, 2, y_waits=False)
            with act.Fori(1, NR // 2 - 1) as i:
                for j in (1, 2):
                    routed(i, j)
            i = NR // 2 - 1
            routed(i, 1)
            routed(i, 2, False)
            outputs(i, 2)

        @block.vector
        def _(dve):
            dve.wait_ge(ids_in, 16)
            dve.tensor_copy(idf[:], ids[:]).then_inc(ids_step, 1)
            dve.wait_ge(ids_step, 1)
            dve.tensor_scalar(neg[:], idf[:], 0.0, float(V), ALU.is_lt, ALU.mult).then_inc(ids_step, 1)
            dve.wait_ge(ids_step, 2)
            dve.tensor_tensor(idf[:], idf[:], neg[:], ALU.add).then_inc(ids_step, 1)
            dve.wait_ge(ids_step, 3)
            dve.tensor_scalar(idu[:], idf[:], 0.0, float(V - 1), ALU.max, ALU.min).then_inc(ids_step, 1)

            def embed(g):
                dve.wait_ge(gathered[g], 16 * GT)
                dve.tensor_copy(xn[g][:].rearrange("p a n -> p (a n)"), hn[:, g * GT * D:(g + 1) * GT * D]).then_inc(xn_ok, 1)

            def mixed(l):
                dve.wait_ge(mm_done, l + 1)
                dve.tensor_tensor(mixT[:].rearrange("p a n -> p (a n)"), bank[0][:], eye2[:].rearrange("p a n -> p (a n)"),
                                  ALU.add).then_inc(mix_ok, 1)

            def norm(n, i, src, step, std, dst, ok):
                for t in range(GT):
                    ins = dve.bn_stats(stat[i][:, t, :], src(t))
                ins.then_inc(step, 1)
                dve.wait_ge(step, n * 3 + 1)
                alone(dve)
                for t in range(GT):
                    ins = dve.bn_aggr(mv[i][:, t, :], stat[i][:, t, :])
                ins.then_inc(step, 1)
                dve.wait_ge(std, n + 1)
                dve.reciprocal(rs[i][:], sd[i][:]).then_inc(step, 1)
                dve.wait_ge(step, n * 3 + 3)
                for t in range(GT):
                    ins = dve.tensor_scalar(dst[:, t, :], src(t), mv[i][:, t, 0:1], rs[i][:, t:t + 1], ALU.subtract, ALU.mult)
                ins.then_inc(ok, 1)

            def norm1(n, b):
                dve.wait_ge(s_done, n * 2 + 2)
                norm(n, 0, lambda t: bank[2 + t // 2][:, (t % 2) * D:(t % 2 + 1) * D], ln1_step, std1, an[b], an_ok)

            def norm2(n, u):
                dve.wait_ge(xn_ok, n + NG)
                dve.wait_ge(ares_ok, n + 1)
                for half in range(2):
                    dve.wait_ge(z_done, n * 2 + (half + 1))
                    dve.tensor_tensor(s2[:, 2 * half:2 * half + 2, :].rearrange("p a n -> p (a n)"), bank[6 + half][:],
                                      ares[u % 2][:, 2 * half:2 * half + 2, :].rearrange("p a n -> p (a n)"), ALU.add)\
                        .then_inc(s2_ok, 1)
                dve.wait_ge(s2_ok, n * 2 + 4)
                norm(n, 1, lambda t: s2[:, t, :], ln2_step, std2, xn[u], xn_ok)

            def group(l, u, last):
                n = l * NG + u
                if u == 2 and not last:
                    mixed(l + 1)
                norm2(n, u)
                if not last or u + 2 < NG:
                    norm1(n + 2, u % 2)

            dve.sem_inc(s2_ok, 2)
            dve.wait_ge(cst_ok, 3)
            mixed(0)
            for g in range(NG):
                embed(g)
            norm1(0, 0)
            norm1(1, 1)
            with dve.Fori(0, NL - 1) as l:
                for u in range(NG):
                    group(l, u, False)
            for u in range(NG):
                group(NL - 1, u, True)

            def norm_all(k):
                with dve.Fori(0, NG) as g:
                    if k == 0:
                        dve.wait_ge(hres_ok, g + 1)
                    else:
                        dve.wait_ge(h2_ok, g * GT + (GT + 2))
                    for t in range(GT):
                        ins = dve.bn_stats(lnst[:, t, :], hres[:, ds(g * (GT * D) + t * D, D)])
                    ins.then_inc(lnb_step[k], 1)
                    dve.wait_ge(lnb_step[k], g * 3 + 1)
                    alone(dve)
                    for t in range(GT):
                        ins = dve.bn_aggr(lnm4[:, 2 * t:2 * t + 2], lnst[:, t, :])
                    ins.then_inc(lnb_step[k], 1)
                    dve.wait_ge(lnb_step[k], g * 3 + 2)
                    dve.tensor_copy(lnmv[:, ds(g * (2 * GT), 2 * GT)], lnm4[:]).then_inc(lnb_step[k], 1)
                dve.wait_ge(lnb_std[k], 1)
                dve.reciprocal(lnrs[:], lnsd[:]).then_inc(lnb_step[k], 1)
                dve.wait_ge(lnb_step[k], 3 * NG + 1)
                with dve.Fori(0, NT) as t:
                    dve.tensor_scalar(hn[:, ds(t * D, D)], hres[:, ds(t * D, D)], lnmv[:, ds(t * 2, 1)], lnrs[:, ds(t, 1)],
                                      ALU.subtract, ALU.mult).then_inc(lnb_ok[k], 1)

            norm_all(0)

            def heads(ap):
                return ap.rearrange("p (h n) -> p h n", n=DH)

            def spread(ap):
                return ap.unsqueeze(2).to_broadcast([P, HH, DH])

            dve.sem_inc(dg_ok, 2)
            dve.sem_inc(ddk_ok, 2)
            with dve.Fori(0, NT // 2) as i:
                for j in range(4):
                    hf = j % 2
                    dve.wait_ge(kd_done, i * 4 + (j + 1))
                    dve.tensor_reduce(mxk[:, ds(i * 4 + j, 1)], bank[2 * hf + 1][:], AX.X, ALU.max)
                    dve.wait_ge(sq_ok, i * 4 + (j + 3))
                    dve.tensor_reduce(dg[hf][:], heads(sq[hf][:]), AX.X, ALU.add).then_inc(dg_ok, 1)
                    dve.wait_ge(dg_ok, i * 4 + (j + 3))
                    dve.tensor_tensor(heads(ddk[:, ds(i * (4 * HALF) + j * HALF, HALF)]), heads(bank[2 * hf + 1][:]),
                                      spread(dg[hf][:]), ALU.subtract).then_inc(ddk_ok, 1)
            dve.wait_ge(ddk_ok, 2 * NT + 2)
            dve.tensor_reduce(mx1[:], mxk[:], AX.X, ALU.max).then_inc(mx_step, 1)
            dve.wait_ge(mxa_ok, 1)
            dve.tensor_scalar(nmx[:], mxa[:], -1.0, None, ALU.mult).then_inc(nmx_ok, 1)
            with dve.Fori(0, NT // 2) as i:
                for b in range(2):
                    dve.wait_ge(ke_ok, i * 2 + (b + 1))
                    dve.tensor_scalar(kp[b][:], kp[b][:], EPS, None, ALU.add).then_inc(kp_ok, 1)

            dve.wait_ge(ctx_done, NT + 2)
            dve.memset(ctxs[:], 0.0).then_inc(ctxs_ok, 1)
            dve.wait_ge(ctxs_ok, 1)
            for c, (bk, np_) in enumerate([(6, 3), (7, 3), (0, 2)]):
                src = bank[bk][:, 0:np_ * PW].rearrange("p (a n) -> p a n", n=PW)
                for k in range(2):
                    r = slice(k * DH, (k + 1) * DH)
                    dve.tensor_copy(ctxs[r, 3 * c:3 * c + np_, r], src[r, :, r]).then_inc(ctxs_ok, 1)
                dve.tensor_copy(kcol[:, 3 * c:3 * c + np_], src[:, :, P]).then_inc(ctxs_ok, 1)
            dve.wait_ge(ctxs_ok, 10)
            for k in range(2):
                dve.tensor_copy(kcb[:, 4 * k:4 * k + 4, :], kcol[:, 4 * k:4 * k + 4].unsqueeze(2).to_broadcast([P, 4, P]))\
                    .then_inc(ctxs_ok, 1)
            dve.wait_ge(kc_done, 1)
            for k in range(2):
                dve.tensor_copy(kcum[:, k * HALF:(k + 1) * HALF], bank[3 + k][:]).then_inc(kc_ok, 1)

            def exponents(i, j):
                hf = j % 2
                src = bank[2 * hf + 1]
                dve.wait_ge(qdd_done, i * 4 + (j + 1))
                dve.tensor_reduce(qs[:, 0, :], heads(src[:]), AX.X, ALU.max)
                dve.wait_ge(qsq_ok, i * 4 + (j + 3))
                dve.tensor_reduce(qs[:, 1, :], heads(qsq[hf][:]), AX.X, ALU.add).then_inc(aq_step, 1)
                dve.wait_ge(aq_step, i * 8 + (2 * j + 1))
                dve.tensor_tensor(qs[:, 2, :], qs[:, 0, :], qs[:, 1, :], ALU.add).then_inc(aq_step, 1)
                dve.wait_ge(aq_step, i * 8 + (2 * j + 2))
                dve.tensor_tensor(heads(qd[hf][:]), heads(src[:]), spread(qs[:, 2, :]), ALU.subtract).then_inc(qd_ok, 1)

            def features(i, j):
                hf = j % 2
                dve.wait_ge(qe_ok, i * 4 + (j + 1))
                dve.scalar_tensor_tensor(out=qt[:], in0=qe[hf][:], scalar=EPS, in1=kcum[:, hf * HALF:(hf + 1) * HALF],
                                         op0=ALU.add, op1=ALU.mult).then_inc(bq_step, 1)
                dve.wait_ge(bq_step, i * 12 + (3 * j + 1))
                dve.tensor_reduce(qr[:, 0, :], heads(qt[:]), AX.X, ALU.add).then_inc(bq_step, 1)
                dve.wait_ge(bq_step, i * 12 + (3 * j + 2))
                dve.reciprocal(qr[:, 1, :], qr[:, 0, :]).then_inc(bq_step, 1)
                dve.wait_ge(bq_step, i * 12 + (3 * j + 3))
                dve.wait_ge(tq_done, i * 4 + (j + 1))
                dve.scalar_tensor_tensor(out=heads(qp[hf][:]), in0=heads(qe[hf][:]), scalar=EPS, in1=spread(qr[:, 1, :]),
                                         op0=ALU.add, op1=ALU.mult).then_inc(qp_ok, 1)

            def residual(i, b):
                dve.wait_ge(o_done, i * 2 + (b + 1))
                dve.tensor_tensor(hres[:, ds(i * (2 * D) + b * D, D)], bank[6 + b % 2][:, 0:D],
                                  hres[:, ds(i * (2 * D) + b * D, D)], ALU.add).then_inc(h2_ok, 1)

            def pair_stats(i, b):
                dve.wait_ge(h2_ok, i * 2 + (b + 1))
                alone(dve)
                dve.bn_stats(lnst[:, b, :], hres[:, ds(i * (2 * D) + (b - 2) * D, D)]).then_inc(ln2p, 1)

            def pair_aggr(i):
                dve.wait_ge(ln2p, i * 4 - 2)
                dve.wait_ge(ln2p_ok, i)
                alone(dve)
                for b in range(2):
                    ins = dve.bn_aggr(lnm4[:, 2 * b:2 * b + 2], lnst[:, b, :])
                ins.then_inc(ln2p, 1)

            def pair_apply(i):
                dve.wait_ge(ln2p_std, i)
                dve.reciprocal(lnrs[:, 0:2], lnsd[:, 0:2]).then_inc(ln2p, 1)
                dve.wait_ge(ln2p, i * 4)
                alone(dve)
                for b in range(2):
                    at = ds(i * (2 * D) + (b - 2) * D, D)
                    ins = dve.tensor_scalar(hn[:, at], hres[:, at], lnm4[:, 2 * b:2 * b + 1], lnrs[:, b:b + 1],
                                            ALU.subtract, ALU.mult)
                ins.then_inc(ln2p_ok, 1)

            dve.sem_inc(ln2p_ok, 1)
            dve.sem_inc(qd_ok, 2)
            dve.sem_inc(qp_ok, 2)
            dve.sem_inc(h2_ok, 2)
            dve.wait_ge(bo_ok, 1)
            for j in range(1, 4):
                exponents(0, j - 1)
                if j >= 2:
                    features(0, j - 2)
            with dve.Fori(1, NT // 2) as i:
                for j in range(4):
                    if j % 2 == 1:
                        residual(i, j // 2 - 2)
                        pair_stats(i, j // 2)
                    if j == 3:
                        pair_aggr(i)
                    exponents(i, j - 1)
                    features(i, j - 2)
                    if j == 3:
                        pair_apply(i)
            last = NT // 2 - 1
            exponents(last, 3)
            features(last, 2)
            residual(last, 0)
            pair_stats(last + 1, 0)
            features(last, 3)
            residual(last, 1)
            pair_stats(last + 1, 1)
            pair_aggr(last + 1)
            pair_apply(last + 1)

            def products(i, j):
                for half in range(2):
                    dve.wait_ge(sg_ok, i * 4 + (2 * j + half + 1))
                    dve.tensor_tensor(h[:, half * FH:(half + 1) * FH], gub[2 * half + 1][:, 0:FH], sg[half][:], ALU.mult)\
                        .then_inc(h_ok, 1)

            def shared_output(i, j):
                dve.wait_ge(y_done, i * 2 + (j + 1))
                dve.tensor_tensor(hres[:, ds(i * (2 * D) + j * D, D)], yb[:, 0:D], hres[:, ds(i * (2 * D) + j * D, D)], ALU.add)\
                    .then_inc(y_used, 1)

            count = [0]

            def step(ins):
                count[0] += 1
                ins.then_inc(rt_step, 1)
                dve.wait_ge(rt_step, count[0])

            def over_experts(ap):
                return ap.unsqueeze(2).to_broadcast([P, NT, 8])

            dve.sem_inc(h_ok, 2)
            dve.sem_inc(y_used, 1)
            dve.wait_ge(rw_in, 32)
            dve.wait_ge(l_done, 1)
            step(dve.tensor_tensor(lg[:], bank[2][:, 0:NT * 8].rearrange("p (t e) -> p t e", e=8),
                                   rb[:].unsqueeze(1).to_broadcast([P, NT, 8]), ALU.add))
            step(dve.tensor_reduce(rsm[:, 0, :], lg[:], AX.X, ALU.max))
            step(dve.tensor_tensor(pr[:], lg[:], over_experts(rsm[:, 0, :]), ALU.subtract))
            dve.wait_ge(pe_exp, 1)
            step(dve.tensor_reduce(rsm[:, 1, :], pr[:], AX.X, ALU.add))
            step(dve.reciprocal(rsm[:, 2, :], rsm[:, 1, :]))
            products(0, 0)
            step(dve.tensor_tensor(pr[:], pr[:], over_experts(rsm[:, 2, :]), ALU.mult))
            for t in range(NT):
                ins = dve.max(top[:, t, :], pr[:, t, :])
            step(ins)
            products(0, 1)
            shared_output(0, 0)
            for t in range(NT):
                ins = dve.max_index(idx[:, t, :], top[:, t, :], pr[:, t, :])
            step(ins)
            step(dve.tensor_tensor(rsm[:, 0, :], top[:, :, 0], top[:, :, 1], ALU.add))
            step(dve.reciprocal(rsm[:, 1, :], rsm[:, 0, :]))
            for k in range(2):
                step(dve.tensor_tensor(wsc[:, k, :], top[:, :, k], rsm[:, 1, :], ALU.mult))
                step(dve.tensor_copy(idxf[:, k, :], idx[:, :, k]))
            products(1, 0)
            shared_output(0, 1)
            dve.wait_ge(io_ok, 6)
            step(dve.tensor_copy(io8[:], io8i[:]))
            step(dve.tensor_copy(iou[:], ioui[:]))
            step(dve.tensor_scalar(iou8[:], io8[:], float(P), None, ALU.mult))
            for k in range(2):
                step(dve.tensor_tensor(hot[k][:], io8[:, 0:8].unsqueeze(1).to_broadcast([P, NT, 8]),
                                       over_experts(idxf[:, k, :]), ALU.is_equal))
            dve.tensor_tensor(hots[:], hot[0][:], hot[1][:], ALU.add).then_inc(hots_ok, 1)
            products(1, 1)
            shared_output(1, 0)
            step(dve.memset(tot[:, 0, :], 0.0))
            step(dve.memset(off[:], 0.0))
            dve.wait_ge(cnt_done, 1)
            counts = cb[:, P:2 * P].rearrange("p (t e) -> p t e", e=8)
            for t in range(NT):
                step(dve.tensor_tensor(tot[:, t + 1, :], counts[:, t, :], tot[:, t, :], ALU.add))
            products(2, 0)
            shared_output(1, 1)
            step(dve.tensor_tensor(over[:], tot[:, NT, :].unsqueeze(2).to_broadcast([P, 8, MU]),
                                   iou8[:].unsqueeze(1).to_broadcast([P, 8, MU]), ALU.is_gt))
            step(dve.tensor_reduce(nun[:], over[:], AX.X, ALU.add))
            for e in range(8):
                step(dve.tensor_tensor(off[:, e + 1:e + 2], off[:, e:e + 1], nun[:, e:e + 1], ALU.add))
            step(dve.tensor_scalar(offs[:], off[:], float(P), None, ALU.mult))
            step(dve.tensor_tensor(pos[:], cb[:, 0:P].rearrange("p (t e) -> p t e", e=8), tot[:, 0:NT, :], ALU.add))
            step(dve.tensor_tensor(pos[:], pos[:], offs[:, 0:8].unsqueeze(1).to_broadcast([P, NT, 8]), ALU.add))
            products(2, 1)
            shared_output(2, 0)
            for k in range(2):
                step(dve.tensor_tensor(pick[:], hot[k][:], pos[:], ALU.mult))
                step(dve.tensor_reduce(slotf[:, k, :], pick[:], AX.X, ALU.add))
            step(dve.tensor_copy(sloti[:], slotf[:].rearrange("p k t -> p (k t)")))
            ne1 = NE - 1
            step(dve.tensor_tensor(ended[:], iou[:].unsqueeze(2).to_broadcast([P, NR, ne1]),
                                   off[:, 1:NE].unsqueeze(1).to_broadcast([P, NR, ne1]), ALU.is_ge))
            step(dve.tensor_reduce(uef[:], ended[:], AX.X, ALU.add))
            dve.tensor_copy(uei[:], uef[:]).then_inc(slots_ok, 1)
            with dve.Fori(3, NT // 2) as i:
                for j in range(2):
                    products(i, j)
                    shared_output(i, j - 1)
            products(NT // 2, 0)
            shared_output(NT // 2, -1)
            with dve.Fori(NT // 2, NT // 2 + NR // 2) as i:
                for j in (1, 2):
                    products(i, j)

            for t in range(NT):
                at = slice(t * D, (t + 1) * D)
                for k in range(2):
                    if t % LG == 0:
                        dve.wait_ge(y_in[t // LG], 32)
                    if k == 1:
                        dve.wait_ge(f_step, t + 1)
                    dve.scalar_tensor_tensor(out=hres[:, at], in0=yl[k][:, at], scalar=wsc[:, k, t:t + 1],
                                             in1=hres[:, at], op0=ALU.mult, op1=ALU.add).then_inc([f_step, yo_ok][k], 1)


def kernel(**inputs):
    import concourse.bacc as bacc
    from concourse.bass_utils import run_bass_kernel_spmd

    a = {k: np.asarray(v) for k, v in inputs.items()}

    def chunks(w, n):
        lead = w.shape[:-2]
        return np.moveaxis(w.reshape(*lead, n, P, w.shape[-1]), -3, -2)

    wq = a["L0_tok_Wq"].reshape(NL, D, D)
    woT = a["L0_tok_Wo"].transpose(0, 2, 1)
    one, nil = np.ones((1, D), np.float32), np.zeros((1, D), np.float32)
    cols = [a["L0_tok_ff_b1"], a["L0_tok_ln1_w"], a["L0_tok_ln1_b"],
            np.concatenate([one, a["L0_tok_ln2_w"][:-1]]), np.concatenate([nil, a["L0_tok_ln2_b"][:-1]])]
    colv = np.concatenate([c.reshape(NL, -1, P) for c in cols], 1)
    pt = a["L0_attn_P"].T
    bp = np.zeros((P, P), np.float32)
    bp[:DH, :DH] = pt
    bp[DH:, DH:] = pt
    gate = np.concatenate([a["L0_ffn_rg"], a["L0_ffn_sg"][None]]).transpose(0, 2, 1)
    up = np.concatenate([a["L0_ffn_ru"], a["L0_ffn_su"][None]]).transpose(0, 2, 1)
    dn = np.concatenate([a["L0_ffn_rd"], a["L0_ffn_sd"][None]]).transpose(0, 2, 1)
    dn = np.concatenate([dn, np.zeros((NE + 1, FIC * P - FI, D), np.float32)], 1)
    flat = [w.reshape(NE + 1, P, -1) for w in (chunks(gate, KD), chunks(up, KD), chunks(dn, FIC))]
    arrays = {
        "ids": a["x"].reshape(NT, P).T,
        "emb": a["L0_tok_emb_table"],
        "mixw": np.concatenate([chunks(wq, KD), chunks(woT, KD)], 2),
        "w1T": chunks(a["L0_tok_ff_w1"].transpose(0, 2, 1), KD),
        "w2T": chunks(a["L0_tok_ff_w2"].transpose(0, 2, 1), FC),
        "colv": colv.transpose(2, 0, 1).reshape(P, -1),
        "ln1row": np.stack([a["L0_tok_ln1_w"].ravel(), a["L0_tok_ln1_b"].ravel(), a["L0_tok_ff_b2"].ravel()]),
        "rowv": np.stack([a["L0_tok_ln2_w"][-1], a["L0_tok_ln2_b"][-1], a["L0_attn_bo"]]),
        "wqkv": np.stack([chunks(a[f"L0_attn_W{k}"], KD) for k in "qkv"], 1),
        "wqkT": np.stack([chunks(a[f"L0_attn_W{k}"].T, NP) for k in "qk"], 1),
        "wo": chunks(a["L0_attn_Wo"], NP),
        "bp": bp,
        "wrT": chunks(np.concatenate([a["L0_ffn_wr"].T, np.zeros((D, 1), np.float32)], 1), KD),
        "rb": np.concatenate([a["L0_ffn_rb"], np.full((1,), -1e30, np.float32)]),
        "we": np.concatenate(flat, 2),
    }
    arrays = {k: np.ascontiguousarray(v) for k, v in arrays.items()}
    nc = bacc.Bacc("TRN2", target_bir_lowering=False, num_devices=1)
    d = {k: nc.dram_tensor(f"in_{k}", v.shape, mybir.dt.from_np(v.dtype), kind="ExternalInput").ap()
         for k, v in arrays.items()}
    out = nc.dram_tensor("out", (T, D), F32, kind="ExternalOutput").ap()
    build(nc, d, out)
    r = run_bass_kernel_spmd(nc, [{f"in_{k}": v for k, v in arrays.items()}], core_ids=[0])
    return r.results[0]["out"].reshape(1, T, D)
```

```python
from contextlib import ExitStack

import numpy as np
import concourse.bass as bass
from concourse import mybir

F32 = mybir.dt.float32
F32R = mybir.dt.float32r
I32 = mybir.dt.int32
U32 = mybir.dt.uint32
ALU = mybir.AluOpType
ACT = mybir.ActivationFunctionType
AX = mybir.AxisListType
RMAX = bass.bass_isa.ReduceOp.max
ds = bass.ds

P = 128
T = 2048
NT = T // P
D = 256
KD = D // P
NL = 6
F = 1024
FC = F // P
GT = 4
NG = NT // GT
GN = GT * P
V = 8000
H = 16
DH = 64
HD = H * DH
NP = H // 2
HALF = HD // 2
HH = H // 2
PW = P + 2
NE = 7
FI = 704
FIC = 6
FH = FI // 2
NR = 2 * T // P + NE
NU = NT + NR
ND = P
MU = T // P
EW = KD * FI * 2 + FIC * D
COLV = FC + 4 * KD
LN_EPS = 1e-5
EPS = 1e-4
DN = DH ** -0.25
LG = 4


def build(nc, d, out):
    ctx = ExitStack()
    with ctx:
        def sem(name):
            return ctx.enter_context(nc.semaphore(name))

        def allocator(stack):
            return lambda name, shape, dt=F32: stack.enter_context(nc.sbuf_tensor(name, shape, dt))

        def beneath(*specs):
            stack = ExitStack()
            made = [allocator(stack)(name, shape, F32R) for name, shape in specs]
            stack.close()
            return made if len(made) > 1 else made[0]

        bank = [ctx.enter_context(nc.psum_tensor(f"bank{i}", [P, 512], F32)) for i in range(8)]
        slots_x = nc.dram_tensor("slots_x", (NR * P, D), F32, kind="Internal").ap()
        slots_a = nc.dram_tensor("slots_a", (NR * P, 1), I32, kind="Internal").ap()
        y_tok = nc.dram_tensor("y_tok", (2 * T + ND, D), F32, kind="Internal").ap()

        sb = allocator(ctx)
        ident = sb("ident", [P, P])
        eps_t = sb("eps_t", [P, 1])
        hres = sb("hres", [P, NT * D])
        hnh = beneath(("hnh", [P, NT * D]))
        hn = sb("hn", [P, NT * D])
        lnst = sb("lnst", [P, GT, 6])
        lnm4 = sb("lnm4", [P, GT * 2])
        lnsd = sb("lnsd", [P, GT])
        lnrs = sb("lnrs", [P, GT])
        wrT = sb("wrT", [P, KD, 8])
        rb = sb("rb", [P, 8])

        both = ExitStack()
        sb = allocator(both)
        wkl = beneath(("wkl", [P, KD, HD]))
        wqh = beneath(("wqh", [P, KD, HD]))
        wk = sb("wk", [P, KD, HD])
        wvh, wpqh = beneath(("wvh", [P, KD, HD]), ("wpqh", [P, KD, HD]))
        wqkT = sb("wqkT", [P, 2, NP, D])
        bp = sb("bp", [P, P])
        rowv = sb("rowv", [P, 3, D])
        late = ExitStack()
        lb = allocator(late)
        w1h = lb("w1h", [P, KD, F], F32R)
        xT = lb("xT", [P, KD, GN])
        zT = lb("zT", [P, KD, GN])
        low = ExitStack()
        w1r = allocator(low)("w1r", [P, KD, F])
        low.close()
        w1l = lb("w1l", [P, KD, F], F32R)
        late.close()
        wkh = beneath(("wkh", [P, KD, HD]))
        wql = beneath(("wql", [P, KD, HD]))
        wq = sb("wq", [P, KD, HD])
        wo = sb("wo", [P, NP, D])
        wvl = beneath(("wvl", [P, KD, HD]))
        wv = sb("wv", [P, KD, HD])
        wpkl = beneath(("wpkl", [P, KD, HD]))
        early = sb("early", [P, 4 * KD * D])
        eye2 = early[:, 0:KD * D].rearrange("p (k n) -> p k n", k=KD)
        mixT = early[:, KD * D:2 * KD * D].rearrange("p (k n) -> p k n", k=KD)
        mixw = early[:, 2 * KD * D:4 * KD * D].rearrange("p (k n) -> p k n", k=4)
        wpk = early[:, 0:KD * HD].rearrange("p (k n) -> p k n", k=KD)
        hnl = beneath(("hnl", [P, NT * D]))
        tokens_mem = sb("tokens_mem", [P, NT * D])
        xn = [tokens_mem[:, g * GT * D:(g + 1) * GT * D].rearrange("p (t n) -> p t n", t=GT) for g in range(NG)]
        hnT_all = tokens_mem
        wpql, hth0, hth1, htl0, htl1 = beneath(("wpql", [P, KD, HD]), *((f"hnT{k}{i}", [P, KD, P]) for k in "hl" for i in range(2)))
        rows_mem = sb("rows_mem", [P, 3 * NL * D])
        ln1row = rows_mem[:].rearrange("p (a n) -> p a n", a=3)
        at = [0]

        def rows(n):
            at[0] += n
            return rows_mem[:, at[0] - n:at[0]]

        wpq = rows(KD * HD).rearrange("p (k n) -> p k n", k=KD)
        hnTh, hnTl = [hth0, hth1], [htl0, htl1]
        rows(4 * KD * P)
        zero = rows(3 * PW)
        sq = [rows(HALF) for i in range(2)]
        qt = sq
        dg = [rows(HH) for i in range(2)]
        mxk = rows(2 * NT)
        mx1, mxa, nmx = rows(1), rows(1), rows(1)

        phase = ExitStack()
        sb = allocator(phase)
        colv = sb("colv", [P, NL * COLV])
        s2 = sb("s2", [P, GT, D])
        ares = [sb(f"ares{i}", [P, GT, D]) for i in range(2)]
        stat = [sb(f"stat{i}", [P, GT, 6]) for i in range(2)]
        mv = [sb(f"mv{i}", [P, GT, 2]) for i in range(2)]
        sd = [sb(f"sd{i}", [P, GT]) for i in range(2)]
        rs = [sb(f"rs{i}", [P, GT]) for i in range(2)]
        an = [sb(f"an{i}", [P, GT, D]) for i in range(2)]

        def low_part(name, shape):
            low = ExitStack()
            whole = allocator(low)(name + "r", shape)
            low.close()
            return whole, sb(name + "l", shape, F32R)

        aTr, aTl = low_part("aT", [P, KD, GN])
        aTh = sb("aTh", [P, KD, GN], F32R)
        hTr, hTl = low_part("hT", [P, FC, GN])
        hTh = sb("hTh", [P, FC, GN], F32R)
        w2r, w2l = low_part("w2", [P, FC, D])
        w2h = sb("w2h", [P, FC, D], F32R)
        ids = sb("ids", [P, NT], I32)
        idf = sb("idf", [P, NT])
        neg = sb("neg", [P, NT])
        idu = sb("idu", [P, NT], I32)
        phase.close()

        phase = ExitStack()
        sb = allocator(phase)
        wpkh = beneath(("wpkh", [P, KD, HD]))
        kp = [sb(f"kp{i}", [P, HD]) for i in range(2)]
        vx = [sb("vx0", [P, NP, PW])]
        sb("gap", [P, 288])
        ddk = sb("ddk", [P, NT * HD])
        vx.append(sb("vx1", [P, NP, PW]))
        phase.close()
        phase = ExitStack()
        sb = allocator(phase)
        ctxs = sb("ctxs", [P, NP, P])
        kcol = sb("kcol", [P, NP])
        kcb = sb("kcb", [P, NP, P])
        ctxT = sb("ctxT", [P, NP, P])
        kcum = sb("kcum", [P, HD])
        cmat = sb("cmat", [P, NP, D])
        qsq = [sb(f"qsq{i}", [P, HALF]) for i in range(2)]
        qe = [sb(f"qe{i}", [P, HALF]) for i in range(2)]
        ekc = sb("ekc", [P, 2 * HH])
        qp = [sb(f"qp{i}", [P, HALF]) for i in range(2)]
        qT = [sb(f"qT{i}", [P, 4, P]) for i in range(2)]
        qs = [sb(f"qs{i}", [P, 2, HH]) for i in range(2)]
        qm = [sb(f"qm{i}", [P, HH]) for i in range(2)]
        qr = sb("qr", [P, 2, HH])
        phase.close()
        both.close()

        sb = allocator(ctx)
        wall = sb("wall", [P, NE * EW])
        lg = sb("lg", [P, NT, 8])
        pr = sb("pr", [P, NT, 8])
        rsm = sb("rsm", [P, 3, NT])
        top = sb("top", [P, NT, 8])
        idx = sb("idx", [P, NT, 8], U32)
        idxf = sb("idxf", [P, 2, NT])
        io8 = sb("io8", [P, MU])
        io8i = sb("io8i", [P, MU], I32)
        iou8 = sb("iou8", [P, MU])
        ioui = sb("ioui", [P, NR], I32)
        iou = sb("iou", [P, NR])
        hot = [sb(f"hot{i}", [P, NT, 8]) for i in range(2)]
        hots = sb("hots", [P, NT, 8])
        tri = sb("tri", [P, P])
        ones = sb("ones", [P, P])
        tot = sb("tot", [P, NT + 1, 8])
        pos = sb("pos", [P, NT, 8])
        over = sb("over", [P, 8, MU])
        ended = sb("ended", [P, NR, NE - 1])
        nun = sb("nun", [P, 8])
        off = sb("off", [P, 9])
        offs = sb("offs", [P, 9])
        pick = sb("pick", [P, NT, 8])
        slotf = sb("slotf", [P, 2, NT])
        sloti = sb("sloti", [P, 2 * NT], I32)
        wsc = sb("wsc", [P, 2, NT])
        uef = sb("uef", [P, NR])
        uei = sb("uei", [P, NR], I32)
        asg = sb("asg", [P, 2 * NT], I32)
        dump = sb("dump", [P, P], I32)
        sa = sb("sa", [P, NR], I32)
        xT1 = [sb(f"xT1_{i}", [P, KD, P]) for i in range(2)]
        sg = [sb(f"sg{i}", [P, FH]) for i in range(2)]
        h = sb("h", [P, FIC * P])
        hhT = sb("hhT", [P, FIC, P])
        ys = [sb(f"ys{i}", [P, D]) for i in range(2)]
        rT = sb("rT", [P, NT * D])
        wsh = sb("wsh", [P, EW])
        xs = [rT[:, i * D:(i + 1) * D] for i in range(2)]
        yl = [hn, rT]

        cst, cst_ok, waited = sem("cst"), sem("cst_ok"), sem("waited")
        ids_in, ids_step, gathered = sem("ids_in"), sem("ids_step"), [sem(f"gathered{g}") for g in range(NG)]
        vec_in, rows_in, rows_ok, aw_in = sem("vec_in"), sem("rows_in"), sem("rows_ok"), sem("aw_in")
        mix_in, w1_in, w2_in = sem("mix_in"), sem("w1_in"), sem("w2_in")
        mm_done, mix_ok = sem("mm_done"), sem("mix_ok")
        xn_ok, tx_done, xt_ok = sem("xn_ok"), sem("tx_done"), sem("xt_ok")
        s_done, ln1_step, std1, an_ok = sem("s_done"), sem("ln1_step"), sem("std1"), sem("an_ok")
        ares_half, ares_ok = sem("ares_half"), sem("ares_ok")
        w1h_ok, w1_ok, w2h_ok, w2_ok = sem("w1h_ok"), sem("w1_ok"), sem("w2h_ok"), sem("w2_ok")
        ta_done, at_evac, at_ok = sem("ta_done"), sem("at_evac"), sem("at_ok")
        h_done, h_evac, hh_ok, h_split = sem("h_done"), sem("h_evac"), sem("hh_ok"), sem("h_split")
        zt_ok, tz_done = sem("zt_ok"), sem("tz_done")
        z_done, s2_ok, ln2_step, std2 = sem("z_done"), sem("s2_ok"), sem("ln2_step"), sem("std2")
        hres_half, hres_ok = sem("hres_half"), sem("hres_ok")
        lnb_step, lnb_std, lnb_ok = sem("lnb_step"), sem("lnb_std"), sem("lnb_ok")
        wv_in, wo_in, wq_in, kc2_ok = sem("wv_in"), sem("wo_in"), sem("wq_in"), sem("kc2_ok")
        wkh_ok, wkl_ok, wvh_ok, wvl_ok = sem("wkh_ok"), sem("wkl_ok"), sem("wvh_ok"), sem("wvl_ok")
        wqh_ok, wql_ok, wpql_ok, qt_ok = sem("wqh_ok"), sem("wql_ok"), sem("wpql_ok"), sem("qt_ok")
        wp_done, wp_evac, wpkl_ok = sem("wp_done"), sem("wp_evac"), sem("wpkl_ok")
        ta2_done, ta2_evac, ta2_ok = sem("ta2_done"), sem("ta2_evac"), sem("ta2_ok")
        hnT_in = [sem(f"hnT_in{i}") for i in range(2)]
        k_done, kd_done, sq_ok, dg_ok, ddk_ok = sem("k_done"), sem("kd_done"), sem("sq_ok"), sem("dg_ok"), sem("ddk_ok")
        mx_step, mxa_ok, nmx_ok = sem("mx_step"), sem("mxa_ok"), sem("nmx_ok")
        z0_done, kset = sem("z0_done"), sem("kset")
        v_done, vx_ok, ke_ok, kp_ok, ctx_done = sem("v_done"), sem("vx_ok"), sem("ke_ok"), sem("kp_ok"), sem("ctx_done")
        ctxs_ok, ct_done, ct_ok, kc_done, kc_ok = sem("ctxs_ok"), sem("ct_done"), sem("ct_ok"), sem("kc_done"), sem("kc_ok")
        c_done, c_ok = sem("c_done"), sem("c_ok")
        q_done, qdd_done, qsq_ok, aq_step, qm_ok = sem("q_done"), sem("qdd_done"), sem("qsq_ok"), sem("aq_step"), sem("qm_ok")
        qe_ok, bq_step, qp_ok, tq_done, qT_ok = sem("qe_ok"), sem("bq_step"), sem("qp_ok"), sem("tq_done"), sem("qT_ok")
        o_done, h2_ok, bo_ok = sem("o_done"), sem("h2_ok"), sem("bo_ok")
        ln2p, ln2p_std, ln2p_ok = sem("ln2p"), sem("ln2p_std"), sem("ln2p_ok")
        rw_in, io_ok, rt_done, rT_ok, l_done = sem("rw_in"), sem("io_ok"), sem("rt_done"), sem("rT_ok"), sem("l_done")
        rt_step, pe_exp, hots_ok, cnt_done, slots_ok = sem("rt_step"), sem("pe_exp"), sem("hots_ok"), sem("cnt_done"), sem("slots_ok")
        zero_in, dump_in, scattered, ids_scattered = sem("zero_in"), sem("dump_in"), sem("scattered"), sem("ids_scattered")
        sa_in, sh_in, wall_in, pad_ok = sem("sa_in"), sem("sh_in"), sem("wall_in"), sem("pad_ok")
        xs_in = [sem(f"xs_in{i}") for i in range(2)]
        tu_done, xT1_ok, gu_done, sg_ok = sem("tu_done"), sem("xT1_ok"), sem("gu_done"), sem("sg_ok")
        h_ok, th_done, hhT_ok = sem("h_ok"), sem("th_done"), sem("hhT_ok")
        y_done, y_used = sem("y_done"), sem("y_used")
        y_out = [sem(f"y_out{i}") for i in range(2)]
        y_in = [sem(f"y_in{g}") for g in range(NT // LG)]
        f_step, yo_ok, f2_step, yo2_ok, o_out = sem("f_step"), sem("yo_ok"), sem("f2_step"), sem("yo2_ok"), sem("o_out")

        cbank = [6, 7, 3]
        cmat_bank = [6, 7, 4, 5]
        gub, thb, yb, xb, cb = [bank[0], bank[1], bank[4], bank[5]], [bank[2], bank[3]], bank[6], bank[7], bank[7]

        def token_bank(p):
            return bank[7 if p == 7 else p % 2]

        def normed_bank(i):
            return bank[(2 if i < 2 * (NG - 1) else 6) + i % 2]

        block = ctx.enter_context(nc.Block())

        def alone(eng):
            eng.sem_inc(waited, 1)

        @block.sync
        def _(sp):
            sp.dma_start(ids[:], d["ids"]).then_inc(ids_in, 16)
            sp.dma_start(mixw[:], d["mixw"][0]).then_inc(mix_in, 16)
            sp.dma_start(colv[:], d["colv"]).then_inc(vec_in, 16)
            sp.wait_ge(gathered[0], 16 * GT)
            sp.dma_start(w1r[:], d["w1T"][0]).then_inc(w1_in, 16)
            sp.wait_ge(gathered[1], 16 * GT)
            sp.dma_start(ln1row.rearrange("p a n -> p (a n)"),
                         d["ln1row"].rearrange("a n -> (a n)").partition_broadcast(P)).then_inc(rows_in, 16)
            sp.dma_start(w2r[:], d["w2T"][0]).then_inc(w2_in, 16)
            sp.wait_ge(gathered[NG - 1], 16 * GT)
            sp.dma_start(rowv[:].rearrange("p a n -> p (a n)"),
                         d["rowv"].rearrange("a n -> (a n)").partition_broadcast(P)).then_inc(rows_in, 16)
            sp.dma_start(wk[:], d["wqkv"][:, 1]).then_inc(aw_in, 16)
            sp.dma_start(wqkT[:], d["wqkT"]).then_inc(aw_in, 16)
            sp.dma_start(bp[:], d["bp"]).then_inc(aw_in, 16)
            sp.dma_start(wrT[:], d["wrT"]).then_inc(rw_in, 16)
            sp.dma_start(rb[:], d["rb"].partition_broadcast(P)).then_inc(rw_in, 16)
            with sp.Fori(0, NL - 1) as l:
                sp.wait_ge(mm_done, l + 1)
                sp.dma_start(mixw[:], d["mixw"][ds(l + 1, 1)].rearrange("o p a n -> (o p) a n")).then_inc(mix_in, 16)
                sp.wait_ge(h_done, l * (NG * FC) + NG * FC)
                sp.dma_start(w1r[:], d["w1T"][ds(l + 1, 1)].rearrange("o p a n -> (o p) a n")).then_inc(w1_in, 16)
                sp.wait_ge(z_done, l * (2 * NG) + 2 * NG)
                sp.dma_start(w2r[:], d["w2T"][ds(l + 1, 1)].rearrange("o p a n -> (o p) a n")).then_inc(w2_in, 16)

            sp.wait_ge(tz_done, NL * NG * 2)
            sp.dma_start(wv[:], d["wqkv"][:, 2]).then_inc(wv_in, 16)
            sp.dma_start(wo[:], d["wo"]).then_inc(wo_in, 16)

            def hnT_load(b, t):
                for part, whole in ((hnTh, hnh), (hnTl, hnl)):
                    sp.dma_start(part[b][:].rearrange("p a n -> p (a n)").bitcast(F32), whole[:, ds(t * D, D)].bitcast(F32))\
                        .then_inc(hnT_in[b], 16)

            for step, (used, per) in enumerate([(None, 0), (kd_done, 2), (v_done, 2)]):
                for b in range(2):
                    if step == 0:
                        sp.wait_ge(ares_ok, NL * NG)
                        sp.wait_ge(ta2_ok, 1)
                    else:
                        sp.wait_ge(used, per * (NT - 1 + b))
                    hnT_load(b, b)
                if step == 1:
                    sp.dma_start(wq[:], d["wqkv"][:, 0]).then_inc(wq_in, 16)
                if step == 2:
                    sp.wait_ge(ctx_done, NT + 2)
                    sp.dma_start(wsh[:], d["we"][NE]).then_inc(sh_in, 16)
                now = [kd_done, v_done, qdd_done][step]
                if step == 0:
                    sp.wait_ge(ta2_ok, 2)
                    for b in range(2):
                        sp.wait_ge(now, 2 * b + 2)
                        hnT_load(b, 2 + b)
                    sp.wait_ge(ta2_ok, 2 * NG)
                with sp.Fori(2 if step == 0 else 1, NT // 2) as i:
                    for b in range(2):
                        sp.wait_ge(now, i * 4 + (2 * b - 2))
                        hnT_load(b, i * 2 + b)

            sp.wait_ge(h2_ok, NT + 2)
            sp.wait_ge(zero_in, 16 * NR)
            for e in range(NE):
                sp.dma_start(wall[:, e * EW:(e + 1) * EW], d["we"][e]).then_inc(wall_in, 16)
            sp.wait_ge(ids_scattered, 16 * 2 * NT)
            sp.dma_start(sa[:], slots_a.rearrange("(u p) o -> p (u o)", p=P), allow_slow_non_contiguous=True).then_inc(sa_in, 16)

            def xs_load(b, r):
                sp.dma_start(xs[b], slots_x[ds(r * P, P), :]).then_inc(xs_in[b], 16)

            sp.wait_ge(scattered, 16 * 2 * NT)
            sp.wait_ge(xT1_ok, NT)
            for b in range(2):
                xs_load(b, b)
            with sp.Fori(0, NR // 2 - 1) as i:
                for b in range(2):
                    sp.wait_ge(tu_done, i * 2 + (b + 1))
                    xs_load(b, i * 2 + (b + 2))
            sp.wait_ge(tu_done, NR - 2)
            xs_load(0, NR - 1)
            sp.wait_ge(y_out[0], 16 * ((NR + 1) // 2))
            sp.wait_ge(y_out[1], 16 * (NR // 2))
            for g in range(NT // LG):
                for k in range(2):
                    r = k * T + g * LG * P
                    sp.dma_start(yl[k][:, g * LG * D:(g + 1) * LG * D].rearrange("p (t n) -> p t n", t=LG),
                                 y_tok[r:r + LG * P, :].rearrange("(t p) n -> p t n", p=P)).then_inc(y_in[g], 16)
            for g in range(NT // 2):
                sp.wait_ge(yo_ok, 2 * g + 2 - (g + 1) // 2 + (g == NT // 2 - 1))
                if g % 2 and g < NT // 2 - 1:
                    sp.wait_ge(yo2_ok, g // 2 + 1)
                sp.dma_start(out[g * 2 * P:(g + 1) * 2 * P, :].rearrange("(t p) n -> p t n", p=P),
                             hres[:, g * 2 * D:(g + 1) * 2 * D].rearrange("p (t n) -> p t n", t=2)).then_inc(o_out, 16)
            sp.wait_ge(o_out, 16 * (NT // 2))

        @block.gpsimd
        def _(pool):
            pool.memset(ident[:], 0.0).then_inc(cst, 1)
            pool.memset(eye2[:], 0.0).then_inc(cst, 1)
            pool.memset(eps_t[:], LN_EPS).then_inc(cst_ok, 1)
            pool.wait_ge(cst, 2)
            pool.affine_select(out=ident[:], in_=ident[:], compare_op=ALU.not_equal, fill=1.0, base=0,
                               pattern=[[-1, P]], channel_multiplier=1).then_inc(cst_ok, 1)
            pool.affine_select(out=eye2[:], in_=eye2[:], compare_op=ALU.not_equal, fill=1.0, base=0,
                               pattern=[[P, KD], [-1, D]], channel_multiplier=1).then_inc(cst_ok, 1)
            pool.wait_ge(ids_step, 4)
            for t in range(NT):
                pool.indirect_dma_start(out=xn[t // GT][:, t % GT, :], out_offset=None, in_=d["emb"],
                                        in_offset=bass.IndirectOffsetOnAxis(ap=idu[:, t:t + 1], axis=0))\
                    .then_inc(gathered[t // GT], 16)
            pool.wait_ge(rows_in, 32)
            pool.tensor_tensor(ln1row[:, 1, :], ln1row[:, 1, :], ln1row[:, 2, :], ALU.add).then_inc(rows_ok, 1)
            pool.wait_ge(rows_ok, 1)

            def residual(l, n, b):
                pool.wait_ge(an_ok, n + 1)
                alone(pool)
                pool.tensor_tensor(ares[b][:], an[b][:],
                                   ln1row[:, 0, ds(l * D, D)].unsqueeze(1).to_broadcast([P, GT, D]), ALU.mult)\
                    .then_inc(ares_half, 1)
                pool.wait_ge(ares_half, n + 1)
                alone(pool)
                pool.tensor_tensor(ares[b][:], ares[b][:],
                                   ln1row[:, 1, ds(l * D, D)].unsqueeze(1).to_broadcast([P, GT, D]), ALU.add)\
                    .then_inc(ares_ok, 1)

            with pool.Fori(0, NL - 1) as l:
                for u in range(NG):
                    residual(l, l * NG + u, u % 2)

            def tower_output(g):
                hg = hres[:, g * GT * D:(g + 1) * GT * D].rearrange("p (t n) -> p t n", t=GT)
                pool.wait_ge(xn_ok, NL * NG + g + 1)
                pool.tensor_tensor(hg, xn[g][:], rowv[:, 0:1, :].to_broadcast([P, GT, D]), ALU.mult).then_inc(hres_half, 1)
                pool.wait_ge(hres_half, g + 1)
                pool.tensor_tensor(hg, hg, rowv[:, 1:2, :].to_broadcast([P, GT, D]), ALU.add).then_inc(hres_ok, 1)

            for u in range(NG):
                residual(NL - 1, (NL - 1) * NG + u, u % 2)
                if u > 1:
                    tower_output(u - 2)
            tower_output(NG - 2)
            tower_output(NG - 1)
            pool.wait_ge(ares_ok, NL * NG)
            pool.memset(zero[:], 0.0).then_inc(kset, 1)
            pool.wait_ge(xn_ok, (NL + 1) * NG)
            for b in range(2):
                pool.memset(vx[b][:, :, P:PW], 1.0).then_inc(kset, 1)
            pool.wait_ge(kset, 1)
            for i in range(NR):
                pool.dma_start(slots_x[i * P:(i + 1) * P, :], zero[:, 0:D]).then_inc(zero_in, 16)
            pool.wait_ge(lnb_ok, NG)
            pool.tensor_tensor(hres[:].rearrange("p (t n) -> p t n", t=NT), hres[:].rearrange("p (t n) -> p t n", t=NT),
                               rowv[:, 2:3, :].to_broadcast([P, NT, D]), ALU.add).then_inc(bo_ok, 1)
            pool.wait_ge(wp_evac, 8)
            pool.tensor_tensor(wpql[:], wpq, wpqh[:], ALU.subtract).then_inc(wpql_ok, 1)
            pool.wait_ge(wvh_ok, 1)
            pool.tensor_tensor(wvl[:], wv[:], wvh[:], ALU.subtract).then_inc(wvl_ok, 1)
            pool.wait_ge(mx_step, 1)
            pool.partition_all_reduce(mxa[:], mx1[:], P, RMAX).then_inc(mxa_ok, 1)
            pool.wait_ge(wqh_ok, 1)
            pool.tensor_tensor(wql[:], wq[:], wqh[:], ALU.subtract).then_inc(wql_ok, 1)
            pool.wait_ge(kc_ok, 2)
            with pool.Fori(0, NT // 2) as i:
                for j in range(4):
                    pool.wait_ge(qe_ok, i * 4 + (j + 1))
                    pool.wait_ge(qp_ok, i * 4 + (j + 1))
                    pool.tensor_tensor(qt[j % 2], qe[j % 2][:], kcum[:, j % 2 * HALF:(j % 2 + 1) * HALF], ALU.mult)\
                        .then_inc(qt_ok, 1)
            pool.wait_ge(h2_ok, NT + 2)
            pool.memset(ones[:], 1.0).then_inc(io_ok, 1)
            pool.iota(io8i[:], [[1, MU]], base=0, channel_multiplier=0).then_inc(io_ok, 1)
            pool.iota(ioui[:], [[1, NR]], base=0, channel_multiplier=0).then_inc(io_ok, 1)
            pool.wait_ge(io_ok, 1)
            pool.affine_select(out=tri[:], in_=ones[:], compare_op=ALU.is_gt, fill=0.0, base=0,
                               pattern=[[1, P]], channel_multiplier=-1).then_inc(io_ok, 1)
            pool.memset(h[:, FI:FIC * P], 0.0).then_inc(pad_ok, 1)
            pool.iota(asg[:], [[P, 2 * NT]], base=0, channel_multiplier=1).then_inc(io_ok, 1)
            pool.iota(dump[:], [[1, P]], base=2 * T, channel_multiplier=0).then_inc(io_ok, 1)
            pool.wait_ge(io_ok, 6)
            pool.dma_start(slots_a.rearrange("(u p) o -> u (p o)", p=P), dump[0:NR, :]).then_inc(dump_in, 16)
            pool.wait_ge(dump_in, 16)
            pool.wait_ge(zero_in, 16 * NR)
            pool.wait_ge(slots_ok, 1)
            for k in range(2):
                for t in range(NT):
                    at = bass.IndirectOffsetOnAxis(ap=sloti[:, k * NT + t:k * NT + t + 1], axis=0)
                    pool.indirect_dma_start(out=slots_x, out_offset=at, in_=hn[:, t * D:(t + 1) * D], in_offset=None)\
                        .then_inc(scattered, 16)
            for j in range(2 * NT):
                at = bass.IndirectOffsetOnAxis(ap=sloti[:, j:j + 1], axis=0)
                pool.indirect_dma_start(out=slots_a, out_offset=at, in_=asg[:, j:j + 1], in_offset=None)\
                    .then_inc(ids_scattered, 16)
            pool.wait_ge(sa_in, 16)
            for r in range(NR):
                pool.wait_ge(y_used, NT + r + 2)
                if r > 0:
                    pool.wait_ge(y_out[(r - 1) % 2], 16 * ((r - 1) // 2 + 1))
                pool.indirect_dma_start(out=y_tok, out_offset=bass.IndirectOffsetOnAxis(ap=sa[:, r:r + 1], axis=0),
                                        in_=ys[r % 2][:], in_offset=None).then_inc(y_out[r % 2], 16)

            for g in range(NT // LG - 1):
                t = g * LG + LG - 1
                at = slice(t * D, (t + 1) * D)
                pool.wait_ge(y_in[g], 32)
                for k in range(2):
                    pool.tensor_tensor(yl[k][:, at], yl[k][:, at], wsc[:, k, t:t + 1].to_broadcast([P, D]), ALU.mult)\
                        .then_inc(f2_step, 1)
                pool.wait_ge(f2_step, 3 * g + 1)
                pool.tensor_tensor(hres[:, at], hres[:, at], yl[0][:, at], ALU.add).then_inc(f2_step, 1)
                pool.wait_ge(f2_step, 3 * g + 3)
                pool.tensor_tensor(hres[:, at], hres[:, at], yl[1][:, at], ALU.add).then_inc(yo2_ok, 1)

        @block.tensor
        def _(pe):
            def mm_mix(l):
                pe.wait_ge(mix_in, l * 16 + 16)
                for ic in range(KD):
                    for jc in range(KD):
                        mm = pe.matmul(bank[2][:, ic * D:(ic + 1) * D], mixw[:, jc, ic * P:(ic + 1) * P],
                                       mixw[:, KD + jc, :], start=(jc == 0), stop=(jc == KD - 1))
                mm.then_inc(mm_done, 1)

            def turn_normed(i):
                pe.wait_ge(lnb_ok, i // 2 + 1)
                if i < 2:
                    pe.wait_ge(an_ok, NL * NG)
                elif i < 2 * (NG - 1):
                    pe.wait_ge(ta2_evac, i - 1)
                else:
                    pe.wait_ge(wp_evac, 8)
                for j in range(4):
                    t, c = 2 * i + j // 2, j % 2
                    mm = pe.transpose(normed_bank(i)[:, j * P:(j + 1) * P], hn[:, t * D + c * P:t * D + (c + 1) * P], ident[:])
                mm.then_inc(ta2_done, 1)

            def turn_x(n, g):
                pe.wait_ge(xn_ok, n + 1)
                for c in range(KD):
                    for t in range(GT):
                        mm = pe.transpose(bank[c][:, t * P:(t + 1) * P], xn[g][:, t, c * P:(c + 1) * P], ident[:])
                mm.then_inc(tx_done, 1)

            def turn_a(n, b):
                pe.wait_ge(an_ok, n + 1)
                for c in range(KD):
                    for t in range(GT):
                        mm = pe.transpose(bank[c][:, t * P:(t + 1) * P], an[b][:, t, c * P:(c + 1) * P], ident[:])
                mm.then_inc(ta_done, 1)

            def turn_z(n):
                pe.wait_ge(zt_ok, n * 2 + 2)
                for t in range(GT):
                    for c in range(KD):
                        at = t % 2 * D + c * P
                        mm = pe.transpose(bank[t // 2][:, at:at + P], zT[:, c, t * P:(t + 1) * P], ident[:])
                    if t % 2:
                        mm.then_inc(tz_done, 1)

            def mix(n):
                pe.wait_ge(xt_ok, n + 1)
                for t in range(GT):
                    for kc in range(KD):
                        mm = pe.matmul(bank[2 + t // 2][:, (t % 2) * D:(t % 2 + 1) * D], xT[:, kc, t * P:(t + 1) * P],
                                       mixT[:, kc, :], start=(kc == 0), stop=(kc == KD - 1))
                    if t % 2:
                        mm.then_inc(s_done, 1)

            def split_product(dst, parts, first, last):
                (wh, wl), (xh, xl) = parts
                pe.matmul(dst, wh, xh, start=first, stop=False)
                pe.matmul(dst, wh, xl, start=False, stop=False)
                return pe.matmul(dst, wl, xh, start=False, stop=last)

            def widen(l, n):
                pe.wait_ge(w1_ok, l + 1)
                pe.wait_ge(at_ok, n + 1)
                for c in range(FC):
                    if c >= 2:
                        pe.wait_ge(h_evac, n * FC + (c - 1))
                    for kc in range(KD):
                        cs = slice(c * P, (c + 1) * P)
                        mm = split_product(bank[4 + c % 2][:], ((w1h[:, kc, cs], w1l[:, kc, cs]), (aTh[:, kc, :], aTl[:, kc, :])),
                                           kc == 0, kc == KD - 1)
                    mm.then_inc(h_done, 1)

            def narrow(l, n, half):
                if half == 0:
                    pe.wait_ge(w2_ok, l + 1)
                for c in range(FC):
                    if half == 0:
                        pe.wait_ge(h_split, n * FC + (c + 1))
                    cs = slice(half * P, (half + 1) * P)
                    mm = split_product(bank[6 + half][:], ((w2h[:, c, cs], w2l[:, c, cs]), (hTh[:, c, :], hTl[:, c, :])),
                                       c == 0, c == FC - 1)
                mm.then_inc(z_done, 1)

            def group(l, u, first, last):
                n = l * NG + u
                before = not first or u > 0
                ahead2 = not last or u + 2 < NG
                ahead1 = not last or u + 1 < NG
                widen(l, n)
                if u == 2 and not last:
                    pe.wait_ge(an_ok, n + 2)
                    mm_mix(l + 1)
                if before:
                    pe.wait_ge(s2_ok, n * 2)
                if ahead2:
                    turn_x(n + 2, (u + 2) % NG)
                narrow(l, n, 0)
                if last and u == NG - 1:
                    for i in range(2):
                        turn_normed(i)
                if ahead1:
                    if ahead2:
                        pe.wait_ge(xt_ok, n + 3)
                    turn_a(n + 1, (u + 1) % 2)
                narrow(l, n, 1)
                if ahead2:
                    pe.wait_ge(an_ok, n + 2)
                    if u == 2:
                        pe.wait_ge(mix_ok, l + 2)
                    mix(n + 2)
                if ahead1:
                    pe.wait_ge(at_evac, n + 2)
                turn_z(n)

            pe.wait_ge(cst_ok, 3)
            mm_mix(0)
            turn_x(0, 0)
            pe.wait_ge(mix_ok, 1)
            mix(0)
            pe.wait_ge(xt_ok, 1)
            turn_x(1, 1)
            pe.wait_ge(xt_ok, 2)
            turn_a(0, 0)
            mix(1)
            for u in range(NG):
                group(0, u, True, False)
            with pe.Fori(1, NL - 1) as l:
                for u in range(NG):
                    group(l, u, False, False)
            for u in range(NG):
                group(NL - 1, u, False, True)

            for i in (2, 3):
                turn_normed(i)
            pe.wait_ge(aw_in, 48)
            pe.wait_ge(h_evac, NL * NG * FC)
            i = 0
            for w in (1, 0):
                for ic in range(KD):
                    for hf in range(2):
                        if i >= 4:
                            pe.wait_ge(wp_evac, i - 3)
                        for q in range(4):
                            mm = pe.matmul(bank[4 + i % 4][:, q * P:(q + 1) * P], wqkT[:, w, hf * 4 + q, ic * P:(ic + 1) * P],
                                           bp[:], start=True, stop=True)
                        mm.then_inc(wp_done, 1)
                        i += 1
                if w == 1 and ic == KD - 1:
                    for i2 in (4, 5):
                        turn_normed(i2)

            def project(b, dst, w, hf, done):
                wh, wl = (x[:, :, hf * HALF:(hf + 1) * HALF] for x in w)
                for kc in range(KD):
                    mm = split_product(bank[dst][:], ((hnTh[b][:, kc, :], hnTl[b][:, kc, :]), (wh[:, kc, :], wl[:, kc, :])),
                                       kc == 0, kc == KD - 1)
                mm.then_inc(done, 1)

            pe.wait_ge(wkl_ok, 1)
            pe.wait_ge(wpkl_ok, 1)
            pe.wait_ge(s2_ok, NL * NG * 2)
            pe.wait_ge(ta2_evac, 2 * (NG - 1))

            def key_pair(i):
                for b in range(2):
                    pe.wait_ge(hnT_in[b], i * 32 + 32)
                    for hf in range(2):
                        w = i * 4 + (2 * b + hf)
                        pe.wait_ge(sq_ok, w + 1)
                        project(b, 2 * hf, (wkh, wkl), hf, k_done)
                        pe.wait_ge(ddk_ok, w + 1)
                        project(b, 2 * hf + 1, (wpkh, wpkl), hf, kd_done)

            key_pair(0)
            for i in (2 * NG - 2, 2 * NG - 1):
                turn_normed(i)
            with pe.Fori(1, NT // 2) as i:
                key_pair(i)
            pe.sem_inc(ctx_done, 2)
            pe.sem_inc(tq_done, 2)
            pe.wait_ge(ta2_evac, 2 * NG)
            pe.wait_ge(kset, 3)
            pe.wait_ge(wvl_ok, 1)
            pe.wait_ge(ddk_ok, 2 * NT + 2)
            for c in range(3):
                mm = pe.matmul(bank[cbank[c]][:, 0:3 * PW], zero[:, 0:P], zero[:, 0:3 * PW], start=True, stop=False,
                               skip_group_check=True)
            mm.then_inc(z0_done, 1)
            with pe.Fori(0, NT // 2) as i:
                for b in range(2):
                    pe.wait_ge(hnT_in[b], i * 32 + 32 * (NT // 2 + 1))
                    for hf in range(2):
                        pe.wait_ge(vx_ok, i * 4 + (2 * b + hf + 1))
                        project(b, 4 + hf, (wvh, wvl), hf, v_done)
                for b in range(2):
                    pe.wait_ge(kp_ok, i * 2 + (b + 1))
                    pe.wait_ge(vx_ok, i * 4 + (2 * b + 4))
                    for p in range(NP):
                        mm = pe.matmul(bank[cbank[p // 3]][:, (p % 3) * PW:(p % 3 + 1) * PW], kp[b][:, p * P:(p + 1) * P],
                                       vx[b][:, p, :], start=False, stop=False, skip_group_check=True)
                    mm.then_inc(ctx_done, 1)

            def query(i, j):
                b, hf, w = j // 2 % 2, j % 2, i * 4 + j
                if hf == 0:
                    pe.wait_ge(hnT_in[b], i * 32 + 32 * (NT + 1 + j // 4))
                pe.wait_ge(qsq_ok, w + 1)
                project(b, 2 * hf, (wqh, wql), hf, q_done)
                if not isinstance(i, int) or w >= 2:
                    pe.wait_ge(qe_ok, w - 1)
                project(b, 2 * hf + 1, (wpqh, wpql), hf, qdd_done)

            def turn_features(i, j):
                hf = j % 2
                pe.wait_ge(qp_ok, i * 4 + (j + 3))
                for p in range(4):
                    mm = pe.transpose(bank[4 + hf][:, p * P:(p + 1) * P], qp[hf][:, p * P:(p + 1) * P], ident[:])
                mm.then_inc(tq_done, 1)

            def attended(i, j):
                b, hf = j // 2 % 2, j % 2
                pe.wait_ge(qT_ok, i * 4 + (j + 1))
                if hf == 0:
                    pe.wait_ge(h2_ok, i * 2 + (j // 2 + 1))
                for p in range(4):
                    mm = pe.matmul(bank[6 + b][:, 0:D], qT[hf][:, p, :], cmat[:, hf * 4 + p, :],
                                   start=(hf == 0 and p == 0), stop=(hf == 1 and p == 3))
                if hf == 1:
                    mm.then_inc(o_done, 1)

            pe.wait_ge(wql_ok, 1)
            pe.wait_ge(wpql_ok, 1)
            pe.wait_ge(wo_in, 16)
            query(0, 0)
            pe.wait_ge(ctxs_ok, 12)
            for p in range(NP):
                mm = pe.transpose(bank[4 + p // 4][:, (p % 4) * P:(p % 4 + 1) * P], ctxs[:, p, :], ident[:])
            mm.then_inc(ct_done, 1)
            for p in range(NP):
                mm = pe.matmul(bank[2 + p // 4][:, (p % 4) * P:(p % 4 + 1) * P], kcb[:, p, :], ident[:], start=True, stop=True)
            mm.then_inc(kc_done, 1)
            for p in range(NP):
                if p == 4:
                    pe.wait_ge(ct_ok, 2)
                elif p == 0:
                    pe.wait_ge(ct_ok, 1)
                mm = pe.matmul(bank[cmat_bank[p // 2]][:, (p % 2) * D:(p % 2 + 1) * D], ctxT[:, p, :], wo[:, p, :],
                               start=True, stop=True)
                if p % 2:
                    mm.then_inc(c_done, 1)
            pe.wait_ge(kc_ok, 2)
            for j in range(4):
                if j > 0:
                    query(0, j)
                if j == 2:
                    pe.wait_ge(c_ok, 4)
                if j == 3:
                    attended(0, 0)
                if j >= 2:
                    turn_features(0, j - 2)
            with pe.Fori(1, NT // 2) as i:
                for j in range(4):
                    query(i, j)
                    attended(i, j - 3)
                    turn_features(i, j - 2)
            def turn_r(p):
                pe.wait_ge(ln2p_ok, p + 2)
                if 2 <= p < 7:
                    pe.wait_ge(rT_ok, p - 1)
                for j in range(4):
                    at = (2 * p + j // 2) * D + j % 2 * P
                    mm = pe.transpose(token_bank(p)[:, j * P:(j + 1) * P], hn[:, at:at + P], ident[:])
                mm.then_inc(rt_done, 1)

            def columns(w, base, at, n):
                return w[:, ds(base + at, n)] if base is not None else w[:, at:at + n]

            def gate_up(i, j, half, w, base):
                if half == 0:
                    pe.wait_ge(xT1_ok, i * 2 + (j + 1))
                pe.wait_ge(h_ok, i * 4 + (2 * j + half + 1))
                for k in range(2):
                    for kc in range(KD):
                        mm = pe.matmul(gub[2 * half + k][:, 0:FH], xT1[j % 2][:, kc, :],
                                       columns(w, base, (k * KD + kc) * FI + half * FH, FH),
                                       start=(kc == 0), stop=(kc == KD - 1))
                mm.then_inc(gu_done, 1)

            def turn_h(i, j):
                pe.wait_ge(h_ok, i * 4 + (2 * j + 4))
                for c in range(FIC):
                    mm = pe.transpose(thb[c // 4][:, (c % 4) * P:(c % 4 + 1) * P], h[:, c * P:(c + 1) * P], ident[:])
                    if c in (3, FIC - 1):
                        mm.then_inc(th_done, 1)

            def down(i, j, w, base):
                pe.wait_ge(hhT_ok, i * 4 + (2 * j + 2))
                pe.wait_ge(y_used, i * 2 + (j + 1))
                for c in range(FIC):
                    mm = pe.matmul(yb[:, 0:D], hhT[:, c, :], columns(w, base, 2 * KD * FI + c * D, D),
                                   start=(c == 0), stop=(c == FIC - 1))
                mm.then_inc(y_done, 1)

            def turn_slots(i, j):
                pe.wait_ge(xs_in[j % 2], i * 16 + 16 * (j // 2 + 1))
                for kc in range(KD):
                    mm = pe.transpose(xb[:, kc * P:(kc + 1) * P], xs[j % 2][:, kc * P:(kc + 1) * P], ident[:])
                mm.then_inc(tu_done, 1)

            def expert(i, j):
                return pe.value_load(uei[0:1, ds(i * 2 + j, 1)], min_val=0, max_val=NE - 1) * EW

            last = NT // 2 - 1
            attended(last, 1)
            pe.wait_ge(qe_ok, 2 * NT - 1)
            for p in (0, 1):
                turn_r(p)
            turn_features(last, 2)
            for p in (2, 3):
                turn_r(p)
            attended(last, 2)
            turn_features(last, 3)
            for p in (4, 5, 6):
                turn_r(p)
            attended(last, 3)

            pe.wait_ge(sh_in, 16)
            pe.wait_ge(rT_ok, 7)
            gate_up(0, 0, 0, wsh, None)
            gate_up(0, 0, 1, wsh, None)
            turn_r(7)

            pe.wait_ge(qsq_ok, 2 * NT + 2)
            pe.wait_ge(qe_ok, 2 * NT)
            pe.wait_ge(rw_in, 32)
            for t in range(NT):
                if t % 2 == 0:
                    pe.wait_ge(rT_ok, t // 2 + 1)
                for kc in range(KD):
                    mm = pe.matmul(bank[6][:, t * 8:(t + 1) * 8], rT[:, t * D + kc * P:t * D + (kc + 1) * P], wrT[:, kc, :],
                                   start=(kc == 0), stop=(kc == KD - 1))
            mm.then_inc(l_done, 1)

            pe.wait_ge(io_ok, 4)
            pe.wait_ge(pad_ok, 1)

            def shared(i, j):
                gate_up(i, j, 0, wsh, None)
                gate_up(i, j, 1, wsh, None)
                down(i, j - 1, wsh, None)
                turn_h(i, j)

            turn_h(0, 0)
            pe.wait_ge(rt_step, 1)
            shared(0, 1)
            shared(1, 0)
            pe.wait_ge(hots_ok, 1)
            hv = hots[:].rearrange("p t e -> p (t e)")
            pe.matmul(cb[:, 0:P], tri[:], hv, start=True, stop=True)
            pe.matmul(cb[:, P:2 * P], ones[:], hv, start=True, stop=True).then_inc(cnt_done, 1)
            shared(1, 1)
            with pe.Fori(2, NT // 2 - 1) as i:
                for j in range(2):
                    shared(i, j)
            i = NT // 2 - 1
            shared(i, 0)
            gate_up(i, 1, 0, wsh, None)
            turn_slots(0, 0)
            gate_up(i, 1, 1, wsh, None)
            down(i, 0, wsh, None)
            turn_h(i, 1)

            HT = NT // 2
            pe.wait_ge(wall_in, 16 * NE)
            pe.wait_ge(slots_ok, 1)

            def routed(i, j, more=True):
                e = expert(i, j)
                gate_up(i + HT, j, 0, wall, e)
                if more:
                    turn_slots(i, j + 1)
                gate_up(i + HT, j, 1, wall, e)
                if isinstance(i, int) and 2 * i + j == 0:
                    down(HT, -1, wsh, None)
                else:
                    down(i + HT, j - 1, wall, expert(i, j - 1))
                turn_h(i + HT, j)

            routed(0, 0)
            with pe.Fori(0, NR // 2 - 1) as i:
                for j in (1, 2):
                    routed(i, j)
            i = NR // 2 - 1
            routed(i, 1)
            routed(i, 2, False)
            down(i + HT, 2, wall, expert(i, 2))

        @block.scalar
        def _(act):
            def widened(l, n, chunks):
                for c in chunks:
                    act.wait_ge(h_done, n * FC + (c + 1))
                    alone(act)
                    act.activation(hTr[:, c, :], bank[4 + c % 2][:], ACT.Relu, bias=colv[:, ds(l * COLV + c, 1)])\
                        .then_inc(h_evac, 1)
                    act.wait_ge(h_evac, n * FC + (c + 1))
                    act.activation(hTh[:, c, :], hTr[:, c, :], ACT.Copy).then_inc(hh_ok, 1)

            def turned(done, n, dsts, l, at, ok):
                act.wait_ge(done, n + 1)
                alone(act)
                for dst in dsts:
                    for c in range(KD):
                        ins = act.activation(dst[:, c, :], bank[c][:], ACT.Identity,
                                             scale=colv[:, ds(l * COLV + (at + c), 1)],
                                             bias=colv[:, ds(l * COLV + (at + KD + c), 1)])
                ins.then_inc(ok, 1)

            def turned_x(l, u, n, ahead):
                turned(tx_done, n + ahead, (xT,), l if u + ahead < NG else l + 1, FC + 2 * KD, xt_ok)

            def turned_a(l, u, n, ahead):
                turned(ta_done, n + ahead, (aTh, aTr), l if u + ahead < NG else l + 1, FC, at_evac)

            def narrowed(n, half):
                act.wait_ge(z_done, n * 2 + (half + 1))
                act.activation(zT[:, half, :], bank[6 + half][:], ACT.Copy).then_inc(zt_ok, 1)

            def root(step, n, i, std):
                act.wait_ge(step, n * 3 + 2)
                act.activation(sd[i][:], mv[i][:, :, 1], ACT.Sqrt, bias=eps_t[:, 0:1]).then_inc(std, 1)

            def root_group(g):
                act.wait_ge(lnb_step, 3 * g + 2)
                act.activation(lnsd[:], lnm4[:].rearrange("p (t k) -> p t k", k=2)[:, :, 1], ACT.Sqrt,
                               bias=eps_t[:, 0:1]).then_inc(lnb_std, 1)

            def normed_turned(i):
                act.wait_ge(ta2_done, i + 1)
                act.wait_ge(hres_ok, i // 2 + 1)
                for dst in (hnh, hnT_all):
                    ins = act.activation(dst[:, i * 512:(i + 1) * 512], normed_bank(i)[:], ACT.Copy)
                ins.then_inc(ta2_evac, 1)

            def group(l, u, first, last):
                n = l * NG + u
                widened(l, n, range(0, 4))
                if not last or u + 1 < NG:
                    root(ln1_step, n + 1, 0, std1)
                widened(l, n, range(4, FC))
                if last and u == NG - 1:
                    act.wait_ge(aw_in, 48)
                    act.activation(wkh[:], wk[:], ACT.Copy).then_inc(wkh_ok, 1)
                if not last or u + 2 < NG:
                    turned_x(l, u, n, 2)
                if not first or u > 0:
                    root(ln2_step, n - 1, 1, std2)
                narrowed(n, 0)
                if not last or u + 1 < NG:
                    turned_a(l, u, n, 1)
                if last and u == 3:
                    normed_turned(0)
                    normed_turned(1)
                narrowed(n, 1)
                if last and u == 2:
                    root_group(0)

            act.wait_ge(vec_in, 16)
            act.wait_ge(cst_ok, 3)
            turned_x(0, 0, 0, 0)
            turned_x(0, 1, 1, 0)
            root(ln1_step, 0, 0, std1)
            turned_a(0, 0, 0, 0)
            for u in range(NG):
                group(0, u, True, False)
            with act.Fori(1, NL - 1) as l:
                for u in range(NG):
                    group(l, u, False, False)
            for u in range(NG):
                group(NL - 1, u, False, True)

            root_group(1)
            for i in (2, 3):
                normed_turned(i)
            root(ln2_step, NL * NG - 1, 1, std2)
            root_group(2)
            act.wait_ge(mix_ok, NL)
            act.wait_ge(ares_ok, NL * NG)
            act.wait_ge(xn_ok, (NL + 1) * NG)
            i = 0
            for high_part, whole in ((wpkh, wpk), (wpqh, wpq)):
                for ic in range(KD):
                    for hf in range(2):
                        act.wait_ge(wp_done, i + 1)
                        for w in (high_part, whole):
                            ins = act.activation(w[:, ic, hf * HALF:(hf + 1) * HALF], bank[4 + i % 4][:], ACT.Copy, scale=DN)
                        ins.then_inc(wp_evac, 1)
                        i += 1
                if high_part is wpkh:
                    for i2 in (4, 5):
                        normed_turned(i2)
                    root_group(NG - 1)

            def key_squares(i):
                for j in range(4):
                    act.wait_ge(k_done, i * 4 + (j + 1))
                    act.wait_ge(dg_ok, i * 4 + (j + 1))
                    act.activation(sq[j % 2][:], bank[2 * (j % 2)][:], ACT.Square, scale=0.25).then_inc(sq_ok, 1)

            act.sem_inc(sq_ok, 2)
            key_squares(0)
            for i in (2 * NG - 2, 2 * NG - 1):
                normed_turned(i)
            act.wait_ge(wv_in, 16)
            act.activation(wvh[:], wv[:], ACT.Copy).then_inc(wvh_ok, 1)
            with act.Fori(1, NT // 2) as i:
                key_squares(i)
            def q_square(i, j):
                act.wait_ge(q_done, i * 4 + (j + 1))
                act.activation(qsq[j % 2][:], bank[2 * (j % 2)][:], ACT.Square, scale=0.25).then_inc(qsq_ok, 1)

            act.wait_ge(kd_done, 2 * NT)
            act.wait_ge(wq_in, 16)
            act.activation(wqh[:], wq[:], ACT.Copy).then_inc(wqh_ok, 1)
            act.sem_inc(vx_ok, 2)
            act.wait_ge(nmx_ok, 1)
            act.wait_ge(kset, 3)
            with act.Fori(0, NT // 2) as i:
                for b in range(2):
                    act.wait_ge(ctx_done, i * 2 + (b + 1))
                    alone(act)
                    act.activation(kp[b][:], ddk[:, ds(i * (2 * HD) + b * HD, HD)], ACT.Exp, bias=nmx[:, 0:1])\
                        .then_inc(ke_ok, 1)
                    for hf in range(2):
                        act.wait_ge(v_done, i * 4 + (2 * b + hf + 1))
                        act.activation(vx[b][:, 4 * hf:4 * hf + 4, 0:P], bank[4 + hf][:].rearrange("p (a n) -> p a n", a=4),
                                       ACT.Copy).then_inc(vx_ok, 1)
            act.sem_inc(qsq_ok, 2)
            q_square(0, 0)
            act.wait_ge(ct_done, 1)
            for k in range(2):
                act.activation(ctxT[:, 4 * k:4 * k + 4, :].rearrange("p a n -> p (a n)"), bank[4 + k][:], ACT.Copy)\
                    .then_inc(ct_ok, 1)
            for k in range(4):
                act.wait_ge(c_done, k + 1)
                act.activation(cmat[:, 2 * k:2 * k + 2, :].rearrange("p a n -> p (a n)"), bank[cmat_bank[k]][:], ACT.Copy)\
                    .then_inc(c_ok, 1)

            def q_turned(i, j):
                act.wait_ge(tq_done, i * 4 + (j + 3))
                act.activation(qT[j % 2][:].rearrange("p a n -> p (a n)"), bank[4 + j % 2][:], ACT.Copy).then_inc(qT_ok, 1)

            def q_exp(i, j):
                act.wait_ge(qm_ok, i * 4 + (j + 1))
                act.wait_ge(qp_ok, i * 4 + (j + 1))
                for h1 in range(HH):
                    hs = slice(h1 * DH, (h1 + 1) * DH)
                    ins = act.activation(qe[j % 2][:, hs], bank[2 * (j % 2) + 1][:, hs], ACT.Exp, bias=qm[j % 2][:, h1:h1 + 1])
                ins.then_inc(qe_ok, 1)

            def pair_root(i):
                act.wait_ge(ln2p, i * 4 - 1)
                act.activation(lnsd[:, 0:2], lnm4[:, 0:4].rearrange("p (t k) -> p t k", k=2)[:, :, 1], ACT.Sqrt,
                               bias=eps_t[:, 0:1]).then_inc(ln2p_std, 1)

            for j in range(4):
                if j == 3:
                    q_turned(0, 0)
                if j > 0:
                    q_square(0, j)
                if j >= 1:
                    q_exp(0, j - 1)
            with act.Fori(1, NT // 2) as i:
                for j in range(4):
                    q_turned(i, j - 3)
                    if j == 3:
                        pair_root(i)
                    q_square(i, j)
                    q_exp(i, j - 1)

            def tokens_turned(p):
                act.wait_ge(rt_done, p + 1)
                act.activation(rT[:, p * 2 * D:(p + 1) * 2 * D], token_bank(p)[:], ACT.Copy).then_inc(rT_ok, 1)

            last = NT // 2 - 1
            q_turned(last, 1)
            q_exp(last, 3)
            tokens_turned(0)
            tokens_turned(1)
            q_turned(last, 2)
            tokens_turned(2)
            tokens_turned(3)
            q_turned(last, 3)
            for p in (4, 5, 6):
                tokens_turned(p)

            def gates(i, j, half):
                act.wait_ge(gu_done, i * 4 + (2 * j + half + 1))
                act.activation(sg[half][:], gub[2 * half][:, 0:FH], ACT.Silu).then_inc(sg_ok, 1)

            def h_turned(i, j):
                for k, n in enumerate((4, 2)):
                    act.wait_ge(th_done, i * 4 + (2 * j + k + 1))
                    act.activation(hhT[:, 4 * k:4 * k + n, :].rearrange("p c n -> p (c n)"), thb[k][:, 0:n * P], ACT.Copy)\
                        .then_inc(hhT_ok, 1)

            def tokens(i, j):
                act.wait_ge(gu_done, i * 4 + (2 * j - 2))
                alone(act)
                act.activation(xT1[j % 2][:].rearrange("p a n -> p (a n)"), rT[:, ds(i * (2 * D) + j * D, D)], ACT.Copy)\
                    .then_inc(xT1_ok, 1)

            def slots_turned(i, j):
                act.wait_ge(tu_done, i * 2 + (j + 1))
                act.activation(xT1[j % 2][:].rearrange("p a n -> p (a n)"), xb[:, 0:D], ACT.Copy).then_inc(xT1_ok, 1)

            def outputs(i, j, waits=True):
                act.wait_ge(y_done, i * 2 + (j + 1 + NT))
                if waits:
                    act.wait_ge(y_out[j % 2], i * 16 + 16 * (j // 2))
                act.activation(ys[j % 2][:], yb[:, 0:D], ACT.Copy).then_inc(y_used, 1)

            HT = NT // 2
            for v in range(2):
                act.activation(xT1[v][:].rearrange("p a n -> p (a n)"), rT[:, v * D:(v + 1) * D], ACT.Copy).then_inc(xT1_ok, 1)
            pair_root(last + 1)
            gates(0, 0, 0)
            gates(0, 0, 1)
            tokens_turned(7)
            act.wait_ge(rt_step, 3)
            act.activation(pr[:], pr[:], ACT.Exp).then_inc(pe_exp, 1)
            h_turned(0, 0)

            def shared(i, j):
                gates(i, j, 0)
                tokens(i, j + 1)
                gates(i, j, 1)
                h_turned(i, j)

            with act.Fori(0, HT - 1) as i:
                for j in (1, 2):
                    shared(i, j)
            gates(HT - 1, 1, 0)
            slots_turned(0, 0)
            gates(HT - 1, 1, 1)
            h_turned(HT - 1, 1)

            def routed(i, j, more=True, y_too=True, y_waits=True):
                gates(i + HT, j, 0)
                if more:
                    slots_turned(i, j + 1)
                gates(i + HT, j, 1)
                if y_too:
                    outputs(i, j - 1, y_waits)
                h_turned(i + HT, j)

            routed(0, 0, y_too=False)
            routed(0, 1, y_waits=False)
            routed(0, 2, y_waits=False)
            with act.Fori(1, NR // 2 - 1) as i:
                for j in (1, 2):
                    routed(i, j)
            i = NR // 2 - 1
            routed(i, 1)
            routed(i, 2, False)
            outputs(i, 2)

        @block.vector
        def _(dve):
            dve.wait_ge(ids_in, 16)
            dve.tensor_copy(idf[:], ids[:]).then_inc(ids_step, 1)
            dve.wait_ge(ids_step, 1)
            dve.tensor_scalar(neg[:], idf[:], 0.0, float(V), ALU.is_lt, ALU.mult).then_inc(ids_step, 1)
            dve.wait_ge(ids_step, 2)
            dve.tensor_tensor(idf[:], idf[:], neg[:], ALU.add).then_inc(ids_step, 1)
            dve.wait_ge(ids_step, 3)
            dve.tensor_scalar(idu[:], idf[:], 0.0, float(V - 1), ALU.max, ALU.min).then_inc(ids_step, 1)

            def embed(g):
                dve.wait_ge(gathered[g], 16 * GT)
                dve.sem_inc(xn_ok, 1)

            def mixed(l):
                dve.wait_ge(mm_done, l + 1)
                dve.tensor_tensor(mixT.rearrange("p a n -> p (a n)"), bank[2][:], eye2.rearrange("p a n -> p (a n)"),
                                  ALU.add).then_inc(mix_ok, 1)

            def statistics(n, i, src, step):
                for t in range(GT):
                    ins = dve.bn_stats(stat[i][:, t, :], src(t))
                ins.then_inc(step, 1)
                dve.wait_ge(step, n * 3 + 1)
                alone(dve)
                for t in range(GT):
                    ins = dve.bn_aggr(mv[i][:, t, :], stat[i][:, t, :])
                ins.then_inc(step, 1)

            def normalise(n, i, src, step, std, dst, ok):
                dve.wait_ge(std, n + 1)
                dve.reciprocal(rs[i][:], sd[i][:]).then_inc(step, 1)
                dve.wait_ge(step, n * 3 + 3)
                for t in range(GT):
                    ins = dve.tensor_scalar(dst[:, t, :], src(t), mv[i][:, t, 0:1], rs[i][:, t:t + 1], ALU.subtract, ALU.mult)
                ins.then_inc(ok, 1)

            def mixed_tile(t):
                return bank[2 + t // 2][:, (t % 2) * D:(t % 2 + 1) * D]

            def stats1(n, earlier=True):
                dve.wait_ge(s_done, n * 2 + 2)
                if earlier:
                    dve.wait_ge(an_ok, n)
                statistics(n, 0, mixed_tile, ln1_step)

            def norm1(n, b):
                normalise(n, 0, mixed_tile, ln1_step, std1, an[b], an_ok)

            def sum2(n, b):
                dve.wait_ge(xn_ok, n + NG)
                dve.wait_ge(ares_ok, n + 1)
                for half in range(2):
                    dve.wait_ge(tz_done, n * 2 + (half + 1))
                    dve.tensor_tensor(s2[:, 2 * half:2 * half + 2, :].rearrange("p a n -> p (a n)"), bank[half][:],
                                      ares[b][:, 2 * half:2 * half + 2, :].rearrange("p a n -> p (a n)"), ALU.add)\
                        .then_inc(s2_ok, 1)

            def norm2(n, g):
                dve.wait_ge(s2_ok, n * 2 + 2)
                statistics(n, 1, lambda t: s2[:, t, :], ln2_step)
                normalise(n, 1, lambda t: s2[:, t, :], ln2_step, std2, xn[g], xn_ok)

            def low(high_ok, value, whole, high_part, part, ok):
                dve.wait_ge(high_ok, value)
                dve.tensor_tensor(part, whole, high_part, ALU.subtract).then_inc(ok, 1)

            def split(w_in, l, whole, high_part, high_ok, part, ok):
                dve.wait_ge(w_in, l * 16 + 16)
                dve.tensor_copy(high_part[:], whole[:]).then_inc(high_ok, 1)
                low(high_ok, l + 1, whole[:], high_part[:], part[:], ok)

            def low_h(n, chunks):
                for c in chunks:
                    low(hh_ok, n * FC + (c + 1), hTr[:, c, :], hTh[:, c, :], hTl[:, c, :], h_split)

            def group(l, u, first, last):
                n = l * NG + u
                before = not first or u > 0
                ahead1 = not last or u + 1 < NG
                if before:
                    sum2(n - 1, (u - 1) % 2)
                if ahead1:
                    stats1(n + 1)
                low_h(n, range(0, 4))
                if u == 0:
                    split(w2_in, l, w2r, w2h, w2h_ok, w2l, w2_ok)
                if ahead1:
                    norm1(n + 1, (u + 1) % 2)
                low_h(n, range(4, FC))
                if last and u == NG - 1:
                    low(wkh_ok, 1, wk[:], wkh[:], wkl[:], wkl_ok)
                if u == 2 and not last:
                    mixed(l + 1)
                if before:
                    norm2(n - 1, (u - 1) % NG)
                if ahead1:
                    low(at_evac, n + 2, aTr[:], aTh[:], aTl[:], at_ok)
                if u == NG - 1 and not last:
                    split(w1_in, l + 1, w1r, w1h, w1h_ok, w1l, w1_ok)

            dve.wait_ge(cst_ok, 3)
            mixed(0)
            embed(0)
            embed(1)
            split(w1_in, 0, w1r, w1h, w1h_ok, w1l, w1_ok)
            stats1(0, False)
            norm1(0, 0)
            low(at_evac, 1, aTr[:], aTh[:], aTl[:], at_ok)
            embed(2)
            embed(3)
            for u in range(NG):
                group(0, u, True, False)
            with dve.Fori(1, NL - 1) as l:
                for u in range(NG):
                    group(l, u, False, False)

            def norm_group(g):
                dve.wait_ge(hres_ok, g + 1)
                if g > 0:
                    dve.wait_ge(lnb_ok, g)
                for t in range(GT):
                    at = (g * GT + t) * D
                    ins = dve.bn_stats(lnst[:, t, :], hres[:, at:at + D])
                ins.then_inc(lnb_step, 1)
                dve.wait_ge(lnb_step, 3 * g + 1)
                for t in range(GT):
                    ins = dve.bn_aggr(lnm4[:, 2 * t:2 * t + 2], lnst[:, t, :])
                ins.then_inc(lnb_step, 1)
                dve.wait_ge(lnb_std, g + 1)
                dve.reciprocal(lnrs[:], lnsd[:]).then_inc(lnb_step, 1)
                dve.wait_ge(lnb_step, 3 * g + 3)
                for t in range(GT):
                    at = slice((g * GT + t) * D, (g * GT + t + 1) * D)
                    ins = dve.tensor_scalar(hn[:, at], hres[:, at], lnm4[:, 2 * t:2 * t + 1], lnrs[:, t:t + 1],
                                            ALU.subtract, ALU.mult)
                ins.then_inc(lnb_ok, 1)

            for u in range(NG):
                group(NL - 1, u, False, True)
                if u == 2:
                    norm_group(0)
            def low_normed(i):
                at = slice(i * 512, (i + 1) * 512)
                low(ta2_evac, i + 1, hnT_all[:, at], hnh[:, at], hnl[:, at], ta2_ok)

            low_normed(0)
            low_normed(1)
            norm_group(1)
            sum2(NL * NG - 1, (NG - 1) % 2)
            norm2(NL * NG - 1, NG - 1)
            norm_group(2)
            for i in (2, 3):
                low_normed(i)
            low(wp_evac, 4, wpk, wpkh[:], wpkl[:], wpkl_ok)
            for i in (4, 5):
                low_normed(i)
            norm_group(NG - 1)

            def heads(ap):
                return ap.rearrange("p (h n) -> p h n", n=DH)

            def spread(ap):
                return ap.unsqueeze(2).to_broadcast([P, HH, DH])

            dve.sem_inc(dg_ok, 2)
            dve.sem_inc(ddk_ok, 2)

            def key_exponents(i):
                for j in range(4):
                    hf = j % 2
                    dve.wait_ge(kd_done, i * 4 + (j + 1))
                    dve.tensor_reduce(mxk[:, ds(i * 4 + j, 1)], bank[2 * hf + 1][:], AX.X, ALU.max)
                    dve.wait_ge(sq_ok, i * 4 + (j + 3))
                    dve.tensor_reduce(dg[hf][:], heads(sq[hf][:]), AX.X, ALU.add).then_inc(dg_ok, 1)
                    dve.wait_ge(dg_ok, i * 4 + (j + 3))
                    dve.tensor_tensor(heads(ddk[:, ds(i * (4 * HALF) + j * HALF, HALF)]), heads(bank[2 * hf + 1][:]),
                                      spread(dg[hf][:]), ALU.subtract).then_inc(ddk_ok, 1)

            key_exponents(0)
            for i in (2 * NG - 2, 2 * NG - 1):
                low_normed(i)
            with dve.Fori(1, NT // 2) as i:
                key_exponents(i)
            dve.wait_ge(ddk_ok, 2 * NT + 2)
            dve.tensor_reduce(mx1[:], mxk[:], AX.X, ALU.max).then_inc(mx_step, 1)
            dve.wait_ge(mxa_ok, 1)
            dve.tensor_scalar(nmx[:], mxa[:], -1.0, None, ALU.mult).then_inc(nmx_ok, 1)
            with dve.Fori(0, NT // 2) as i:
                for b in range(2):
                    dve.wait_ge(ke_ok, i * 2 + (b + 1))
                    dve.tensor_scalar(kp[b][:], kp[b][:], EPS, None, ALU.add).then_inc(kp_ok, 1)

            dve.wait_ge(ctx_done, NT + 2)
            dve.memset(ctxs[:], 0.0).then_inc(ctxs_ok, 1)
            dve.wait_ge(ctxs_ok, 1)
            for c, (bk, np_) in enumerate(zip(cbank, (3, 3, 2))):
                src = bank[bk][:, 0:np_ * PW].rearrange("p (a n) -> p a n", n=PW)
                for k in range(2):
                    r = slice(k * DH, (k + 1) * DH)
                    dve.tensor_copy(ctxs[r, 3 * c:3 * c + np_, r], src[r, :, r]).then_inc(ctxs_ok, 1)
                dve.tensor_copy(kcol[:, 3 * c:3 * c + np_], src[:, :, P]).then_inc(ctxs_ok, 1)
            dve.wait_ge(ctxs_ok, 10)
            for k in range(2):
                dve.tensor_copy(kcb[:, 4 * k:4 * k + 4, :], kcol[:, 4 * k:4 * k + 4].unsqueeze(2).to_broadcast([P, 4, P]))\
                    .then_inc(ctxs_ok, 1)
            dve.wait_ge(kc_done, 1)
            for k in range(2):
                dve.tensor_copy(kcum[:, k * HALF:(k + 1) * HALF], bank[2 + k][:]).then_inc(kc_ok, 1)

            dve.wait_ge(kc_ok, 2)
            dve.tensor_reduce(ekc[:], heads(kcum[:]), AX.X, ALU.add).then_inc(kc2_ok, 1)
            dve.wait_ge(kc2_ok, 1)
            dve.tensor_scalar(ekc[:], ekc[:], EPS, None, ALU.mult).then_inc(kc2_ok, 1)

            def exponents(i, j):
                hf = j % 2
                src = bank[2 * hf + 1]
                dve.wait_ge(qdd_done, i * 4 + (j + 1))
                dve.tensor_reduce(qs[hf][:, 0, :], heads(src[:]), AX.X, ALU.max)
                dve.wait_ge(qsq_ok, i * 4 + (j + 3))
                dve.tensor_reduce(qs[hf][:, 1, :], heads(qsq[hf][:]), AX.X, ALU.add).then_inc(aq_step, 1)
                dve.wait_ge(aq_step, i * 4 + (j + 1))
                dve.scalar_tensor_tensor(out=qm[hf][:], in0=qs[hf][:, 0, :], scalar=-1.0, in1=qs[hf][:, 1, :], op0=ALU.mult,
                                         op1=ALU.subtract).then_inc(qm_ok, 1)

            def features(i, j):
                hf = j % 2
                dve.wait_ge(qt_ok, i * 4 + (j + 1))
                dve.tensor_reduce(qr[:, 0, :], heads(qt[hf]), AX.X, ALU.add).then_inc(bq_step, 1)
                dve.wait_ge(bq_step, i * 12 + (3 * j + 1))
                dve.tensor_tensor(qr[:, 0, :], qr[:, 0, :], ekc[:, hf * HH:(hf + 1) * HH], ALU.add).then_inc(bq_step, 1)
                dve.wait_ge(bq_step, i * 12 + (3 * j + 2))
                dve.reciprocal(qr[:, 1, :], qr[:, 0, :]).then_inc(bq_step, 1)
                dve.wait_ge(bq_step, i * 12 + (3 * j + 3))
                dve.wait_ge(tq_done, i * 4 + (j + 1))
                dve.scalar_tensor_tensor(out=heads(qp[hf][:]), in0=heads(qe[hf][:]), scalar=EPS, in1=spread(qr[:, 1, :]),
                                         op0=ALU.add, op1=ALU.mult).then_inc(qp_ok, 1)

            def residual(i, b):
                dve.wait_ge(o_done, i * 2 + (b + 1))
                dve.tensor_tensor(hres[:, ds(i * (2 * D) + b * D, D)], bank[6 + b % 2][:, 0:D],
                                  hres[:, ds(i * (2 * D) + b * D, D)], ALU.add).then_inc(h2_ok, 1)

            def pair_stats(i, b):
                dve.wait_ge(h2_ok, i * 2 + (b + 1))
                alone(dve)
                dve.bn_stats(lnst[:, b, :], hres[:, ds(i * (2 * D) + (b - 2) * D, D)]).then_inc(ln2p, 1)

            def pair_aggr(i):
                dve.wait_ge(ln2p, i * 4 - 2)
                dve.wait_ge(ln2p_ok, i)
                alone(dve)
                for b in range(2):
                    ins = dve.bn_aggr(lnm4[:, 2 * b:2 * b + 2], lnst[:, b, :])
                ins.then_inc(ln2p, 1)

            def pair_apply(i):
                dve.wait_ge(ln2p_std, i)
                dve.reciprocal(lnrs[:, 0:2], lnsd[:, 0:2]).then_inc(ln2p, 1)
                dve.wait_ge(ln2p, i * 4)
                alone(dve)
                for b in range(2):
                    at = ds(i * (2 * D) + (b - 2) * D, D)
                    ins = dve.tensor_scalar(hn[:, at], hres[:, at], lnm4[:, 2 * b:2 * b + 1], lnrs[:, b:b + 1],
                                            ALU.subtract, ALU.mult)
                ins.then_inc(ln2p_ok, 1)

            dve.sem_inc(h_ok, 2)
            dve.sem_inc(ln2p_ok, 1)
            dve.sem_inc(qp_ok, 2)
            dve.sem_inc(h2_ok, 2)
            dve.wait_ge(bo_ok, 1)
            dve.wait_ge(kc2_ok, 2)
            for j in range(1, 4):
                exponents(0, j - 1)
                if j >= 2:
                    features(0, j - 2)
            with dve.Fori(1, NT // 2) as i:
                for j in range(4):
                    if j % 2 == 1:
                        residual(i, j // 2 - 2)
                        pair_stats(i, j // 2)
                    if j == 3:
                        pair_aggr(i)
                    exponents(i, j - 1)
                    features(i, j - 2)
                    if j == 3:
                        pair_apply(i)
            last = NT // 2 - 1
            exponents(last, 3)
            features(last, 2)
            residual(last, 0)
            pair_stats(last + 1, 0)
            features(last, 3)
            residual(last, 1)
            pair_stats(last + 1, 1)
            pair_aggr(last + 1)
            pair_apply(last + 1)

            def products(i, j):
                for half in range(2):
                    dve.wait_ge(sg_ok, i * 4 + (2 * j + half + 1))
                    dve.tensor_tensor(h[:, half * FH:(half + 1) * FH], gub[2 * half + 1][:, 0:FH], sg[half][:], ALU.mult)\
                        .then_inc(h_ok, 1)

            def shared_output(i, j):
                dve.wait_ge(y_done, i * 2 + (j + 1))
                dve.tensor_tensor(hres[:, ds(i * (2 * D) + j * D, D)], yb[:, 0:D], hres[:, ds(i * (2 * D) + j * D, D)], ALU.add)\
                    .then_inc(y_used, 1)

            count = [0]

            def step(ins):
                count[0] += 1
                ins.then_inc(rt_step, 1)
                dve.wait_ge(rt_step, count[0])

            def over_experts(ap):
                return ap.unsqueeze(2).to_broadcast([P, NT, 8])

            dve.sem_inc(y_used, 1)
            products(0, 0)
            dve.wait_ge(rw_in, 32)
            dve.wait_ge(l_done, 1)
            step(dve.tensor_tensor(lg[:], bank[6][:, 0:NT * 8].rearrange("p (t e) -> p t e", e=8),
                                   rb[:].unsqueeze(1).to_broadcast([P, NT, 8]), ALU.add))
            step(dve.tensor_reduce(rsm[:, 0, :], lg[:], AX.X, ALU.max))
            step(dve.tensor_tensor(pr[:], lg[:], over_experts(rsm[:, 0, :]), ALU.subtract))
            dve.wait_ge(pe_exp, 1)
            step(dve.tensor_reduce(rsm[:, 1, :], pr[:], AX.X, ALU.add))
            step(dve.reciprocal(rsm[:, 2, :], rsm[:, 1, :]))
            step(dve.tensor_tensor(pr[:], pr[:], over_experts(rsm[:, 2, :]), ALU.mult))
            for t in range(NT):
                ins = dve.max(top[:, t, :], pr[:, t, :])
            step(ins)
            products(0, 1)
            shared_output(0, 0)
            for t in range(NT):
                ins = dve.max_index(idx[:, t, :], top[:, t, :], pr[:, t, :])
            step(ins)
            step(dve.tensor_tensor(rsm[:, 0, :], top[:, :, 0], top[:, :, 1], ALU.add))
            step(dve.reciprocal(rsm[:, 1, :], rsm[:, 0, :]))
            for k in range(2):
                step(dve.tensor_tensor(wsc[:, k, :], top[:, :, k], rsm[:, 1, :], ALU.mult))
                step(dve.tensor_copy(idxf[:, k, :], idx[:, :, k]))
            products(1, 0)
            shared_output(0, 1)
            dve.wait_ge(io_ok, 6)
            step(dve.tensor_copy(io8[:], io8i[:]))
            step(dve.tensor_copy(iou[:], ioui[:]))
            step(dve.tensor_scalar(iou8[:], io8[:], float(P), None, ALU.mult))
            for k in range(2):
                step(dve.tensor_tensor(hot[k][:], io8[:, 0:8].unsqueeze(1).to_broadcast([P, NT, 8]),
                                       over_experts(idxf[:, k, :]), ALU.is_equal))
            dve.tensor_tensor(hots[:], hot[0][:], hot[1][:], ALU.add).then_inc(hots_ok, 1)
            products(1, 1)
            shared_output(1, 0)
            step(dve.memset(tot[:, 0, :], 0.0))
            step(dve.memset(off[:], 0.0))
            dve.wait_ge(cnt_done, 1)
            counts = cb[:, P:2 * P].rearrange("p (t e) -> p t e", e=8)
            for t in range(NT):
                step(dve.tensor_tensor(tot[:, t + 1, :], counts[:, t, :], tot[:, t, :], ALU.add))
            products(2, 0)
            shared_output(1, 1)
            step(dve.tensor_tensor(over[:], tot[:, NT, :].unsqueeze(2).to_broadcast([P, 8, MU]),
                                   iou8[:].unsqueeze(1).to_broadcast([P, 8, MU]), ALU.is_gt))
            step(dve.tensor_reduce(nun[:], over[:], AX.X, ALU.add))
            for e in range(8):
                step(dve.tensor_tensor(off[:, e + 1:e + 2], off[:, e:e + 1], nun[:, e:e + 1], ALU.add))
            step(dve.tensor_scalar(offs[:], off[:], float(P), None, ALU.mult))
            step(dve.tensor_tensor(pos[:], cb[:, 0:P].rearrange("p (t e) -> p t e", e=8), tot[:, 0:NT, :], ALU.add))
            step(dve.tensor_tensor(pos[:], pos[:], offs[:, 0:8].unsqueeze(1).to_broadcast([P, NT, 8]), ALU.add))
            products(2, 1)
            shared_output(2, 0)
            for k in range(2):
                step(dve.tensor_tensor(pick[:], hot[k][:], pos[:], ALU.mult))
                step(dve.tensor_reduce(slotf[:, k, :], pick[:], AX.X, ALU.add))
            step(dve.tensor_copy(sloti[:], slotf[:].rearrange("p k t -> p (k t)")))
            ne1 = NE - 1
            step(dve.tensor_tensor(ended[:], iou[:].unsqueeze(2).to_broadcast([P, NR, ne1]),
                                   off[:, 1:NE].unsqueeze(1).to_broadcast([P, NR, ne1]), ALU.is_ge))
            step(dve.tensor_reduce(uef[:], ended[:], AX.X, ALU.add))
            dve.tensor_copy(uei[:], uef[:]).then_inc(slots_ok, 1)
            with dve.Fori(3, NT // 2) as i:
                for j in range(2):
                    products(i, j)
                    shared_output(i, j - 1)
            products(NT // 2, 0)
            shared_output(NT // 2, -1)
            with dve.Fori(NT // 2, NT // 2 + NR // 2) as i:
                for j in (1, 2):
                    products(i, j)

            def weigh(t, k):
                at = slice(t * D, (t + 1) * D)
                return dve.scalar_tensor_tensor(out=hres[:, at], in0=yl[k][:, at], scalar=wsc[:, k, t:t + 1], in1=hres[:, at],
                                                op0=ALU.mult, op1=ALU.add)

            for n, t in enumerate(t for t in range(NT) if t % LG != LG - 1 or t == NT - 1):
                if t % LG == 0:
                    dve.wait_ge(y_in[t // LG], 32)
                weigh(t, 0).then_inc(f_step, 1)
                dve.wait_ge(f_step, n + 1)
                weigh(t, 1).then_inc(yo_ok, 1)


def kernel(**inputs):
    import concourse.bacc as bacc
    from concourse.bass_utils import run_bass_kernel_spmd

    a = {k: np.asarray(v) for k, v in inputs.items()}

    def chunks(w, n):
        lead = w.shape[:-2]
        return np.moveaxis(w.reshape(*lead, n, P, w.shape[-1]), -3, -2)

    wq = a["L0_tok_Wq"].reshape(NL, D, D)
    woT = a["L0_tok_Wo"].transpose(0, 2, 1)
    one, nil = np.ones((1, D), np.float32), np.zeros((1, D), np.float32)
    cols = [a["L0_tok_ff_b1"], a["L0_tok_ln1_w"], a["L0_tok_ln1_b"],
            np.concatenate([one, a["L0_tok_ln2_w"][:-1]]), np.concatenate([nil, a["L0_tok_ln2_b"][:-1]])]
    colv = np.concatenate([c.reshape(NL, -1, P) for c in cols], 1)
    pt = a["L0_attn_P"].T
    bp = np.zeros((P, P), np.float32)
    bp[:DH, :DH] = pt
    bp[DH:, DH:] = pt
    gate = np.concatenate([a["L0_ffn_rg"], a["L0_ffn_sg"][None]]).transpose(0, 2, 1)
    up = np.concatenate([a["L0_ffn_ru"], a["L0_ffn_su"][None]]).transpose(0, 2, 1)
    dn = np.concatenate([a["L0_ffn_rd"], a["L0_ffn_sd"][None]]).transpose(0, 2, 1)
    dn = np.concatenate([dn, np.zeros((NE + 1, FIC * P - FI, D), np.float32)], 1)
    flat = [w.reshape(NE + 1, P, -1) for w in (chunks(gate, KD), chunks(up, KD), chunks(dn, FIC))]
    arrays = {
        "ids": a["x"].reshape(NT, P).T,
        "emb": a["L0_tok_emb_table"],
        "mixw": np.concatenate([chunks(wq, KD), chunks(woT, KD)], 2),
        "w1T": chunks(a["L0_tok_ff_w1"].transpose(0, 2, 1), KD),
        "w2T": chunks(a["L0_tok_ff_w2"].transpose(0, 2, 1), FC),
        "colv": colv.transpose(2, 0, 1).reshape(P, -1),
        "ln1row": np.stack([a["L0_tok_ln1_w"].ravel(), a["L0_tok_ln1_b"].ravel(), a["L0_tok_ff_b2"].ravel()]),
        "rowv": np.stack([a["L0_tok_ln2_w"][-1], a["L0_tok_ln2_b"][-1], a["L0_attn_bo"]]),
        "wqkv": np.stack([chunks(a[f"L0_attn_W{k}"], KD) for k in "qkv"], 1),
        "wqkT": np.stack([chunks(a[f"L0_attn_W{k}"].T, NP) for k in "qk"], 1),
        "wo": chunks(a["L0_attn_Wo"], NP),
        "bp": bp,
        "wrT": chunks(np.concatenate([a["L0_ffn_wr"].T, np.zeros((D, 1), np.float32)], 1), KD),
        "rb": np.concatenate([a["L0_ffn_rb"], np.full((1,), -1e30, np.float32)]),
        "we": np.concatenate(flat, 2),
    }
    arrays = {k: np.ascontiguousarray(v) for k, v in arrays.items()}
    nc = bacc.Bacc("TRN2", target_bir_lowering=False, num_devices=1)
    d = {k: nc.dram_tensor(f"in_{k}", v.shape, mybir.dt.from_np(v.dtype), kind="ExternalInput").ap()
         for k, v in arrays.items()}
    out = nc.dram_tensor("out", (T, D), F32, kind="ExternalOutput").ap()
    build(nc, d, out)
    r = run_bass_kernel_spmd(nc, [{f"in_{k}": v for k, v in arrays.items()}], core_ids=[0])
    return r.results[0]["out"].reshape(1, T, D)
```
